# Optimizing a Trainium2 kernel written in Bass

```python
import numpy as np
import jax
import jax.numpy as jnp

def _softmax(x, axis=-1):
    return jax.nn.softmax(x, axis=axis)

def _gelu(x):
    return jax.nn.gelu(x, approximate=True)

def _silu(x):
    return jax.nn.silu(x)

def _sigmoid(x):
    return jax.nn.sigmoid(x)

def _layernorm(x, axis=-1, eps=1e-05):
    m = jnp.mean(x, axis=axis, keepdims=True)
    v = jnp.var(x, axis=axis, keepdims=True)
    return (x - m) / jnp.sqrt(v + eps)

def _scatter_add(tgt, idx, src, axis=0):
    return tgt.at[idx].add(src)

def _segment_sum(src, seg, n):
    return jax.ops.segment_sum(src, seg, n)
kernel_name = 'mk_sandwich_d2_jaxref_r8_448179'

def setup_inputs(seed: int=0):
    np.random.seed(seed)
    _w = jnp.asarray

    def _L0_attn_setup():
        import jax, jax.numpy as jnp
        import numpy as np
        import math
        H = 16
        LORA_SCALING = 16 / 8
        NEG_INF = -1e+30

        def _alibi_slopes(n_heads):
            start = 2.0 ** (-2.0 ** (-(math.log2(n_heads) - 3)))
            return jnp.asarray([start * start ** i for i in range(n_heads)], dtype=jnp.float32)

        def _lora(x, W, A, Bm):
            return x @ W.T + x @ Bm.T @ A.T * LORA_SCALING
        key = jax.random.key(seed)
        ks = jax.random.split(key, 11)
        B, T, E, r = (4, 256, 128, 8)
        d = {'x': jax.random.normal(ks[0], (B, T, E), jnp.float32), 'Wq': jax.random.normal(ks[1], (E, E), jnp.float32) * E ** (-0.5), 'Aq': jax.random.normal(ks[2], (E, r), jnp.float32) * 0.01, 'Bq': jax.random.normal(ks[3], (r, E), jnp.float32) * 0.01, 'Wk': jax.random.normal(ks[4], (E, E), jnp.float32) * E ** (-0.5), 'Ak': jax.random.normal(ks[5], (E, r), jnp.float32) * 0.01, 'Bk': jax.random.normal(ks[6], (r, E), jnp.float32) * 0.01, 'Wv': jax.random.normal(ks[7], (E, E), jnp.float32) * E ** (-0.5), 'Av': jax.random.normal(ks[8], (E, r), jnp.float32) * 0.01, 'Bv': jax.random.normal(ks[9], (r, E), jnp.float32) * 0.01, 'Wp': jax.random.normal(ks[10], (E, E), jnp.float32) * E ** (-0.5)}
        return d
    _L0_attn_in = _L0_attn_setup()

    def _L0_ffn_setup():
        import jax, jax.numpy as jnp
        import numpy as np
        B, S, H, I, E, K = (4, 256, 128, 128, 8, 2)
        LIMIT = 7.0
        ALPHA = 1.702
        EPS = 1e-05
        key = jax.random.key(seed)
        ks = jax.random.split(key, 5)
        x = jax.random.normal(ks[0], (B, S, H), dtype=jnp.float32)
        norm_weight = jnp.ones((H,), dtype=jnp.float32)
        gate_weight = (jax.random.normal(ks[1], (E, H), dtype=jnp.float32) / np.sqrt(H)).astype(jnp.bfloat16)
        gate_bias = jnp.zeros((E,), dtype=jnp.bfloat16)
        mlp1_weight = (jax.random.normal(ks[2], (E, 2 * I, H), dtype=jnp.float32) / np.sqrt(H)).astype(jnp.bfloat16)
        mlp1_bias = jnp.zeros((E, 2 * I), dtype=jnp.bfloat16)
        mlp2_weight = (jax.random.normal(ks[3], (E, H, I), dtype=jnp.float32) / np.sqrt(I)).astype(jnp.bfloat16)
        mlp2_bias = jnp.zeros((E, H), dtype=jnp.bfloat16)
        return {'x': x, 'norm_weight': norm_weight, 'gate_weight': gate_weight, 'gate_bias': gate_bias, 'mlp1_weight': mlp1_weight, 'mlp1_bias': mlp1_bias, 'mlp2_weight': mlp2_weight, 'mlp2_bias': mlp2_bias}
    _L0_ffn_in = _L0_ffn_setup()

    def _L1_attn_setup():
        import jax, jax.numpy as jnp
        import numpy as np
        B, S, IN_DIM = (2, 256, 128)
        OUT_DIM, H = (128, 16)
        D = OUT_DIM // H
        W1, W2 = (16, 16)
        LN_EPS = 1e-05

        def _causal_windows(t, w):
            b, s, h, d = t.shape
            padded = jnp.concatenate([jnp.zeros((b, w - 1, h, d), t.dtype), t], axis=1)
            return jnp.stack([padded[:, j:j + s] for j in range(w)], axis=2)

        def _forward(x, Wq, Wk, Wv, Wkp, Wo, gamma, beta):
            b, s, _ = x.shape
            proj = lambda W: (x @ W.T).reshape(b, s, H, D)
            Q, K, V, Kp = (proj(Wq), proj(Wk), proj(Wv), proj(Wkp))
            K_win = _causal_windows(K, W1)
            Kp_win = _causal_windows(Kp, W2)
            V_win = _causal_windows(V, W1)
            Vp_win = _causal_windows(V, W2)
            A = jnp.einsum('bshd,bsjhd,bskhd->bshjk', Q, K_win, Kp_win) / jnp.sqrt(jnp.float32(D))
            s_idx = jnp.arange(s)[:, None]
            m1 = jnp.arange(W1)[None, :] >= W1 - 1 - s_idx
            m2 = jnp.arange(W2)[None, :] >= W2 - 1 - s_idx
            mask = m1[:, :, None] & m2[:, None, :]
            A = jnp.where(mask[None, :, None], A, -jnp.inf)
            P = jax.nn.softmax(A.reshape(b, s, H, W1 * W2), axis=-1).reshape(b, s, H, W1, W2)
            Z = jnp.einsum('bshjk,bsjhd,bskhd->bshd', P, V_win, Vp_win)
            out = Z.reshape(b, s, OUT_DIM) @ Wo.T + x
            mu = jnp.mean(out, axis=-1, keepdims=True)
            var = jnp.mean(jnp.square(out - mu), axis=-1, keepdims=True)
            return (out - mu) / jnp.sqrt(var + LN_EPS) * gamma + beta
        key = jax.random.key(seed)
        ks = jax.random.split(key, 8)
        sc_in = 1.0 / np.sqrt(IN_DIM)
        sc_out = 1.0 / np.sqrt(OUT_DIM)
        return {'x': jax.random.normal(ks[0], (B, S, IN_DIM), dtype=jnp.float32), 'Wq': jax.random.normal(ks[1], (OUT_DIM, IN_DIM), dtype=jnp.float32) * sc_in, 'Wk': jax.random.normal(ks[2], (OUT_DIM, IN_DIM), dtype=jnp.float32) * sc_in, 'Wv': jax.random.normal(ks[3], (OUT_DIM, IN_DIM), dtype=jnp.float32) * sc_in, 'Wkp': jax.random.normal(ks[4], (OUT_DIM, IN_DIM), dtype=jnp.float32) * sc_in, 'Wo': jax.random.normal(ks[5], (OUT_DIM, OUT_DIM), dtype=jnp.float32) * sc_out, 'gamma': jnp.ones((OUT_DIM,), dtype=jnp.float32), 'beta': jnp.zeros((OUT_DIM,), dtype=jnp.float32)}
    _L1_attn_in = _L1_attn_setup()

    def _L1_ffn_setup():
        import jax, jax.numpy as jnp
        import numpy as np
        B, S, D, F, E, NS, K = (2, 128, 128, 512, 8, 8, 2)
        FS = F // NS
        key = jax.random.key(seed)
        ks = jax.random.split(key, 8)
        scale = 0.02
        return {'hidden_states': jax.random.normal(ks[0], (B, S, D), jnp.float32), 'gate_W': jax.random.normal(ks[1], (E, D), jnp.float32) * scale, 'w1_e': jax.random.normal(ks[2], (E, D, F), jnp.float32) * scale, 'w3_e': jax.random.normal(ks[3], (E, D, F), jnp.float32) * scale, 'w2_e': jax.random.normal(ks[4], (E, F, D), jnp.float32) * scale, 'w1_s': jax.random.normal(ks[5], (NS, D, FS), jnp.float32) * scale, 'w3_s': jax.random.normal(ks[6], (NS, D, FS), jnp.float32) * scale, 'w2_s': jax.random.normal(ks[7], (NS, FS, D), jnp.float32) * scale}
    _L1_ffn_in = _L1_ffn_setup()
    _d = {'L0_attn_x': _L0_attn_in['x'], 'L0_attn_Wq': _L0_attn_in['Wq'], 'L0_attn_Aq': _L0_attn_in['Aq'], 'L0_attn_Bq': _L0_attn_in['Bq'], 'L0_attn_Wk': _L0_attn_in['Wk'], 'L0_attn_Ak': _L0_attn_in['Ak'], 'L0_attn_Bk': _L0_attn_in['Bk'], 'L0_attn_Wv': _L0_attn_in['Wv'], 'L0_attn_Av': _L0_attn_in['Av'], 'L0_attn_Bv': _L0_attn_in['Bv'], 'L0_attn_Wp': _L0_attn_in['Wp'], 'L0_ffn_norm_weight': _L0_ffn_in['norm_weight'], 'L0_ffn_gate_weight': _L0_ffn_in['gate_weight'], 'L0_ffn_gate_bias': _L0_ffn_in['gate_bias'], 'L0_ffn_mlp1_weight': _L0_ffn_in['mlp1_weight'], 'L0_ffn_mlp1_bias': _L0_ffn_in['mlp1_bias'], 'L0_ffn_mlp2_weight': _L0_ffn_in['mlp2_weight'], 'L0_ffn_mlp2_bias': _L0_ffn_in['mlp2_bias'], 'L1_attn_Wq': _L1_attn_in['Wq'], 'L1_attn_Wk': _L1_attn_in['Wk'], 'L1_attn_Wv': _L1_attn_in['Wv'], 'L1_attn_Wkp': _L1_attn_in['Wkp'], 'L1_attn_Wo': _L1_attn_in['Wo'], 'L1_attn_gamma': _L1_attn_in['gamma'], 'L1_attn_beta': _L1_attn_in['beta'], 'L1_ffn_gate_W': _L1_ffn_in['gate_W'], 'L1_ffn_w1_e': _L1_ffn_in['w1_e'], 'L1_ffn_w3_e': _L1_ffn_in['w3_e'], 'L1_ffn_w2_e': _L1_ffn_in['w2_e'], 'L1_ffn_w1_s': _L1_ffn_in['w1_s'], 'L1_ffn_w3_s': _L1_ffn_in['w3_s'], 'L1_ffn_w2_s': _L1_ffn_in['w2_s']}
    _x0 = _d['L0_attn_x']
    _d['L0_attn_x'] = jax.random.normal(jax.random.fold_in(jax.random.key(seed), 1), (4, 1024, 128), dtype=_x0.dtype)
    del _x0
    return _d

def reference(L0_attn_x, L0_attn_Wq, L0_attn_Aq, L0_attn_Bq, L0_attn_Wk, L0_attn_Ak, L0_attn_Bk, L0_attn_Wv, L0_attn_Av, L0_attn_Bv, L0_attn_Wp, L0_ffn_norm_weight, L0_ffn_gate_weight, L0_ffn_gate_bias, L0_ffn_mlp1_weight, L0_ffn_mlp1_bias, L0_ffn_mlp2_weight, L0_ffn_mlp2_bias, L1_attn_Wq, L1_attn_Wk, L1_attn_Wv, L1_attn_Wkp, L1_attn_Wo, L1_attn_gamma, L1_attn_beta, L1_ffn_gate_W, L1_ffn_w1_e, L1_ffn_w3_e, L1_ffn_w2_e, L1_ffn_w1_s, L1_ffn_w3_s, L1_ffn_w2_s):

    def _L0_attn_ref(x, Wq, Aq, Bq, Wk, Ak, Bk, Wv, Av, Bv, Wp):
        import jax, jax.numpy as jnp
        import numpy as np
        import math
        H = 16
        LORA_SCALING = 16 / 8
        NEG_INF = -1e+30

        def _alibi_slopes(n_heads):
            start = 2.0 ** (-2.0 ** (-(math.log2(n_heads) - 3)))
            return jnp.asarray([start * start ** i for i in range(n_heads)], dtype=jnp.float32)

        def _lora(x, W, A, Bm):
            return x @ W.T + x @ Bm.T @ A.T * LORA_SCALING
        B, T, E = x.shape
        dh = E // H
        q = _lora(x, Wq, Aq, Bq).reshape(B, T, H, dh).transpose(0, 2, 1, 3)
        k = _lora(x, Wk, Ak, Bk).reshape(B, T, H, dh).transpose(0, 2, 1, 3)
        v = _lora(x, Wv, Av, Bv).reshape(B, T, H, dh).transpose(0, 2, 1, 3)
        s = jnp.einsum('bhqd,bhkd->bhqk', q, k) / jnp.sqrt(jnp.float32(dh))
        i = jnp.arange(T)[:, None]
        j = jnp.arange(T)[None, :]
        slopes = _alibi_slopes(H)
        bias = slopes[:, None, None] * (i - j).astype(jnp.float32)
        s = s + bias[None]
        s = jnp.where(j[None, None] <= i[None, None], s, NEG_INF)
        out = jnp.einsum('bhqk,bhkd->bhqd', jax.nn.softmax(s, axis=-1), v)
        out = out.transpose(0, 2, 1, 3).reshape(B, T, E)
        return out @ Wp.T

    def _L0_ffn_ref(x, norm_weight, gate_weight, gate_bias, mlp1_weight, mlp1_bias, mlp2_weight, mlp2_bias):
        import jax, jax.numpy as jnp
        import numpy as np
        B, S, H, I, E, K = (4, 256, 128, 128, 8, 2)
        LIMIT = 7.0
        ALPHA = 1.702
        EPS = 1e-05
        xc = x.astype(jnp.bfloat16)
        xf = xc.astype(jnp.float32)
        rms = jnp.mean(xf * xf, axis=-1, keepdims=True)
        normed = (xf * jax.lax.rsqrt(rms + EPS) * norm_weight).astype(jnp.bfloat16)
        nf = normed.astype(jnp.float32)
        logits = (jnp.einsum('bsh,eh->bse', nf, gate_weight.astype(jnp.float32)) + gate_bias.astype(jnp.float32)).astype(jnp.bfloat16).astype(jnp.float32)
        scores, idx = jax.lax.top_k(logits, K)
        w = jax.nn.softmax(scores, axis=-1)
        combine = jnp.sum(jax.nn.one_hot(idx, E, dtype=jnp.float32) * w[..., None], axis=-2)
        p1 = jnp.einsum('bsh,eoh->bseo', nf, mlp1_weight.astype(jnp.float32)) + mlp1_bias.astype(jnp.float32)
        g = jnp.minimum(p1[..., 0::2], LIMIT)
        lin = jnp.clip(p1[..., 1::2], -LIMIT, LIMIT)
        act = g * jax.nn.sigmoid(ALPHA * g) * (lin + 1.0)
        p2 = jnp.einsum('bsei,ehi->bseh', act, mlp2_weight.astype(jnp.float32)) + mlp2_bias.astype(jnp.float32)
        combined = jnp.einsum('bseh,bse->bsh', p2, combine)
        out = (xc + combined.astype(jnp.bfloat16)).astype(x.dtype)
        return out

    def _L1_attn_ref(x, Wq, Wk, Wv, Wkp, Wo, gamma, beta):
        import jax, jax.numpy as jnp
        import numpy as np
        B, S, IN_DIM = (2, 256, 128)
        OUT_DIM, H = (128, 16)
        D = OUT_DIM // H
        W1, W2 = (16, 16)
        LN_EPS = 1e-05

        def _causal_windows(t, w):
            b, s, h, d = t.shape
            padded = jnp.concatenate([jnp.zeros((b, w - 1, h, d), t.dtype), t], axis=1)
            return jnp.stack([padded[:, j:j + s] for j in range(w)], axis=2)

        def _forward(x, Wq, Wk, Wv, Wkp, Wo, gamma, beta):
            b, s, _ = x.shape
            proj = lambda W: (x @ W.T).reshape(b, s, H, D)
            Q, K, V, Kp = (proj(Wq), proj(Wk), proj(Wv), proj(Wkp))
            K_win = _causal_windows(K, W1)
            Kp_win = _causal_windows(Kp, W2)
            V_win = _causal_windows(V, W1)
            Vp_win = _causal_windows(V, W2)
            A = jnp.einsum('bshd,bsjhd,bskhd->bshjk', Q, K_win, Kp_win) / jnp.sqrt(jnp.float32(D))
            s_idx = jnp.arange(s)[:, None]
            m1 = jnp.arange(W1)[None, :] >= W1 - 1 - s_idx
            m2 = jnp.arange(W2)[None, :] >= W2 - 1 - s_idx
            mask = m1[:, :, None] & m2[:, None, :]
            A = jnp.where(mask[None, :, None], A, -jnp.inf)
            P = jax.nn.softmax(A.reshape(b, s, H, W1 * W2), axis=-1).reshape(b, s, H, W1, W2)
            Z = jnp.einsum('bshjk,bsjhd,bskhd->bshd', P, V_win, Vp_win)
            out = Z.reshape(b, s, OUT_DIM) @ Wo.T + x
            mu = jnp.mean(out, axis=-1, keepdims=True)
            var = jnp.mean(jnp.square(out - mu), axis=-1, keepdims=True)
            return (out - mu) / jnp.sqrt(var + LN_EPS) * gamma + beta
        return _forward(x, Wq, Wk, Wv, Wkp, Wo, gamma, beta)

    def _L1_ffn_ref(hidden_states, gate_W, w1_e, w3_e, w2_e, w1_s, w3_s, w2_s):
        import jax, jax.numpy as jnp
        import numpy as np
        B, S, D, F, E, NS, K = (2, 128, 128, 512, 8, 8, 2)
        FS = F // NS
        b, s, d = hidden_states.shape
        e = gate_W.shape[0]
        flat = hidden_states.reshape(-1, d)
        T = flat.shape[0]
        logits = (flat @ gate_W.T).astype(jnp.float32)
        probs = jax.nn.softmax(logits, axis=-1)
        top_v, top_i = jax.lax.top_k(probs, K)
        gates = jnp.zeros((T, e), probs.dtype).at[jnp.arange(T)[:, None], top_i].set(top_v)
        g = jax.nn.silu(jnp.einsum('td,edf->etf', flat, w1_e))
        u = jnp.einsum('td,edf->etf', flat, w3_e)
        out_e = jnp.einsum('etf,efd->etd', g * u, w2_e)
        routed = jnp.einsum('te,etd->td', gates, out_e).reshape(b, s, d)
        gs = jax.nn.silu(jnp.einsum('bsd,ndf->nbsf', hidden_states, w1_s))
        us = jnp.einsum('bsd,ndf->nbsf', hidden_states, w3_s)
        shared = jnp.einsum('nbsf,nfd->bsd', gs * us, w2_s) / w1_s.shape[0]
        alpha = 0.5
        return alpha * shared + (1.0 - alpha) * routed
    x = L0_attn_x
    x = x + _layernorm(_L0_attn_ref(_layernorm(x, axis=-1), L0_attn_Wq, L0_attn_Aq, L0_attn_Bq, L0_attn_Wk, L0_attn_Ak, L0_attn_Bk, L0_attn_Wv, L0_attn_Av, L0_attn_Bv, L0_attn_Wp), axis=-1)
    x = x + _layernorm(_L0_ffn_ref(_layernorm(x, axis=-1), L0_ffn_norm_weight, L0_ffn_gate_weight, L0_ffn_gate_bias, L0_ffn_mlp1_weight, L0_ffn_mlp1_bias, L0_ffn_mlp2_weight, L0_ffn_mlp2_bias), axis=-1)
    x = x + _layernorm(_L1_attn_ref(_layernorm(x, axis=-1), L1_attn_Wq, L1_attn_Wk, L1_attn_Wv, L1_attn_Wkp, L1_attn_Wo, L1_attn_gamma, L1_attn_beta), axis=-1)
    x = x + _layernorm(_L1_ffn_ref(_layernorm(x, axis=-1), L1_ffn_gate_W, L1_ffn_w1_e, L1_ffn_w3_e, L1_ffn_w2_e, L1_ffn_w1_s, L1_ffn_w3_s, L1_ffn_w2_s), axis=-1)
    return x

_drawn_inputs = setup_inputs


def setup_inputs(seed=0):
    import zlib

    import numpy as np

    out = dict(_drawn_inputs(seed))
    spreads = {'L0_ffn_norm_weight': (1.0, 0.2),
     'L0_ffn_gate_bias': (0.0, 0.1),
     'L0_ffn_mlp1_bias': (0.0, 0.1),
     'L0_ffn_mlp2_bias': (0.0, 0.1),
     'L1_attn_gamma': (1.0, 0.2),
     'L1_attn_beta': (0.0, 0.1)}
    factors = {'L0_attn_Aq': 4.412,
     'L0_attn_Bq': 5.582,
     'L0_attn_Ak': 4.789,
     'L0_attn_Bk': 4.03,
     'L0_attn_Av': 4.516,
     'L0_attn_Bv': 4.199}
    for name, (base, spread) in spreads.items():
        noise = np.random.default_rng([zlib.crc32(name.encode()), seed]).standard_normal(out[name].shape)
        drawn = base * np.exp(spread * noise) if base else spread * noise
        out[name] = jnp.asarray(drawn.astype(out[name].dtype))
    for name, factor in factors.items():
        out[name] = (out[name] * factor).astype(out[name].dtype)
    return out
```

```python
from contextlib import ExitStack, contextmanager

import concourse.bass as bass
from concourse import mybir

fp32 = mybir.dt.float32
bf16 = mybir.dt.bfloat16
ALU = mybir.AluOpType
ACT = mybir.ActivationFunctionType
AX = mybir.AxisListType

P = 128
B, T = 4, 1024
NTOK = B * T
TILES = NTOK // P
CH = 512
NCH = NTOK // CH
CT = CH // P
H, DH = 16, 8
EPS = 1e-5
NEG = -1e30


class Mem:

    def __init__(self, nc, ctx, stage):
        self.nc, self.ctx, self.stage = nc, ctx, stage + "_"

    def sb(self, name, shape, dt=fp32):
        return self.ctx.enter_context(self.nc.sbuf_tensor(self.stage + name, shape, dt))

    def ps(self, name, shape, dt=fp32):
        return self.ctx.enter_context(self.nc.psum_tensor(self.stage + name, shape, dt))

    def sem(self, name):
        return self.nc.alloc_semaphore(self.stage + name)


@contextmanager
def semaphores_of(nc):
    before = nc.snapshot_sems()
    yield
    nc.clear_and_free_semaphores(nc.allocated_since(before))
    nc.all_engine_barrier()


def ds(at, n):
    return bass.ds(at, n)


def view(ap, dims, offset=0):
    return bass.AP(ap.tensor, ap.offset + offset, [list(ap.ap[0]), *dims])


def load_stage(nc, io, g):
    with ExitStack() as ctx:
        m = Mem(nc, ctx, "load")
        names = ["L0_attn_Wq", "L0_attn_Wk", "L0_attn_Wv", "L0_attn_Wp",
                 "L1_attn_Wq", "L1_attn_Wk", "L1_attn_Wv", "L1_attn_Wkp", "L1_attn_Wo"]
        w_nat = m.sb("w_nat", [P, len(names), P])
        lora_a = m.sb("lora_a", [P, 3, DH])
        lora_b = m.sb("lora_b", [DH, 3, P])
        lora_at = m.sb("lora_at", [DH, 3, P])
        place_i = m.sb("place_i", [P, E_], mybir.dt.int32)
        ps_a = m.ps("ps_a", [P, 3, 512])
        ps_w = m.ps("ps_w", [P, 3, 512])
        loaded, x_loaded, consts, at_ready, at_copied, w_ready, w_copied = (
            m.sem(s) for s in ("loaded", "x_loaded", "consts", "at_ready", "at_copied", "w_ready", "w_copied"))
        N_LOADS = len(names) + 6
        block = ctx.enter_context(nc.Block())

        @block.sync
        def _(sp):
            for i, n in enumerate(names):
                sp.dma_start(w_nat[:, i, :], io[n]).then_inc(loaded, 16)
            for i, n in enumerate("qkv"):
                sp.dma_start(lora_a[:, i, :], io["L0_attn_A" + n]).then_inc(loaded, 16)
                sp.dma_start(lora_b[:, i, :], io["L0_attn_B" + n]).then_inc(loaded, 16)
            sp.dma_start(g["x_tok"][:, :, :], io["L0_attn_x"].rearrange("b (k p) e -> p (b k) e", p=P)).then_inc(x_loaded, 16)
            sp.wait_ge(x_loaded, 16)

        @block.gpsimd
        def _(pool):
            pool.memset(g["ident"][:, :], 0.0).then_inc(consts, 1)
            pool.memset(g["ident_h"][:, :], 0.0).then_inc(consts, 1)
            pool.memset(g["mask_qk"][:, :], 0.0).then_inc(consts, 1)
            pool.memset(g["mask_kq"][:, :], 0.0).then_inc(consts, 1)
            pool.wait_ge(consts, 4)
            for t in ("ident", "ident_h"):
                pool.affine_select(out=g[t][:, :], in_=g[t][:, :], compare_op=ALU.not_equal, fill=1.0,
                                   base=0, pattern=[[-1, P]], channel_multiplier=1).then_inc(consts, 1)
            pool.iota(place_i[:, :], pattern=[[1, E_]], base=-E_, channel_multiplier=0).then_inc(consts, 1)
            pool.wait_ge(consts, 7)
            pool.tensor_copy(g["place"][:, :], place_i[:, :]).then_inc(consts, 1)
            pool.memset(g["pick"][:, :, :], 0.0).then_inc(consts, 1)
            for s in range(PARTS):
                pool.wait_ge(consts, 9 + s)
                pool.affine_select(out=g["pick"][:, :, :], in_=g["pick"][:, :, :], compare_op=ALU.not_equal, fill=1.0,
                                   base=-s * E_, pattern=[[-1, E_], [0, P]], channel_multiplier=1).then_inc(consts, 1)
            pool.affine_select(out=g["mask_qk"][:, :], in_=g["mask_qk"][:, :], compare_op=ALU.is_ge, fill=NEG,
                               base=0, pattern=[[-1, P]], channel_multiplier=1).then_inc(consts, 1)
            pool.affine_select(out=g["mask_kq"][:, :], in_=g["mask_kq"][:, :], compare_op=ALU.is_ge, fill=NEG,
                               base=0, pattern=[[1, P]], channel_multiplier=-1).then_inc(consts, 1)

        @block.tensor
        def _(pe):
            pe.wait_ge(consts, 9 + PARTS + 2)
            pe.wait_ge(loaded, 16 * N_LOADS)
            for i in range(3):
                pe.matmul(ps_a[0:DH, i, 0:P], lora_a[:, i, :], g["ident"][:, :], start=True, stop=True).then_inc(at_ready, 1)
            pe.wait_ge(at_copied, 3)
            for i in range(len(names)):
                if i >= 3:
                    pe.wait_ge(w_copied, i - 2)
                mm = pe.matmul(ps_w[:, i % 3, 0:P], w_nat[:, i, :], g["ident"][:, :], start=True, stop=i >= 3)
                if i < 3:
                    mm = pe.matmul(ps_w[:, i % 3, 0:P], lora_b[:, i, :], lora_at[:, i, :], start=False, stop=True)
                mm.then_inc(w_ready, 1)

        @block.vector
        def _(v):
            v.wait_ge(at_ready, 3)
            for i in range(3):
                v.tensor_scalar(lora_at[:, i, :], ps_a[0:DH, i, 0:P], 2.0, None, ALU.mult).then_inc(at_copied, 1)
            for i, n in enumerate(names):
                v.wait_ge(w_ready, i + 1)
                scale = DH ** -0.5 if n.endswith("Wq") else 1.0
                v.tensor_scalar(g["w_t"][:, i, :], ps_w[:, i % 3, 0:P], scale, None, ALU.mult).then_inc(w_copied, 1)
            v.wait_ge(w_copied, len(names))


def stats_buffers(m):
    d = {n: m.sb("ln_" + n, [P, TILES]) for n in ("sum", "dif", "m2", "sq", "var", "std")}
    d["raw"] = m.sb("ln_raw", [P, TILES, 6])
    d["step"] = m.sem("ln_step")
    d["raw_done"] = m.sem("ln_raw_done")
    d["var_ready"] = m.sem("ln_var_ready")
    d["std_ready"] = m.sem("ln_std_ready")
    d["uses"] = 0
    return d


def vector_stats(v, src, s, mean, rstd, use):
    with v.Fori(0, TILES // CT) as c:
        for k in range(CT):
            v.bn_stats(s["raw"][:, ds(c * CT + k, 1), :], src[:, ds(c * CT + k, 1), :]).then_inc(s["raw_done"], 1)
    v.wait_ge(s["raw_done"], TILES * (use + 1))
    raw, n = s["raw"], 4 * use
    v.tensor_tensor(s["sum"][:, :], raw[:, :, 1], raw[:, :, 4], ALU.add).then_inc(s["step"], 1)
    v.tensor_tensor(s["dif"][:, :], raw[:, :, 1], raw[:, :, 4], ALU.subtract).then_inc(s["step"], 1)
    v.tensor_tensor(s["m2"][:, :], raw[:, :, 2], raw[:, :, 5], ALU.add).then_inc(s["step"], 1)
    v.wait_ge(s["step"], 8 * use + 3)
    v.tensor_scalar(mean[:, :], s["sum"][:, :], 0.5, None, ALU.mult).then_inc(s["step"], 1)
    v.tensor_tensor(s["sq"][:, :], s["dif"][:, :], s["dif"][:, :], ALU.mult).then_inc(s["step"], 1)
    v.tensor_scalar(s["var"][:, :], s["m2"][:, :], 1.0 / P, EPS, ALU.mult, ALU.add).then_inc(s["step"], 1)
    v.wait_ge(s["step"], 8 * use + 6)
    v.scalar_tensor_tensor(s["m2"][:, :], s["sq"][:, :], 0.25, s["var"][:, :], ALU.mult, ALU.add).then_inc(s["var_ready"], 1)
    v.wait_ge(s["std_ready"], use + 1)
    v.reciprocal(rstd[:, :], s["std"][:, :]).then_inc(s["step"], 2)
    v.wait_ge(s["step"], 8 * use + 8)


def scalar_stats(act, s, use):
    act.wait_ge(s["var_ready"], use + 1)
    act.activation(s["std"][:, :], s["m2"][:, :], ACT.Sqrt).then_inc(s["std_ready"], 1)


def first_norm_stage(nc, g):
    with ExitStack() as ctx:
        m = Mem(nc, ctx, "first")
        s = stats_buffers(m)
        block = ctx.enter_context(nc.Block())

        @block.vector
        def _(v):
            vector_stats(v, g["x_tok"], s, g["mean"], g["rstd"], 0)

        @block.scalar
        def _(act):
            scalar_stats(act, s, 0)


def residual_stage(nc, g, tag, out=None):
    with ExitStack() as ctx:
        m = Mem(nc, ctx, tag)
        s = stats_buffers(m)
        y_mean, y_rstd = m.sb("y_mean", [P, TILES]), m.sb("y_rstd", [P, TILES])
        normed, added, stored = m.sem("normed"), m.sem("added"), m.sem("stored")
        x, y = g["x_tok"], g["y_tok"]
        block = ctx.enter_context(nc.Block())

        @block.vector
        def _(v):
            vector_stats(v, y, s, y_mean, y_rstd, 0)
            with v.Fori(0, NCH) as c:
                for k in range(CT):
                    t = c * CT + k
                    v.tensor_scalar(y[:, ds(t, 1), :], y[:, ds(t, 1), :], y_mean[:, ds(t, 1)], y_rstd[:, ds(t, 1)],
                                    ALU.subtract, ALU.mult).then_inc(normed, 1)
                v.wait_ge(normed, c * CT + CT)
                v.tensor_tensor(x[:, ds(c * CT, CT), :], x[:, ds(c * CT, CT), :], y[:, ds(c * CT, CT), :], ALU.add).then_inc(added, 1)
            v.wait_ge(added, NCH)
            if out is None:
                vector_stats(v, x, s, g["mean"], g["rstd"], 1)

        @block.scalar
        def _(act):
            scalar_stats(act, s, 0)
            if out is None:
                scalar_stats(act, s, 1)

        @block.sync
        def _(sp):
            if out is not None:
                o = out.rearrange("b (k p) e -> p (b k) e", p=P)
                with sp.Fori(0, NCH) as c:
                    sp.wait_ge(added, c + 1)
                    sp.dma_start(o[:, ds(c * CT, CT), :], x[:, ds(c * CT, CT), :]).then_inc(stored, 16)
                sp.wait_ge(stored, 16 * NCH)


def attn0_project_stage(nc, g, scratch):
    with ExitStack() as ctx:
        m = Mem(nc, ctx, "a0p")
        norm = m.sb("norm", [P, 2, CT, P])
        norm_t = m.sb("norm_t", [P, 2, CH])
        full = m.sb("full", [P, 2, 2, CH])
        rest = m.sb("rest", [P, 2, 2, 2, CH])
        parts = m.sb("parts", [P, 2, 2, 3, CH], bf16)
        ps_t = m.ps("ps_t", [P, 2, CH])
        ps_qk = m.ps("ps_qk", [P, 2, CH])
        ps_v = m.ps("ps_v", [P, CT, P])
        normed, turned, t_copied, qk_ready, full_ready, v_ready, v_copied, split = (
            m.sem(s) for s in ("normed", "turned", "t_copied", "qk_ready", "full_ready", "v_ready", "v_copied", "split"))
        stored = [m.sem("stored0"), m.sem("stored1")]
        SPLIT = 5 * 2
        block = ctx.enter_context(nc.Block())

        @block.vector
        def _(v):
            with v.Fori(0, NCH // 2) as pair:
                for u in range(2):
                    c = pair * 2 + u
                    v.wait_ge(turned, c * 1)
                    for k in range(CT):
                        t = c * CT + k
                        v.tensor_scalar(norm[:, u, k, :], g["x_tok"][:, ds(t, 1), :], g["mean"][:, ds(t, 1)], g["rstd"][:, ds(t, 1)],
                                        ALU.subtract, ALU.mult).then_inc(normed, 1)
                    v.wait_ge(stored[u], pair * 32)
                    v.wait_ge(full_ready, c * 2 + 2)
                    for i in range(2):
                        v.tensor_copy(parts[:, u, i, 0, :], full[:, u, i, :]).then_inc(split, 1)
                    v.wait_ge(split, c * SPLIT + 2)
                    for i in range(2):
                        v.tensor_tensor(rest[:, u, i, 0, :], full[:, u, i, :], parts[:, u, i, 0, :], ALU.subtract).then_inc(split, 1)
                    v.wait_ge(split, c * SPLIT + 4)
                    for i in range(2):
                        v.tensor_copy(parts[:, u, i, 1, :], rest[:, u, i, 0, :]).then_inc(split, 1)
                    v.wait_ge(split, c * SPLIT + 6)
                    for i in range(2):
                        v.tensor_tensor(parts[:, u, i, 2, :], rest[:, u, i, 0, :], parts[:, u, i, 1, :], ALU.subtract).then_inc(split, 2)

        @block.tensor
        def _(pe):
            with pe.Fori(0, NCH // 2) as pair:
                for u in range(2):
                    c = pair * 2 + u
                    pe.wait_ge(normed, c * CT + CT)
                    for k in range(CT):
                        mm = pe.transpose(ps_t[:, u, k * P:(k + 1) * P], norm[:, u, k, :], g["ident"][:, :])
                    mm.then_inc(turned, 1)
                    pe.wait_ge(t_copied, c + 1)
                    pe.wait_ge(full_ready, c * 2)
                    for i in range(2):
                        pe.matmul(ps_qk[:, i, :], g["w_t"][:, i, :], norm_t[:, u, :], start=True, stop=True).then_inc(qk_ready, 1)
                    pe.wait_ge(v_copied, c)
                    for k in range(CT):
                        mm = pe.matmul(ps_v[:, k, :], norm_t[:, u, k * P:(k + 1) * P], g["w_t"][:, 2, :], start=True, stop=True)
                    mm.then_inc(v_ready, 1)

        @block.scalar
        def _(act):
            with act.Fori(0, NCH // 2) as pair:
                for u in range(2):
                    c = pair * 2 + u
                    act.wait_ge(turned, c + 1)
                    act.wait_ge(v_ready, c)
                    act.activation(norm_t[:, u, :], ps_t[:, u, :], ACT.Copy).then_inc(t_copied, 1)
                    for i in range(2):
                        act.wait_ge(qk_ready, c * 2 + i + 1)
                        act.wait_ge(split, c * SPLIT)
                        act.activation(full[:, u, i, :], ps_qk[:, i, :], ACT.Copy).then_inc(full_ready, 1)
                    act.wait_ge(v_ready, c + 1)
                    act.activation(g["v_tok"][:, ds(c * CT, CT), :], ps_v[:, :, :], ACT.Copy).then_inc(v_copied, 1)

        @block.sync
        def _(sp):
            dst = scratch["qk_parts"].rearrange("i s f t -> f i s t")
            with sp.Fori(0, NCH // 2) as pair:
                for u in range(2):
                    c = pair * 2 + u
                    sp.wait_ge(split, c * SPLIT + SPLIT)
                    for i in range(2):
                        sp.dma_start(dst[:, i, :, ds(c * CH, CH)], parts[:, u, i, :, :]).then_inc(stored[u], 16)
            for u in range(2):
                sp.wait_ge(stored[u], 16 * NCH)


def attn0_heads_stage(nc, g, scratch, io):
    HEADS = B * H
    RING = 4
    STEPS = HEADS // RING
    KB = T // P
    HALF = T // 2
    ST = [(kb, 1, min(HALF, T - kb * P)) for kb in range(KB)] + [(kb, 0, HALF - kb * P) for kb in range(KB // 2)]
    S = []
    for qb in range(KB):
        w = (qb + 1) * P
        S.append((qb, 0, min(w, HALF)))
        if w > HALF:
            S.append((qb, 1, w - HALF))
    N = len(ST)
    assert len(S) == N
    LOADED = (6 + 3 + 1) * 16
    with ExitStack() as ctx:
        m = Mem(nc, ctx, "a0h")
        q_st = m.sb("q_st", [P, RING, T], bf16)
        k_st = m.sb("k_st", [P, RING, T], bf16)
        v_st = m.sb("v_st", [P, 2, KB, 32])
        probs = m.sb("probs", [P, N, HALF])
        group_sum = m.sb("group_sum", [P, 32])
        o_sb = m.sb("o_sb", [P, 2, HALF])
        o_sum = m.sb("o_sum", [64, HALF])
        mx = m.sb("mx", [P, 2, 2, KB])
        nm = m.sb("nm", [P, 2, 2 * KB], bf16)
        nm_t = m.sb("nm_t", [P, 2, P], bf16)
        ps_s = m.ps("ps_s", [P, 2, HALF])
        ps_st = m.ps("ps_st", [P, 3, HALF])
        ps_o = m.ps("ps_o", [P, 2, HALF])
        ps_misc = m.ps("ps_misc", [P, HALF])
        ps_nm = ps_misc[96:96 + 2 * KB, 0:P // 2].bitcast(bf16)
        init = m.sem("init")
        gs_init = m.sem("gs_init")
        consts = m.sem("consts")
        qk_loaded = [m.sem(f"qk_loaded{i}") for i in range(RING)]
        s_ready, s_used = m.sem("s_ready"), m.sem("s_used")
        st_ready, p_ready = m.sem("st_ready"), m.sem("p_ready")
        pv_done = m.sem("pv_done")
        max_done, nm_ready, nm_turned, nm_copied = m.sem("max_done"), m.sem("nm_ready"), m.sem("nm_turned"), m.sem("nm_copied")
        m_step = m.sem("m_step")
        m_loaded = [m.sem(f"m_loaded{i}") for i in range(RING)]
        v_ready = m.sem("v_ready")
        o_copied, summed, sum_copied, o_stored = m.sem("o_copied"), m.sem("summed"), m.sem("sum_copied"), m.sem("o_stored")
        block = ctx.enter_context(nc.Block())

        def at(i, u, k=0):
            r, slot = i + (u + k) // RING, (u + k) % RING
            return r * RING + slot, slot, r, r // (H // RING), (r % (H // RING)) * RING + slot

        parts = scratch["qk_parts"]

        @block.sync
        def _(sp):
            for u in range(RING):
                sp.dma_start(k_st[48:P, u, :], io["key_rows"]).then_inc(consts, 16)
                sp.dma_start(q_st[48:P, u, :], io["query_rows"]).then_inc(consts, 16)
            sp.wait_ge(consts, 2 * 16 * RING)

            def load_head(i, u, k=0):
                _, slot, _, b, h = at(i, u, k)
                tok = ds(b * T, T)
                for part, n, row in ((0, 3, 0), (1, 2, 24), (2, 1, 40)):
                    for c in range(n):
                        sp.dma_start(q_st[row + c * DH:row + (c + 1) * DH, slot, :],
                                     parts[0, part, ds(h * DH, DH), tok]).then_inc(qk_loaded[slot], 16)
                for n, row in ((3, 0), (2, 24), (1, 40)):
                    sp.dma_start(k_st[row:row + n * DH, slot, :], parts[1, 0:n, ds(h * DH, DH), tok]).then_inc(qk_loaded[slot], 16)
                sp.dma_start(q_st[48:56, slot, :], io["slope_rows"][ds(h, 1), :, :].rearrange("a r t -> (a r) t")).then_inc(qk_loaded[slot], 16)

            def load_max(i, u, k=0):
                t, slot, _, _, _ = at(i, u, k)
                sp.wait_ge(nm_copied, t + 1)
                sp.dma_start(q_st[54:56, slot, :].rearrange("r (q c) -> r q c", c=P), nm_t[96:96 + 2 * KB, slot % 2, :]).then_inc(m_loaded[slot], 16)

            def store(i, u, k=0):
                t, _, _, b, h = at(i, u, k)
                sp.wait_ge(sum_copied, t + 2)
                for half in range(2):
                    sp.dma_start(scratch["o_raw"][ds(h, 1), :, ds(b * T + half * HALF, HALF)].rearrange("a r t -> (a r) t"),
                                 o_sum[32 * half:32 * half + DH + 1, :]).then_inc(o_stored, 16)

            def step(i, u, loads, maxes, prev):
                if loads:
                    sp.wait_ge(st_ready, (i * RING + u) * N)
                    load_head(i, u, 3)
                if prev:
                    store(i, u, -1)
                if maxes:
                    load_max(i, u, 2)

            for u in range(3):
                load_head(0, u)
            load_max(0, 0)
            load_max(0, 1)
            for u in range(RING):
                step(0, u, True, True, u > 0)
            with sp.Fori(1, STEPS - 1) as i:
                for u in range(RING):
                    step(i, u, True, True, True)
            for u in range(RING):
                step(STEPS - 1, u, u + 3 < RING, u + 2 < RING, True)
            store(STEPS - 1, RING - 1)
            sp.wait_ge(o_stored, 2 * 16 * HEADS)

        @block.gpsimd
        def _(pool):
            pool.memset(group_sum[:, :], 0.0).then_inc(gs_init, 1)
            for gq in range(4):
                pool.wait_ge(gs_init, gq + 1)
                pool.affine_select(out=group_sum[:, 0:DH + 1], in_=group_sum[:, 0:DH + 1], compare_op=ALU.not_equal, fill=1.0,
                                   base=-32 * gq, pattern=[[-1, DH + 1]], channel_multiplier=1).then_inc(gs_init, 1)
            pool.memset(v_st[:, :, :, :], 0.0).then_inc(init, 1)
            pool.memset(mx[:, :, :, :], NEG).then_inc(init, 1)
            pool.wait_ge(init, 2)
            pool.memset(v_st[:, :, :, DH:DH + 1], 1.0).then_inc(init, 1)
            pool.memset(probs[:, KB:N, :], 0.0).then_inc(pv_done, 3)
            pool.wait_ge(init, 3)
            with pool.Fori(0, STEPS) as i:
                for u in range(RING):
                    t, _, _, b, h = at(i, u)
                    pool.wait_ge(pv_done, t * 3)
                    pool.tensor_copy(v_st[:, u % 2, :, 0:DH], g["v_tok"][:, ds(b * KB, KB), ds(h * DH, DH)]).then_inc(v_ready, 1)

        @block.tensor
        def _(pe):
            def s_unit(i, u, k, n):
                t, slot, r, _, _ = at(i, u, k)
                qb, half, w = S[n]
                bank, k0 = n % 2, half * HALF
                if n == 0:
                    pe.wait_ge(qk_loaded[slot], (r + 1) * LOADED)
                pe.wait_ge(s_used, t * N + n + 1)
                diag = qb * P - k0
                masked = 0 <= diag < w
                mm = pe.matmul(ps_s[:, bank, 0:w], q_st[:, slot, qb * P:(qb + 1) * P], k_st[:, slot, k0:k0 + w],
                               start=True, stop=not masked)
                if masked:
                    mm = pe.matmul(ps_s[:, bank, diag:diag + P], g["ident_h"][:, :], g["mask_qk"][:, :], start=False, stop=True)
                mm.then_inc(s_ready, 1)

            def st_unit(i, u, n):
                t, slot, r, _, _ = at(i, u)
                kb, half, w = ST[n]
                bank, q0 = n % 3, (half + 1) * HALF - w
                if n == 0:
                    pe.wait_ge(m_loaded[slot], (r + 1) * 16)
                pe.wait_ge(p_ready, t * N + n + 1)
                masked = q0 == kb * P
                mm = pe.matmul(ps_st[:, bank, 0:w], k_st[:, slot, kb * P:(kb + 1) * P], q_st[:, slot, q0:q0 + w],
                               start=True, stop=not masked)
                if masked:
                    mm = pe.matmul(ps_st[:, bank, 0:P], g["ident_h"][:, :], g["mask_kq"][:, :], start=False, stop=True)
                mm.then_inc(st_ready, 1)

            def times_v(i, u, k, first, half):
                t, slot, _, _, _ = at(i, u, k)
                if first != KB:
                    pe.wait_ge(v_ready, t + 1)
                pe.wait_ge(p_ready, 3 + t * N + first + 4)
                if first != 4:
                    pe.wait_ge(o_copied, t * 2 + (1 if half else 2))
                for q in range(4):
                    kb, _, w = ST[first + q]
                    w = w if half else HALF
                    mm = pe.matmul(ps_o[32 * q:32 * q + 32, half, HALF - w:HALF], v_st[:, slot % 2, kb, :], probs[:, first + q, 0:w],
                                   start=first != 4, stop=first != 0)
                mm.then_inc(pv_done, 1)

            def group_sums(i, u, k=0):
                t, _, _, _, _ = at(i, u, k)
                pe.wait_ge(o_copied, t * 2 + 4)
                pe.wait_ge(sum_copied, t + 1)
                for half in range(2):
                    mm = pe.matmul(ps_misc[32 * half:32 * half + 32, :], group_sum[:, :], o_sb[:, half, :], start=True, stop=True)
                mm.then_inc(summed, 1)

            def turn_max(i, u, k=0):
                t, slot, _, _, _ = at(i, u, k)
                pe.wait_ge(nm_ready, t + 1)
                pe.wait_ge(nm_copied, t)
                pe.transpose(ps_nm, nm[:, slot % 2, :], g["ident_h"][:, :]).then_inc(nm_turned, 1)

            def step(i, u, ahead, prev):
                for n in range(N):
                    st_unit(i, u, n)
                    if ahead:
                        s_unit(i, u, 2, n)
                    if n == 2 and prev:
                        times_v(i, u, -1, KB, 0)
                    if n == 5 and prev:
                        group_sums(i, u, -1)
                    if n == 7:
                        times_v(i, u, 0, 0, 1)
                times_v(i, u, 0, 4, 1)
                if ahead:
                    turn_max(i, u, 2)

            pe.wait_ge(consts, 2 * 16 * RING)
            pe.wait_ge(gs_init, 5)
            pe.wait_ge(pv_done, 3)
            for u in range(2):
                for n in range(N):
                    s_unit(0, u, 0, n)
                turn_max(0, u)
            for u in range(RING):
                step(0, u, True, u > 0)
            with pe.Fori(1, STEPS - 1) as i:
                for u in range(RING):
                    step(i, u, True, True)
            for u in range(RING):
                step(STEPS - 1, u, u + 2 < RING, True)
            times_v(STEPS - 1, RING - 1, 0, KB, 0)
            group_sums(STEPS - 1, RING - 1)

        @block.vector
        def _(v):
            v.wait_ge(init, 3)
            v.sem_inc(s_used, 2)
            with v.Fori(0, STEPS) as i:
                for u in range(RING):
                    t, _, _, _, _ = at(i, u)
                    b2 = u % 2
                    for n, (qb, half, w) in enumerate(S):
                        v.wait_ge(s_ready, t * N + n + 1)
                        v.reduce_max(mx[:, b2, half, qb:qb + 1], ps_s[:, n % 2, 0:w], AX.X).then_inc(s_used, 1)
                    v.wait_ge(s_used, t * N + N + 2)
                    v.tensor_tensor(mx[:, b2, 0, :], mx[:, b2, 0, :], mx[:, b2, 1, :], ALU.max).then_inc(m_step, 1)
                    v.wait_ge(m_step, t * 2 + 1)
                    v.tensor_scalar(nm[:, b2, 0:KB], mx[:, b2, 0, :], -1.0, None, ALU.mult).then_inc(m_step, 1)
                    v.wait_ge(m_step, t * 2 + 2)
                    v.scalar_tensor_tensor(nm[:, b2, KB:2 * KB], mx[:, b2, 0, :], -1.0, nm[:, b2, 0:KB],
                                           ALU.mult, ALU.subtract).then_inc(nm_ready, 1)
                    v.wait_ge(nm_turned, t + 1)
                    v.wait_ge(m_loaded[(u + 2) % RING], (i + u // 2) * 16)
                    v.tensor_copy(nm_t[96:96 + 2 * KB, b2, :], ps_nm).then_inc(nm_copied, 1)

        @block.scalar
        def _(act):
            act.sem_inc(p_ready, 3)
            act.sem_inc(o_copied, 2)
            act.sem_inc(sum_copied, 1)

            def exps(i, u, lo, hi):
                t, _, _, _, _ = at(i, u)
                for n in range(lo, hi):
                    kb, half, w = ST[n]
                    if n % 4 == 0:
                        act.wait_ge(pv_done, t * 3 + 1 + n // 4)
                    act.wait_ge(st_ready, t * N + n + 1)
                    o = HALF - w if n >= KB else 0
                    act.activation(probs[:, n, o:o + w], ps_st[:, n % 3, 0:w], ACT.Exp).then_inc(p_ready, 1)

            def outputs(i, u, k, half):
                t, _, _, _, _ = at(i, u, k)
                act.wait_ge(pv_done, t * 3 + (5 if half else 6))
                act.wait_ge(summed, t)
                act.activation(o_sb[:, half, :], ps_o[:, half, :], ACT.Copy).then_inc(o_copied, 1)

            def sums(i, u, k=0):
                t, _, _, _, _ = at(i, u, k)
                act.wait_ge(summed, t + 1)
                act.wait_ge(o_stored, t * 32)
                act.activation(o_sum[:, :], ps_misc[0:64, :], ACT.Copy).then_inc(sum_copied, 1)

            def step(i, u, prev):
                exps(i, u, 0, 5)
                if prev:
                    outputs(i, u, -1, 0)
                exps(i, u, 5, 9)
                if prev:
                    sums(i, u, -1)
                exps(i, u, 9, N)
                outputs(i, u, 0, 1)

            for u in range(RING):
                step(0, u, u > 0)
            with act.Fori(1, STEPS) as i:
                for u in range(RING):
                    step(i, u, True)
            outputs(STEPS - 1, RING - 1, 0, 0)
            sums(STEPS - 1, RING - 1)


def attn0_output_stage(nc, g, scratch):
    with ExitStack() as ctx:
        m = Mem(nc, ctx, "a0o")
        l_sum = m.sb("l_sum", [P, CH])
        l_inv = m.sb("l_inv", [P, CH])
        o_t = m.sb("o_t", [P, 2, CH])
        inv_t = m.sb("inv_t", [P, 2, CH])
        on_t = m.sb("on_t", [P, 2, CH])
        ps_y = m.ps("ps_y", [P, 2, CT, P])
        l_loaded, inverted, inv_stored, loaded, divided, projected, copied = (
            m.sem(s) for s in ("l_loaded", "inverted", "inv_stored", "loaded", "divided", "projected", "copied"))
        loaded = [m.sem("loaded0"), m.sem("loaded1")]
        block = ctx.enter_context(nc.Block())

        @block.sync
        def _(sp):
            for h in range(H):
                sp.dma_start(l_sum[h * NCH:(h + 1) * NCH, :], scratch["o_raw"][h, DH, :].rearrange("(c t) -> c t", t=CH)).then_inc(l_loaded, 16)
            sp.wait_ge(inverted, 1)
            sp.dma_start(scratch["l_inv"].rearrange("h (c t) -> (h c) t", t=CH), l_inv[:, :]).then_inc(inv_stored, 16)
            sp.wait_ge(inv_stored, 16)
            with sp.Fori(0, NCH // 2) as pair:
                for u in range(2):
                    c = pair * 2 + u
                    sp.wait_ge(divided, c)
                    inv = scratch["l_inv"][:, ds(c * CH, CH)]
                    for h in range(H):
                        sp.dma_start(o_t[h * DH:(h + 1) * DH, u, :], scratch["o_raw"][h, 0:DH, ds(c * CH, CH)]).then_inc(loaded[u], 16)
                        sp.dma_start(inv_t[h * DH:(h + 1) * DH, u, :],
                                     scratch["l_inv"][h:h + 1, ds(c * CH, CH)].to_broadcast([DH, CH])).then_inc(loaded[u], 16)

        @block.vector
        def _(v):
            v.wait_ge(l_loaded, 16 * H)
            v.reciprocal(l_inv[:, :], l_sum[:, :]).then_inc(inverted, 1)
            with v.Fori(0, NCH // 2) as pair:
                for u in range(2):
                    c = pair * 2 + u
                    v.wait_ge(loaded[u], (pair + 1) * 32 * H)
                    v.wait_ge(projected, c)
                    v.tensor_tensor(on_t[:, u, :], o_t[:, u, :], inv_t[:, u, :], ALU.mult).then_inc(divided, 1)

        @block.tensor
        def _(pe):
            with pe.Fori(0, NCH // 2) as pair:
                for u in range(2):
                    c = pair * 2 + u
                    pe.wait_ge(divided, c + 1)
                    pe.wait_ge(copied, c)
                    for k in range(CT):
                        mm = pe.matmul(ps_y[:, u, k, :], on_t[:, u, k * P:(k + 1) * P], g["w_t"][:, 3, :], start=True, stop=True)
                    mm.then_inc(projected, 1)

        @block.scalar
        def _(act):
            with act.Fori(0, NCH // 2) as pair:
                for u in range(2):
                    c = pair * 2 + u
                    act.wait_ge(projected, c + 1)
                    act.activation(g["y_tok"][:, ds(c * CT, CT), :], ps_y[:, u, :, :], ACT.Copy).then_inc(copied, 1)


E_ = 8
PARTS = 3


def route_buffers(m):
    d = {n: m.sb("route_" + n, [P, TILES, E_]) for n in ("eq", "sel1", "sel2", "rest", "gate", "tmp")}
    d.update({n: m.sb("route_" + n, [P, TILES]) for n in ("first", "v1", "v2", "w1", "w2")})
    d["step"] = m.sem("route_step")
    return d


class Chain:

    def __init__(self, v, sem):
        self.v, self.sem, self.n = v, sem, 0

    def __call__(self, instruction):
        self.n += 1
        instruction.then_inc(self.sem, 1)
        self.v.wait_ge(self.sem, self.n)


def per_tile(ap):
    return ap[:, :].unsqueeze(2).to_broadcast([P, TILES, E_])


def top_two(v, step, r, scores, g):
    place = g["place"][:, :].unsqueeze(1).to_broadcast([P, TILES, E_])
    for value, sel, src in (("v1", "sel1", scores), ("v2", "sel2", r["rest"])):
        step(v.reduce_max(r[value][:, :], src[:, :, :], AX.X))
        step(v.tensor_tensor(r["eq"][:, :, :], src[:, :, :], per_tile(r[value]), ALU.is_equal))
        step(v.tensor_tensor(r["eq"][:, :, :], r["eq"][:, :, :], place, ALU.mult))
        step(v.tensor_reduce(r["first"][:, :], r["eq"][:, :, :], AX.X, ALU.min))
        step(v.tensor_tensor(r[sel][:, :, :], per_tile(r["first"]), place, ALU.is_equal))
        if sel == "sel1":
            step(v.scalar_tensor_tensor(r["rest"][:, :, :], r["sel1"][:, :, :], NEG, scores[:, :, :], ALU.mult, ALU.add))


def split_gates(v, step, r, parts):
    step(v.tensor_copy(parts[:, :, 0, :], r["gate"][:, :, :]))
    step(v.tensor_tensor(r["rest"][:, :, :], r["gate"][:, :, :], parts[:, :, 0, :], ALU.subtract))
    step(v.tensor_copy(parts[:, :, 1, :], r["rest"][:, :, :]))
    step(v.tensor_tensor(parts[:, :, 2, :], r["rest"][:, :, :], parts[:, :, 1, :], ALU.subtract))


def gate_rows_stage(nc, g, parts, gate_t, tag):
    with ExitStack() as ctx:
        m = Mem(nc, ctx, tag)
        held = m.sb("held", [P, 2, CT, PARTS * E_], bf16)
        ps_g = m.ps("ps_g", [P, 2, 2 * CH], bf16)
        zeroed, picked, turned, copied = (m.sem(s) for s in ("zeroed", "picked", "turned", "copied"))
        block = ctx.enter_context(nc.Block())

        @block.gpsimd
        def _(pool):
            pool.memset(gate_t[:, :], 0.0).then_inc(zeroed, 1)
            pool.wait_ge(zeroed, 1)

        @block.vector
        def _(v):
            with v.Fori(0, NCH // 2) as pair:
                for u in range(2):
                    c = pair * 2 + u
                    v.wait_ge(turned, c)
                    v.tensor_copy(held[:, u, :, :], parts[:, ds(c * CT, CT), :, :].rearrange("p k s e -> p k (s e)")).then_inc(picked, 1)

        @block.tensor
        def _(pe):
            with pe.Fori(0, NCH // 2) as pair:
                for u in range(2):
                    c = pair * 2 + u
                    pe.wait_ge(picked, c + 1)
                    pe.wait_ge(copied, c)
                    for k in range(CT):
                        mm = pe.transpose(ps_g[0:PARTS * E_, u, k * P:(k + 1) * P], held[:, u, k, :], g["ident_h"][:, :])
                    mm.then_inc(turned, 1)

        @block.scalar
        def _(act):
            act.wait_ge(zeroed, 1)
            with act.Fori(0, NCH // 2) as pair:
                for u in range(2):
                    c = pair * 2 + u
                    act.wait_ge(turned, c + 1)
                    act.activation(gate_t[0:PARTS * E_, ds(c * CH, CH)], ps_g[0:PARTS * E_, u, 0:CH], ACT.Copy).then_inc(copied, 1)
            act.wait_ge(copied, NCH)


LIMIT, ALPHA = 7.0, 1.702


def moe0_weights_stage(nc, g, io, w):
    with ExitStack() as ctx:
        m = Mem(nc, ctx, "m0w")
        up = m.sb("up", [P, E_, 2, P], bf16)
        down = m.sb("down", [P, E_, P], bf16)
        gate = m.sb("gate", [E_, P], bf16)
        b1 = m.sb("b1", [E_, P, 2], bf16)
        ps_w = m.ps("ps_w", [P, 4, E_, P], bf16)
        loaded, b2_loaded, rows_loaded, turned, copied, zeroed = (
            m.sem(s) for s in ("loaded", "b2_loaded", "rows_loaded", "turned", "copied", "zeroed"))
        block = ctx.enter_context(nc.Block())

        @block.sync
        def _(sp):
            sp.dma_start(up[:, :, :, :], io["L0_ffn_mlp1_weight"].rearrange("e (i s) h -> i e s h", s=2)).then_inc(loaded, 16)
            sp.dma_start(down[:, :, :], io["L0_ffn_mlp2_weight"].rearrange("e h i -> h e i")).then_inc(loaded, 16)
            sp.dma_start(gate[:, :], io["L0_ffn_gate_weight"]).then_inc(loaded, 16)
            sp.dma_start(b1[:, :, :], io["L0_ffn_mlp1_bias"].rearrange("e (i s) -> e i s", s=2)).then_inc(loaded, 16)
            sp.dma_start(w["norm_w"][:, :], io["L0_ffn_norm_weight"].partition_broadcast(P)).then_inc(rows_loaded, 16)
            sp.dma_start(w["gate_b"][:, :], io["L0_ffn_gate_bias"].partition_broadcast(P)).then_inc(rows_loaded, 16)
            sp.wait_ge(zeroed, 1)
            for s in range(PARTS):
                sp.dma_start(w["b2_rows"][s * E_:(s + 1) * E_, :], io["L0_ffn_mlp2_bias"]).then_inc(b2_loaded, 16)
            sp.wait_ge(b2_loaded, 16 * PARTS)
            sp.wait_ge(rows_loaded, 32)

        @block.gpsimd
        def _(pool):
            pool.memset(w["b2_rows"][:, :], 0.0).then_inc(zeroed, 1)

        @block.tensor
        def _(pe):
            pe.wait_ge(loaded, 64)
            for s in range(2):
                for e in range(E_):
                    mm = pe.transpose(ps_w[:, s, e, :], up[:, e, s, :], g["ident_h"][:, :])
            for e in range(E_):
                mm = pe.transpose(ps_w[:, 2, e, :], down[:, e, :], g["ident_h"][:, :])
            for s in range(2):
                mm = pe.transpose(ps_w[:, 3, s, 0:E_], b1[:, :, s], g["ident_h"][0:E_, 0:E_])
            mm = pe.transpose(ps_w[:, 3, 2, 0:E_], gate[:, :], g["ident_h"][0:E_, 0:E_])
            mm.then_inc(turned, 1)

        @block.vector
        def _(v):
            v.wait_ge(turned, 1)
            for s in range(2):
                v.tensor_copy(w["up_t"][:, s, :, :], ps_w[:, s, :, :]).then_inc(copied, 1)
                v.tensor_copy(w["b1_t"][:, s, :], ps_w[:, 3, s, 0:E_]).then_inc(copied, 1)
            v.tensor_copy(w["down_t"][:, :, :], ps_w[:, 2, :, :]).then_inc(copied, 1)
            v.tensor_copy(w["gate_w"][:, :], ps_w[:, 3, 2, 0:E_]).then_inc(copied, 1)
            v.wait_ge(copied, 6)


def moe0_norm_stage(nc, g, w, xc, rms_inv):
    with ExitStack() as ctx:
        m = Mem(nc, ctx, "m0n")
        sq = m.sb("sq", [P, 2, CT, P])
        ss, root = m.sb("ss", [P, TILES]), m.sb("root", [P, TILES])
        normed, squared, mean_ready, rooted, inverted = (m.sem(s) for s in ("normed", "squared", "mean_ready", "rooted", "inverted"))
        block = ctx.enter_context(nc.Block())

        @block.vector
        def _(v):
            with v.Fori(0, NCH) as c:
                for k in range(CT):
                    t = c * CT + k
                    v.tensor_scalar(xc[:, ds(t, 1), :], g["x_tok"][:, ds(t, 1), :], g["mean"][:, ds(t, 1)], g["rstd"][:, ds(t, 1)],
                                    ALU.subtract, ALU.mult).then_inc(normed, 1)
            v.wait_ge(squared, TILES)
            v.tensor_scalar(ss[:, :], ss[:, :], 1.0 / P, EPS, ALU.mult, ALU.add).then_inc(mean_ready, 1)
            v.wait_ge(rooted, 1)
            v.reciprocal(rms_inv[:, :], root[:, :]).then_inc(inverted, 1)
            v.wait_ge(inverted, 1)

        @block.scalar
        def _(act):
            with act.Fori(0, NCH // 2) as pair:
                for u in range(2):
                    for k in range(CT):
                        t = (pair * 2 + u) * CT + k
                        act.wait_ge(normed, t + 1)
                        act.wait_ge(squared, (pair * 2) * CT)
                        act.activation(sq[:, u, k, :], xc[:, ds(t, 1), :], ACT.Square, accum_out=ss[:, ds(t, 1)]).then_inc(squared, 1)
            act.wait_ge(mean_ready, 1)
            act.activation(root[:, :], ss[:, :], ACT.Sqrt).then_inc(rooted, 1)


def moe0_route_stage(nc, g, w, xc, rms_inv, nf_t, gate_parts):
    with ExitStack() as ctx:
        m = Mem(nc, ctx, "m0r")
        nf = m.sb("nf", [P, 2, CT, P], bf16)
        nf_c = m.sb("nf_c", [P, 2, CH], bf16)
        logits = m.sb("logits", [P, TILES, E_])
        rounded = m.sb("rounded", [P, TILES, E_], bf16)
        r = route_buffers(m)
        ps_t = m.ps("ps_t", [P, 2, 2 * CH], bf16)
        ps_l = m.ps("ps_l", [P, 2, CT, P])
        scaled, turned, t_copied, c_copied, scored, l_copied, diff_ready, weights_ready = (
            m.sem(s) for s in ("scaled", "turned", "t_copied", "c_copied", "scored", "l_copied", "diff_ready", "weights_ready"))
        block = ctx.enter_context(nc.Block())

        @block.vector
        def _(v):
            with v.Fori(0, NCH // 2) as pair:
                for u in range(2):
                    c = pair * 2 + u
                    v.wait_ge(turned, c)
                    for k in range(CT):
                        t = c * CT + k
                        v.scalar_tensor_tensor(nf[:, u, k, :], xc[:, ds(t, 1), :].rearrange("p a e -> p (a e)"), rms_inv[:, ds(t, 1)], w["norm_w"][:, :],
                                               ALU.mult, ALU.mult).then_inc(scaled, 1)
            v.wait_ge(l_copied, NCH)
            step = Chain(v, r["step"])
            bias = w["gate_b"][:, :].unsqueeze(1).to_broadcast([P, TILES, E_])
            step(v.tensor_tensor(rounded[:, :, :], logits[:, :, :], bias, ALU.add))
            step(v.tensor_copy(logits[:, :, :], rounded[:, :, :]))
            top_two(v, step, r, logits, g)
            v.tensor_tensor(r["first"][:, :], r["v1"][:, :], r["v2"][:, :], ALU.subtract).then_inc(diff_ready, 1)
            v.wait_ge(weights_ready, 2)
            step(v.tensor_tensor(r["gate"][:, :, :], r["sel1"][:, :, :], per_tile(r["w1"]), ALU.mult))
            step(v.tensor_tensor(r["tmp"][:, :, :], r["sel2"][:, :, :], per_tile(r["w2"]), ALU.mult))
            step(v.tensor_tensor(r["gate"][:, :, :], r["gate"][:, :, :], r["tmp"][:, :, :], ALU.add))
            split_gates(v, step, r, gate_parts)

        @block.tensor
        def _(pe):
            with pe.Fori(0, NCH // 2) as pair:
                for u in range(2):
                    c = pair * 2 + u
                    pe.wait_ge(scaled, c * CT + CT)
                    pe.wait_ge(t_copied, c)
                    for k in range(CT):
                        mm = pe.transpose(ps_t[:, u, k * P:(k + 1) * P], nf[:, u, k, :], g["ident_h"][:, :])
                    mm.then_inc(turned, 1)
                    pe.wait_ge(t_copied, c + 1)
                    pe.wait_ge(l_copied, c)
                    for k in range(CT):
                        mm = pe.matmul(ps_l[:, u, k, 0:E_], nf_c[:, u, k * P:(k + 1) * P], w["gate_w"][:, :], start=True, stop=True)
                    mm.then_inc(scored, 1)

        @block.scalar
        def _(act):
            with act.Fori(0, NCH // 2) as pair:
                for u in range(2):
                    c = pair * 2 + u
                    act.wait_ge(turned, c + 1)
                    act.wait_ge(scored, c)
                    act.activation(nf_c[:, u, :], ps_t[:, u, 0:CH], ACT.Copy).then_inc(t_copied, 1)
                    act.wait_ge(t_copied, c + 1)
                    act.activation(nf_t[:, ds(c * CH, CH)], nf_c[:, u, :], ACT.Copy).then_inc(c_copied, 1)
                    act.wait_ge(scored, c + 1)
                    act.activation(logits[:, ds(c * CT, CT), :], ps_l[:, u, :, 0:E_], ACT.Copy).then_inc(l_copied, 1)
            act.wait_ge(diff_ready, 1)
            act.activation(r["w1"][:, :], r["first"][:, :], ACT.Sigmoid).then_inc(weights_ready, 1)
            act.activation(r["w2"][:, :], r["first"][:, :], ACT.Sigmoid, scale=-1.0).then_inc(weights_ready, 1)
            act.wait_ge(c_copied, NCH)


def moe0_experts_stage(nc, g, w, xc, nf_t, gate_t):
    with ExitStack() as ctx:
        m = Mem(nc, ctx, "m0e")
        nf_c = m.sb("nf_c", [P, 2, CH], bf16)
        gate_c = m.sb("gate_c", [P, 2, CH], bf16)
        glu0, glu, sig, lin0, lin = (m.sb(n, [P, 2, CH]) for n in ("glu0", "glu", "sig", "lin0", "lin"))
        prod, gated, hid = (m.sb(n, [P, 2, CH]) for n in ("prod", "gated", "hid"))
        comb = m.sb("comb", [P, 2, CH], bf16)
        summed = m.sb("summed", [P, 2, CT, P], bf16)
        ps_up = m.ps("ps_up", [P, 2, 2, CH])
        ps_g = m.ps("ps_g", [P, CH])
        ps_y = m.ps("ps_y", [P, CH])
        ps_c = m.ps("ps_c", [P, 2 * CH], bf16)
        (picked, up_ready, biased, glu_ready, lin_ready, sig_ready, prod_ready, gated_ready, gates_ready, hid_ready, y_ready,
         comb_ready, turned, sum_ready, y_copied) = (
            m.sem(s) for s in ("picked", "up_ready", "biased", "glu_ready", "lin_ready", "sig_ready", "prod_ready", "gated_ready",
                               "gates_ready", "hid_ready", "y_ready", "comb_ready", "turned", "sum_ready", "y_copied"))
        block = ctx.enter_context(nc.Block())

        @block.tensor
        def _(pe):
            def up(c, u, e):
                n, q = c * E_ + e, e % 2
                pe.wait_ge(biased, n * 2)
                for s in range(2):
                    mm = pe.matmul(ps_up[:, q, s, :], w["up_t"][:, s, e, :], nf_c[:, u, :], start=True, stop=True)
                    mm.then_inc(up_ready, 1)

            def gates(c, u, e):
                n = c * E_ + e
                pe.wait_ge(hid_ready, n)
                pe.matmul(ps_g[:, :], w["pick"][:, e, :], gate_c[:, u, :], start=True, stop=True).then_inc(gates_ready, 1)

            def down(c, e):
                n = c * E_ + e
                pe.wait_ge(hid_ready, n + 1)
                if e == 0:
                    pe.wait_ge(comb_ready, c)
                mm = pe.matmul(ps_y[:, :], w["down_t"][:, e, :], hid[:, e % 2, :], start=e == 0, stop=False)
                mm.then_inc(y_ready, 1)

            with pe.Fori(0, NCH // 2) as pair:
                for u in range(2):
                    c = pair * 2 + u
                    pe.wait_ge(picked, c * 2 + 2)
                    up(c, u, 0)
                    gates(c, u, 0)
                    for e in range(E_):
                        if e + 1 < E_:
                            up(c, u, e + 1)
                        down(c, e)
                        if e + 1 < E_:
                            gates(c, u, e + 1)
                    pe.matmul(ps_y[:, :], w["b2_rows"][:, :], gate_c[:, u, :], start=False, stop=True).then_inc(y_ready, 1)
                    pe.wait_ge(comb_ready, c + 1)
                    pe.wait_ge(sum_ready, c)
                    for k in range(CT):
                        mm = pe.transpose(ps_c[:, k * P:(k + 1) * P], comb[:, u, k * P:(k + 1) * P], g["ident_h"][:, :])
                    mm.then_inc(turned, 1)

        @block.scalar
        def _(act):
            with act.Fori(0, NCH // 2) as pair:
                for u in range(2):
                    c = pair * 2 + u
                    for e in range(E_):
                        n, q = c * E_ + e, e % 2
                        act.wait_ge(up_ready, n * 2 + 1)
                        act.wait_ge(lin_ready, n)
                        act.activation(glu0[:, q, :], ps_up[:, q, 0, :], ACT.Identity, bias=w["b1_t"][:, 0, e:e + 1]).then_inc(biased, 1)
                        act.wait_ge(up_ready, n * 2 + 2)
                        act.activation(lin0[:, q, :], ps_up[:, q, 1, :], ACT.Identity, bias=w["b1_t"][:, 1, e:e + 1]).then_inc(biased, 1)
                        act.wait_ge(glu_ready, n + 1)
                        act.wait_ge(gated_ready, n)
                        act.activation(sig[:, q, :], glu[:, q, :], ACT.Sigmoid, scale=ALPHA).then_inc(sig_ready, 1)
                    act.wait_ge(y_ready, (c + 1) * (E_ + 1))
                    act.wait_ge(turned, c)
                    act.activation(comb[:, u, :], ps_y[:, :], ACT.Copy).then_inc(comb_ready, 1)
                    act.wait_ge(sum_ready, c + 1)
                    act.activation(g["y_tok"][:, ds(c * CT, CT), :], summed[:, u, :, :], ACT.Copy).then_inc(y_copied, 1)

        @block.vector
        def _(v):
            with v.Fori(0, NCH // 2) as pair:
                for u in range(2):
                    c = pair * 2 + u
                    for e in range(E_):
                        n, q = c * E_ + e, e % 2
                        v.wait_ge(biased, n * 2 + 1)
                        v.wait_ge(sig_ready, n)
                        v.tensor_scalar(glu[:, q, :], glu0[:, q, :], LIMIT, None, ALU.min).then_inc(glu_ready, 1)
                        v.wait_ge(biased, n * 2 + 2)
                        v.tensor_scalar(lin[:, q, :], lin0[:, q, :], LIMIT, -LIMIT, ALU.min, ALU.max).then_inc(lin_ready, 1)
                        v.wait_ge(lin_ready, n + 1)
                        v.wait_ge(glu_ready, n + 1)
                        v.wait_ge(gated_ready, n)
                        v.scalar_tensor_tensor(prod[:, q, :], lin[:, q, :], 1.0, glu[:, q, :], ALU.add, ALU.mult).then_inc(prod_ready, 1)
                        v.wait_ge(gated_ready, n + 1)
                        v.wait_ge(gates_ready, n + 1)
                        v.wait_ge(y_ready, c * (E_ + 1) + e)
                        v.tensor_tensor(hid[:, q, :], gated[:, q, :], ps_g[:, :], ALU.mult).then_inc(hid_ready, 1)
                    v.wait_ge(turned, c + 1)
                    v.wait_ge(y_copied, c)
                    v.tensor_tensor(summed[:, u, :, :].rearrange("p k e -> p (k e)"), xc[:, ds(c * CT, CT), :].rearrange("p k e -> p (k e)"),
                                    ps_c[:, 0:CH], ALU.add).then_inc(sum_ready, 1)

        @block.gpsimd
        def _(pool):
            def pick(c, u):
                pool.wait_ge(y_ready, (c - 1) * (E_ + 1)) if not isinstance(c, int) else None
                pool.tensor_copy(nf_c[:, u, :], nf_t[:, ds(c * CH, CH)]).then_inc(picked, 1)
                pool.tensor_copy(gate_c[:, u, :], gate_t[:, ds(c * CH, CH)]).then_inc(picked, 1)

            pick(0, 0)
            pick(1, 1)

            def experts(c):
                for e in range(E_):
                    n, q = c * E_ + e, e % 2
                    pool.wait_ge(sig_ready, n + 1)
                    pool.wait_ge(prod_ready, n + 1)
                    pool.wait_ge(hid_ready, n)
                    pool.tensor_tensor(gated[:, q, :], prod[:, q, :], sig[:, q, :], ALU.mult).then_inc(gated_ready, 1)

            with pool.Fori(0, NCH // 2 - 1) as pair:
                for u in range(2):
                    c = pair * 2 + u
                    experts(c)
                    pick(c + 2, u)
            experts(NCH - 2)
            experts(NCH - 1)


WIN = 16
PAD = 16


def attn1_project_stage(nc, g, q_t, k_t, kp_t, v_t, v_rows):
    with ExitStack() as ctx:
        m = Mem(nc, ctx, "a1p")
        norm = m.sb("norm", [P, 2, CT, P])
        norm_t = m.sb("norm_t", [P, 2, CH])
        v_c = m.sb("v_c", [P, 2, CT, P])
        ps_t = m.ps("ps_t", [P, 2, CH])
        ps_p = m.ps("ps_p", [P, 4, CH])
        ps_v = m.ps("ps_v", [P, CT, P])
        normed, turned, t_copied, projected, p_copied, v_ready, v_copied, padded = (
            m.sem(s) for s in ("normed", "turned", "t_copied", "projected", "p_copied", "v_ready", "v_copied", "padded"))
        stored = [m.sem("stored0"), m.sem("stored1")]
        block = ctx.enter_context(nc.Block())
        weights = (4, 5, 7, 6)

        @block.vector
        def _(v):
            with v.Fori(0, B) as b:
                for u in range(2):
                    c = b * 2 + u
                    v.wait_ge(turned, c)
                    for k in range(CT):
                        t = c * CT + k
                        v.tensor_scalar(norm[:, u, k, :], g["x_tok"][:, ds(t, 1), :], g["mean"][:, ds(t, 1)], g["rstd"][:, ds(t, 1)],
                                        ALU.subtract, ALU.mult).then_inc(normed, 1)
                    v.wait_ge(v_ready, c + 1)
                    v.wait_ge(stored[u], b * 16)
                    v.tensor_copy(v_c[:, u, :, :], ps_v[:, :, :]).then_inc(v_copied, 1)

        @block.tensor
        def _(pe):
            with pe.Fori(0, B) as b:
                for u in range(2):
                    c = b * 2 + u
                    pe.wait_ge(normed, c * CT + CT)
                    for k in range(CT):
                        mm = pe.transpose(ps_t[:, u, k * P:(k + 1) * P], norm[:, u, k, :], g["ident"][:, :])
                    mm.then_inc(turned, 1)
                    pe.wait_ge(t_copied, c + 1)
                    for i in range(4):
                        pe.wait_ge(p_copied, c * 4 + 0)
                        pe.matmul(ps_p[:, i, :], g["w_t"][:, weights[i], :], norm_t[:, u, :], start=True, stop=True).then_inc(projected, 1)
                    pe.wait_ge(v_copied, c)
                    for k in range(CT):
                        mm = pe.matmul(ps_v[:, k, :], norm_t[:, u, k * P:(k + 1) * P], g["w_t"][:, 6, :], start=True, stop=True)
                    mm.then_inc(v_ready, 1)

        @block.scalar
        def _(act):
            with act.Fori(0, B) as b:
                for u in range(2):
                    c = b * 2 + u
                    act.wait_ge(turned, c + 1)
                    act.wait_ge(v_ready, c)
                    act.activation(norm_t[:, u, :], ps_t[:, u, :], ACT.Copy).then_inc(t_copied, 1)
                    for i, (dst, pad) in enumerate(((q_t, 0), (k_t, PAD), (kp_t, 0), (v_t, PAD))):
                        act.wait_ge(projected, c * 4 + i + 1)
                        act.activation(dst[:, ds(b, 1), pad + u * CH:pad + (u + 1) * CH].rearrange("p a t -> p (a t)"),
                                       ps_p[:, i, :], ACT.Copy).then_inc(p_copied, 1)
            act.wait_ge(p_copied, 4 * NCH)

        @block.gpsimd
        def _(pool):
            pool.memset(v_t[:, :, 0:PAD], 0.0).then_inc(padded, 1)
            pool.wait_ge(p_copied, 4 * NCH)
            pool.tensor_copy(k_t[:, :, 0:PAD], k_t[:, :, PAD:PAD + 1].to_broadcast([P, B, PAD])).then_inc(padded, 1)
            pool.wait_ge(padded, 2)

        @block.sync
        def _(sp):
            dst = v_rows.rearrange("(k p) e -> p k e", p=P)
            with sp.Fori(0, B) as b:
                for u in range(2):
                    c = b * 2 + u
                    sp.wait_ge(v_copied, c + 1)
                    sp.dma_start(dst[:, ds(c * CT, CT), :], v_c[:, u, :, :]).then_inc(stored[u], 16)
            for u in range(2):
                sp.wait_ge(stored[u], 16 * B)


BLK = 32
GK = 8
BLOCKS = NTOK // BLK
PER_SEQ = T // BLK
GROUPS = [(0, 0, 8), (1, 0, 16), (2, 0, 24), (0, 8, 32), (1, 16, 32), (2, 24, 32)]


def attn1_windows_stage(nc, g, io, q_t, k_t, kp_t, v_t, v_rows, z_t):
    with ExitStack() as ctx:
        m = Mem(nc, ctx, "a1w")
        W = 3 * BLK * WIN
        head_mask = m.sb("head_mask", [P, H])
        key_mask = m.sb("key_mask", [P, P])
        m_pick = m.sb("m_pick", [P, P], bf16)
        m_rows = m.sb("m_rows", [P, 2, 2, 3, BLK, WIN], bf16)
        r_mask = m.sb("r_mask", [P, 2, 3, BLK])
        qk = m.sb("qk", [P, 2, BLK, WIN])
        bd_k = m.sb("bd_k", [P, 2, BLK, H])
        v_raw = m.sb("v_raw", [P, 2, 4, P])
        bd_v = m.sb("bd_v", [P, 2, 4, P])
        probs = m.sb("probs", [P, 2, 3, BLK, WIN])
        pj = m.sb("pj", [P, 2, 3, BLK])
        r_raw = m.sb("r_raw", [P, 3, BLK])
        r_masked = m.sb("r_masked", [P, 3, BLK])
        r_max = m.sb("r_max", [P, 2, BLK])
        max_h = m.sb("max_h", [BLK, H])
        nm = m.sb("nm", [P, 2, H], bf16)
        uv = m.sb("uv", [P, BLK, WIN])
        z_raw, l_sum, l_inv = m.sb("z_raw", [P, BLK]), m.sb("l_sum", [P, BLK]), m.sb("l_inv", [P, BLK])
        ps_a = m.ps("ps_a", [P, 2, 3, BLK, WIN])
        ps_u = m.ps("ps_u", [P, BLK, WIN])
        ps_m = m.ps("ps_m", [P, CH])
        ps_max = ps_m[0:BLK, 0:P]
        ps_nm = ps_m[0:BLK, P:P + P // 2].bitcast(bf16)
        ps_l = ps_m[:, 2 * P:2 * P + 3 * BLK]
        (const_loaded, zeroed, qk_built, k_built, v_built, prior_done, logits_ready, r_ready, max_turned, nm_ready, nm_turned,
         rows_ready, m_added, p_ready, pj_ready, v_prior_done, u_ready, l_ready, u_read, l_read, z_ready, z_step, c_step, r_step) = (
            m.sem(s) for s in ("const_loaded", "zeroed", "qk_built", "k_built", "v_built", "prior_done", "logits_ready", "r_ready",
                               "max_turned", "nm_ready", "nm_turned", "rows_ready", "m_added", "p_ready", "pj_ready", "v_prior_done",
                               "u_ready", "l_ready", "u_read", "l_read", "z_ready", "z_step", "c_step", "r_step"))
        v_loaded = [m.sem("v_loaded0"), m.sem("v_loaded1")]
        N_CONST = 5 * 16
        PAIRS = BLOCKS // 2
        block = ctx.enter_context(nc.Block())

        def at(i, u, k=0):
            i, p = i + (u + k) // 2, (u + k) % 2
            half = PER_SEQ // 2
            later = 1 if p else ((i % half) + half - 1) // half
            return i * 2 + p, p, i, i // half, (i % half) * 2 * BLK + p * BLK, later

        def pairs(eng, step):
            for u in range(2):
                step(0, u, u > 0, True, True)
            with eng.Fori(1, PAIRS - 1) as i:
                for u in range(2):
                    step(i, u, True, True, True)
            for u in range(2):
                step(PAIRS - 1, u, True, u == 0, False)

        @block.sync
        def _(sp):
            sp.dma_start(head_mask[:, :], io["head_mask"]).then_inc(const_loaded, 16)
            sp.dma_start(key_mask[:, :], io["key_mask"]).then_inc(const_loaded, 16)
            sp.dma_start(m_pick[:, :], io["m_pick"]).then_inc(const_loaded, 16)
            sp.dma_start(m_rows[:, 0, :, :, :, :].rearrange("p a b c d -> p a (b c d)"), io["window_rows"]).then_inc(const_loaded, 16)
            sp.dma_start(m_rows[:, 1, :, :, :, :].rearrange("p a b c d -> p a (b c d)"), io["window_rows"]).then_inc(const_loaded, 16)
            sp.dma_start(r_mask[:, :, :, :].rearrange("p a b c -> p a (b c)"), io["window_mask"]).then_inc(zeroed, 16)

            def load(i, u):
                n, p, i, b, s0, _ = at(i, u)
                if not isinstance(n, int) or n >= 2:
                    sp.wait_ge(v_built, n - 1)
                rows = v_rows[ds(n * BLK, BLK), :]
                for k in range(GK):
                    src = bass.AP(rows.tensor, rows.offset + k * P, [[0, H], [GK * P, 4], [1, P]])
                    sp.dma_start(v_raw[k * H:(k + 1) * H, p, :, :], src).then_inc(v_loaded[p], 16)

            for u in range(2):
                load(0, u)
            with sp.Fori(1, PAIRS) as i:
                for u in range(2):
                    load(i, u)
            sp.wait_ge(zeroed, 16 + 3)

        @block.gpsimd
        def _(pool):
            pool.memset(bd_k[:, :, :, :], 0.0).then_inc(zeroed, 1)
            pool.memset(bd_v[:, :, :, :], 0.0).then_inc(zeroed, 1)
            pool.memset(nm[:, :, :], 0.0).then_inc(zeroed, 1)
            pool.wait_ge(const_loaded, N_CONST)
            pool.wait_ge(zeroed, 16 + 3)

            def build_keys(i, u, k=0, first=False):
                n, p, i, b, s0, _ = at(i, u, k)
                if not first:
                    pool.wait_ge(prior_done, n)
                keys = kp_t[:, ds(b, 1), ds(s0, BLK)].rearrange("p a t -> p (a t)").unsqueeze(2).to_broadcast([P, BLK, H])
                pool.tensor_tensor(bd_k[:, p, :, :], keys, head_mask[:, :].unsqueeze(1).to_broadcast([P, BLK, H]), ALU.mult).then_inc(k_built, 1)
                if not first:
                    pool.wait_ge(logits_ready, n - 1 if not isinstance(n, int) else max(n - 1, 0))
                queries = q_t[:, ds(b, 1), ds(s0, BLK)].rearrange("p a t -> p (a t)").unsqueeze(2).to_broadcast([P, BLK, WIN])
                window = view(k_t[:, ds(b, 1), ds(s0 + PAD - WIN + 1, 1)], [[1, BLK], [1, WIN]])
                pool.tensor_tensor(qk[:, p, :, :], queries, window, ALU.mult).then_inc(qk_built, 1)

            def build_values(i, u, first=False):
                n, p, i, b, s0, _ = at(i, u)
                pool.wait_ge(v_loaded[p], (i + 1) * 16 * GK)
                if not first:
                    pool.wait_ge(v_prior_done, n)
                pool.tensor_tensor(bd_v[:, p, :, :], v_raw[:, p, :, :], key_mask[:, :].unsqueeze(1).to_broadcast([P, 4, P]), ALU.mult).then_inc(v_built, 1)

            build_keys(0, 0, 0, True)
            build_keys(0, 1)

            def step(i, u, prev, ahead, ahead2):
                if ahead2:
                    build_keys(i, u, 2)
                build_values(i, u, not prev)

            pairs(pool, step)

        @block.tensor
        def _(pe):
            def group_keys(ring, p, q):
                return ring[:, p, q - 2] if q >= 2 else ring[:, 1 - p, q + 2]

            k_ring = bd_k[:, :, :, :].rearrange("p a (q k) h -> p a q (k h)", q=4)

            def logits(i, u, k=0):
                n, p, _, _, _, _ = at(i, u, k)
                pe.wait_ge(k_built, n + 1)
                pe.wait_ge(qk_built, n + 1)
                if not isinstance(n, int) or n >= 2:
                    pe.wait_ge(p_ready, n - 1)
                for q, (slot, lo, hi) in enumerate(GROUPS):
                    mm = pe.matmul(ps_a[:, p, slot, lo:hi, :], group_keys(k_ring, p, q), qk[:, p, lo:hi, :],
                                   start=q < 3, stop=False, skip_group_check=True)
                    if q == 1:
                        mm.then_inc(prior_done, 1)
                mm.then_inc(logits_ready, 1)

            def turn_max(i, u):
                n, p, _, _, _, _ = at(i, u)
                pe.wait_ge(r_ready, n + 1)
                if not isinstance(n, int) or n >= 2:
                    pe.wait_ge(l_read, n - 1)
                pe.transpose(ps_max, r_max[:, p, :], g["ident"][:, :]).then_inc(max_turned, 1)

            def turn_back(i, u):
                n, _, _, _, _, _ = at(i, u)
                pe.wait_ge(nm_ready, n + 1)
                pe.transpose(ps_nm, nm[:, :, :].rearrange("p a h -> p (a h)"), g["ident_h"][:, :]).then_inc(nm_turned, 1)

            def add_max(i, u):
                n, p, _, _, _, later = at(i, u)
                pe.wait_ge(rows_ready, n + 1)
                for slot in range(3):
                    rows = m_rows[:, p, ds(later, 1), slot, :, :].rearrange("p a s j -> p (a s) j")
                    mm = pe.matmul(ps_a[:, p, slot, :, :], m_pick[:, :], rows, start=False, stop=True, skip_group_check=True)
                mm.then_inc(m_added, 1)

            def times_v(i, u, k, groups):
                n, p, _, _, _, _ = at(i, u, k)
                if 2 in groups:
                    pe.wait_ge(v_built, n + 1)
                    pe.wait_ge(p_ready, n + 1)
                    pe.wait_ge(u_read, n)
                for q in groups:
                    slot, lo, hi = GROUPS[q]
                    mm = pe.matmul(ps_u[:, lo:hi, :], group_keys(bd_v, p, q), probs[:, p, slot, lo:hi, :],
                                   start=q == 2, stop=q == 4, skip_group_check=True)
                    if q == 1:
                        mm.then_inc(v_prior_done, 1)
                    if q == 4:
                        mm.then_inc(u_ready, 1)

            def sums(i, u, k=0):
                n, p, _, _, _, _ = at(i, u, k)
                pe.wait_ge(pj_ready, n + 1)
                pe.matmul(ps_l, key_mask[:, :], pj[:, p, :, :].rearrange("p a s -> p (a s)"), start=True, stop=True).then_inc(l_ready, 1)

            pe.wait_ge(const_loaded, N_CONST)
            logits(0, 0)

            def step(i, u, prev, ahead, ahead2):
                if ahead:
                    logits(i, u, 1)
                turn_max(i, u)
                if prev:
                    times_v(i, u, -1, (2, 5))
                turn_back(i, u)
                if prev:
                    times_v(i, u, -1, (0, 1, 3))
                add_max(i, u)
                if prev:
                    times_v(i, u, -1, (4,))
                    sums(i, u, -1)

            pairs(pe, step)
            times_v(PAIRS - 1, 1, 0, (2, 5, 0, 1, 3, 4))
            sums(PAIRS - 1, 1)

        @block.vector
        def _(v):
            def finish(i, u, k):
                n, p, _, b, s0, _ = at(i, u, k)
                window = view(v_t[:, ds(b, 1), ds(s0 + PAD - WIN + 1, 1)], [[1, BLK], [1, WIN]])
                v.wait_ge(u_ready, n + 1)
                v.tensor_tensor(uv[:, :, :], ps_u[:, :, :], window, ALU.mult).then_inc(u_read, 1)
                v.wait_ge(l_ready, n + 1)
                v.tensor_reduce(l_sum[:, :], ps_l.rearrange("p (a s) -> p s a", a=3), AX.X, ALU.add).then_inc(l_read, 1)
                v.wait_ge(u_read, n + 1)
                v.tensor_reduce(z_raw[:, :], uv[:, :, :], AX.X, ALU.add).then_inc(z_step, 1)
                v.wait_ge(l_read, n + 1)
                v.reciprocal(l_inv[:, :], l_sum[:, :]).then_inc(z_step, 1)
                v.wait_ge(z_step, n * 2 + 2)
                v.tensor_tensor(z_t[:, ds(n * BLK, BLK)], z_raw[:, :], l_inv[:, :], ALU.mult).then_inc(z_ready, 1)
                v.wait_ge(z_ready, n + 1)

            def sum_j(i, u, k):
                n, p, _, _, _, _ = at(i, u, k)
                v.wait_ge(p_ready, n + 1)
                if not isinstance(n, int) or n >= 2:
                    v.wait_ge(l_ready, n - 1)
                v.tensor_reduce(pj[:, p, :, :], probs[:, p, :, :, :], AX.X, ALU.add).then_inc(pj_ready, 1)

            def negate(i, u):
                n, _, _, _, _, _ = at(i, u)
                v.wait_ge(max_turned, n + 1)
                v.tensor_reduce(max_h[:, :], ps_max.rearrange("s (k h) -> s h k", h=H), AX.X, ALU.max).then_inc(c_step, 1)
                v.wait_ge(nm_turned, n)
                v.wait_ge(c_step, n * 2 + 1)
                v.tensor_scalar(nm[0:BLK, 0, :], max_h[:, :], -1.0, None, ALU.mult).then_inc(c_step, 1)
                v.wait_ge(c_step, n * 2 + 2)
                v.scalar_tensor_tensor(nm[0:BLK, 1, :], max_h[:, :], -1.0, nm[0:BLK, 0, :], ALU.mult, ALU.subtract).then_inc(nm_ready, 1)
                v.wait_ge(nm_ready, n + 1)

            def maximum(i, u, k=0):
                n, p, _, _, _, later = at(i, u, k)
                v.wait_ge(logits_ready, n + 1)
                v.tensor_reduce(r_raw[:, :, :], ps_a[:, p, :, :, :], AX.X, ALU.max).then_inc(r_step, 1)
                v.wait_ge(r_step, n * 2 + 1)
                mask = r_mask[:, ds(later, 1), :, :].rearrange("p a b s -> p (a b) s")
                v.tensor_tensor(r_masked[:, :, :], r_raw[:, :, :], mask, ALU.add).then_inc(r_step, 1)
                v.wait_ge(r_step, n * 2 + 2)
                if not isinstance(n, int) or n >= 2:
                    v.wait_ge(max_turned, n - 1)
                v.tensor_reduce(r_max[:, p, :], r_masked[:, :, :].rearrange("p a s -> p s a"), AX.X, ALU.max).then_inc(r_ready, 1)
                v.wait_ge(r_ready, n + 1)

            v.wait_ge(zeroed, 16 + 3)
            maximum(0, 0)

            def step(i, u, prev, ahead, ahead2):
                if prev and not (isinstance(i, int) and i == 0):
                    finish(i, u, -2)
                if prev:
                    sum_j(i, u, -1)
                negate(i, u)
                if ahead:
                    maximum(i, u, 1)

            pairs(v, step)
            finish(PAIRS - 1, 0, 0)
            sum_j(PAIRS - 1, 1, 0)
            finish(PAIRS - 1, 1, 0)

        @block.scalar
        def _(act):
            act.wait_ge(const_loaded, N_CONST)

            def step(i, u, prev, ahead, ahead2):
                n, p, _, _, _, later = at(i, u)
                act.wait_ge(nm_turned, n + 1)
                if not isinstance(n, int) or n >= 2:
                    act.wait_ge(m_added, n - 1)
                dst = m_rows[0:BLK, p, ds(later, 1), :, :, :].rearrange("r a b s j -> r (a b) s j")
                src = ps_nm[:, 0:BLK].unsqueeze(1).unsqueeze(3).to_broadcast([BLK, 3, BLK, WIN])
                act.activation(dst, src, ACT.Copy).then_inc(rows_ready, 1)
                act.wait_ge(m_added, n + 1)
                if not isinstance(n, int) or n >= 2:
                    act.wait_ge(u_ready, n - 1)
                    act.wait_ge(pj_ready, n - 1)
                act.activation(probs[:, p, :, :, :], ps_a[:, p, :, :, :], ACT.Exp).then_inc(p_ready, 1)

            pairs(act, step)


def attn1_output_stage(nc, g, io, z_t):
    with ExitStack() as ctx:
        m = Mem(nc, ctx, "a1o")
        s = stats_buffers(m)
        z_c = m.sb("z_c", [P, 2, CH])
        norm = m.sb("norm", [P, 2, CT, P])
        gamma, beta = m.sb("gamma", [P, P]), m.sb("beta", [P, P])
        y_mean, y_rstd = m.sb("y_mean", [P, TILES]), m.sb("y_rstd", [P, TILES])
        ps_y = m.ps("ps_y", [P, 2, CT, P])
        loaded, picked, projected, normed, added, y_normed, scaled, shifted = (
            m.sem(x) for x in ("loaded", "picked", "projected", "normed", "added", "y_normed", "scaled", "shifted"))
        y = g["y_tok"]
        block = ctx.enter_context(nc.Block())

        @block.sync
        def _(sp):
            sp.dma_start(gamma[:, :], io["L1_attn_gamma"].partition_broadcast(P)).then_inc(loaded, 16)
            sp.dma_start(beta[:, :], io["L1_attn_beta"].partition_broadcast(P)).then_inc(loaded, 16)
            sp.wait_ge(loaded, 32)

        @block.scalar
        def _(act):
            with act.Fori(0, NCH // 2) as pair:
                for u in range(2):
                    c = pair * 2 + u
                    act.wait_ge(projected, c)
                    act.activation(z_c[:, u, :], z_t[:, ds(c * CH, CH)], ACT.Copy).then_inc(picked, 1)
            scalar_stats(act, s, 0)

        @block.tensor
        def _(pe):
            with pe.Fori(0, NCH // 2) as pair:
                for u in range(2):
                    c = pair * 2 + u
                    pe.wait_ge(picked, c + 1)
                    pe.wait_ge(added, c)
                    for k in range(CT):
                        mm = pe.matmul(ps_y[:, u, k, :], z_c[:, u, k * P:(k + 1) * P], g["w_t"][:, 8, :], start=True, stop=True)
                    mm.then_inc(projected, 1)

        @block.vector
        def _(v):
            with v.Fori(0, NCH // 2) as pair:
                for u in range(2):
                    c = pair * 2 + u
                    for k in range(CT):
                        t = c * CT + k
                        v.tensor_scalar(norm[:, u, k, :], g["x_tok"][:, ds(t, 1), :], g["mean"][:, ds(t, 1)], g["rstd"][:, ds(t, 1)],
                                        ALU.subtract, ALU.mult).then_inc(normed, 1)
                    v.wait_ge(normed, c * CT + CT)
                    v.wait_ge(projected, c + 1)
                    v.tensor_tensor(y[:, ds(c * CT, CT), :], ps_y[:, u, :, :], norm[:, u, :, :], ALU.add).then_inc(added, 1)
            v.wait_ge(added, NCH)
            vector_stats(v, y, s, y_mean, y_rstd, 0)
            v.wait_ge(loaded, 32)
            with v.Fori(0, NCH) as c:
                for k in range(CT):
                    t = c * CT + k
                    v.tensor_scalar(y[:, ds(t, 1), :], y[:, ds(t, 1), :], y_mean[:, ds(t, 1)], y_rstd[:, ds(t, 1)],
                                    ALU.subtract, ALU.mult).then_inc(y_normed, 1)
                v.wait_ge(y_normed, c * CT + CT)
                yc = y[:, ds(c * CT, CT), :]
                v.tensor_tensor(yc, yc, gamma[:, :].unsqueeze(1).to_broadcast([P, CT, P]), ALU.mult).then_inc(scaled, 1)

        @block.gpsimd
        def _(pool):
            pool.wait_ge(loaded, 32)
            with pool.Fori(0, NCH) as c:
                pool.wait_ge(scaled, c + 1)
                yc = y[:, ds(c * CT, CT), :]
                pool.tensor_tensor(yc, yc, beta[:, :].unsqueeze(1).to_broadcast([P, CT, P]), ALU.add).then_inc(shifted, 1)
            pool.wait_ge(shifted, NCH)


F1 = 512
FB = F1 // P
SHARED = E_
EXPERTS = E_ + 1


def moe1_weights_stage(nc, g, io, w):
    with ExitStack() as ctx:
        m = Mem(nc, ctx, "m1w")
        gate = m.sb("gate", [P, P])
        ps_w = m.ps("ps_w", [P, P])
        loaded, gate_loaded, zeroed, turned, copied = (m.sem(s) for s in ("loaded", "gate_loaded", "zeroed", "turned", "copied"))
        block = ctx.enter_context(nc.Block())

        @block.sync
        def _(sp):
            sp.wait_ge(zeroed, 1)
            sp.dma_start(gate[0:E_, :], io["L1_ffn_gate_W"]).then_inc(gate_loaded, 16)
            for dst, name in ((w["w1"], "w1"), (w["w3"], "w3")):
                sp.dma_start(dst[:, 0:E_, :], io[f"L1_ffn_{name}_e"].rearrange("e d f -> d e f")).then_inc(loaded, 16)
                shared = dst[:, SHARED, :].rearrange("d (n f) -> d n f", n=E_)
                sp.dma_start(shared, io[f"L1_ffn_{name}_s"].rearrange("n d f -> d n f")).then_inc(loaded, 16)
            sp.dma_start(w["w2"][:, 0:E_, :, :].rearrange("p e b d -> p (e b) d"),
                         io["L1_ffn_w2_e"].rearrange("e (b p) d -> p (e b) d", p=P)).then_inc(loaded, 16)
            sp.dma_start(w["w2"][:, SHARED, :, :], io["L1_ffn_w2_s"].rearrange("n f d -> (n f) d").rearrange("(b p) d -> p b d", p=P)).then_inc(loaded, 16)
            sp.wait_ge(loaded, 16 * 6)

        @block.gpsimd
        def _(pool):
            pool.memset(gate[:, :], 0.0).then_inc(zeroed, 1)

        @block.tensor
        def _(pe):
            pe.wait_ge(gate_loaded, 16)
            pe.matmul(ps_w[:, :], gate[:, :], g["ident"][:, :], start=True, stop=True).then_inc(turned, 1)

        @block.vector
        def _(v):
            v.wait_ge(turned, 1)
            v.tensor_copy(w["gate_w"][:, :], ps_w[:, :]).then_inc(copied, 1)
            v.wait_ge(copied, 1)


def moe1_route_stage(nc, g, w, x_t, gate_parts):
    with ExitStack() as ctx:
        m = Mem(nc, ctx, "m1r")
        norm = m.sb("norm", [P, 2, CT, P])
        x_c = m.sb("x_c", [P, 2, CH])
        logits = m.sb("logits", [P, TILES, E_])
        exps = m.sb("exps", [P, TILES, E_])
        r = route_buffers(m)
        ps_t = m.ps("ps_t", [P, 2, CH])
        ps_l = m.ps("ps_l", [P, 2, CT, P])
        normed, turned, t_copied, c_copied, scored, l_copied, exps_ready = (
            m.sem(s) for s in ("normed", "turned", "t_copied", "c_copied", "scored", "l_copied", "exps_ready"))
        block = ctx.enter_context(nc.Block())

        @block.vector
        def _(v):
            with v.Fori(0, NCH // 2) as pair:
                for u in range(2):
                    c = pair * 2 + u
                    v.wait_ge(turned, c)
                    for k in range(CT):
                        t = c * CT + k
                        v.tensor_scalar(norm[:, u, k, :], g["x_tok"][:, ds(t, 1), :], g["mean"][:, ds(t, 1)], g["rstd"][:, ds(t, 1)],
                                        ALU.subtract, ALU.mult).then_inc(normed, 1)
            v.wait_ge(l_copied, NCH)
            step = Chain(v, r["step"])
            step(v.reduce_max(r["v1"][:, :], logits[:, :, :], AX.X))
            step(v.tensor_tensor(logits[:, :, :], logits[:, :, :], per_tile(r["v1"]), ALU.subtract))
            v.wait_ge(exps_ready, 1)
            step(v.tensor_reduce(r["w1"][:, :], exps[:, :, :], AX.X, ALU.add))
            step(v.reciprocal(r["w2"][:, :], r["w1"][:, :]))
            step(v.tensor_tensor(logits[:, :, :], exps[:, :, :], per_tile(r["w2"]), ALU.mult))
            top_two(v, step, r, logits, g)
            step(v.tensor_tensor(r["eq"][:, :, :], r["sel1"][:, :, :], r["sel2"][:, :, :], ALU.add))
            step(v.scalar_tensor_tensor(r["gate"][:, :, :], r["eq"][:, :, :], 0.5, logits[:, :, :], ALU.mult, ALU.mult))
            split_gates(v, step, r, gate_parts)

        @block.tensor
        def _(pe):
            with pe.Fori(0, NCH // 2) as pair:
                for u in range(2):
                    c = pair * 2 + u
                    pe.wait_ge(normed, c * CT + CT)
                    pe.wait_ge(t_copied, c)
                    for k in range(CT):
                        mm = pe.transpose(ps_t[:, u, k * P:(k + 1) * P], norm[:, u, k, :], g["ident"][:, :])
                    mm.then_inc(turned, 1)
                    pe.wait_ge(t_copied, c + 1)
                    pe.wait_ge(l_copied, c)
                    for k in range(CT):
                        mm = pe.matmul(ps_l[:, u, k, :], x_c[:, u, k * P:(k + 1) * P], w["gate_w"][:, :], start=True, stop=True)
                    mm.then_inc(scored, 1)

        @block.scalar
        def _(act):
            with act.Fori(0, NCH // 2) as pair:
                for u in range(2):
                    c = pair * 2 + u
                    act.wait_ge(turned, c + 1)
                    act.wait_ge(scored, c)
                    act.wait_ge(c_copied, c)
                    act.activation(x_c[:, u, :], ps_t[:, u, :], ACT.Copy).then_inc(t_copied, 1)
                    act.wait_ge(scored, c + 1)
                    act.activation(logits[:, ds(c * CT, CT), :], ps_l[:, u, :, 0:E_], ACT.Copy).then_inc(l_copied, 1)
            act.wait_ge(r["step"], 2)
            act.activation(exps[:, :, :], logits[:, :, :], ACT.Exp).then_inc(exps_ready, 1)

        @block.gpsimd
        def _(pool):
            with pool.Fori(0, NCH // 2) as pair:
                for u in range(2):
                    c = pair * 2 + u
                    pool.wait_ge(t_copied, c + 1)
                    pool.tensor_copy(x_t[:, ds(c * CH, CH)], x_c[:, u, :]).then_inc(c_copied, 1)
            pool.wait_ge(c_copied, NCH)


def moe1_experts_stage(nc, g, w, x_t, gate_t):
    with ExitStack() as ctx:
        m = Mem(nc, ctx, "m1e")
        silu, hid = m.sb("silu", [P, 2, CH]), m.sb("hid", [P, 2, CH])
        gates, scaled = m.sb("gates", [P, 2, CH]), m.sb("scaled", [P, 2, CH])
        total, mixed = m.sb("total", [P, 2, CH]), m.sb("mixed", [P, 2, CH])
        ps_h = m.ps("ps_h", [P, 2, 2, CH])
        ps_y = m.ps("ps_y", [P, 2, CH])
        ps_g = m.ps("ps_g", [P, CH])
        ps_t = m.ps("ps_t", [P, CH])
        h_ready, silu_ready, hid_ready, down_done, gates_turned, gates_ready, scaled_ready, added, mixed_ready, turned, y_copied = (
            m.sem(s) for s in ("h_ready", "silu_ready", "hid_ready", "down_done", "gates_turned", "gates_ready", "scaled_ready",
                               "added", "mixed_ready", "turned", "y_copied"))
        STEPS = EXPERTS * FB
        block = ctx.enter_context(nc.Block())

        def chunks(eng, body):
            with eng.Fori(0, NCH // 2) as pair:
                for u in range(2):
                    body(pair * 2 + u, u)

        @block.tensor
        def _(pe):
            def up(c, u, n):
                e, b = n // FB, n % FB
                pe.wait_ge(hid_ready, c * STEPS + n + 1)
                for s, name in ((0, "w1"), (1, "w3")):
                    pe.matmul(ps_h[:, n % 2, s, :], w[name][:, e, b * P:(b + 1) * P], x_t[:, ds(c * CH, CH)],
                              start=True, stop=True).then_inc(h_ready, 1)

            def down(c, u, n):
                e, b = n // FB, n % FB
                pe.wait_ge(hid_ready, c * STEPS + n + 3)
                if b == 0:
                    pe.wait_ge(scaled_ready, c * EXPERTS + e + 1)
                pe.matmul(ps_y[:, (u + e) % 2, :], w["w2"][:, e, b, :], hid[:, n % 2, :], start=b == 0, stop=b == FB - 1).then_inc(down_done, 1)

            def spread(c, e):
                pe.wait_ge(gates_ready, c * E_ + e)
                pe.matmul(ps_g[:, :], g["pick"][:, e, :], gate_t[:, ds(c * CH, CH)], start=True, stop=True).then_inc(gates_turned, 1)

            def chunk(c, u):
                up(c, u, 0)
                for n in range(STEPS):
                    if n + 1 < STEPS:
                        up(c, u, n + 1)
                    if n % FB == 0 and n // FB < E_:
                        spread(c, n // FB)
                    down(c, u, n)
                pe.wait_ge(mixed_ready, c + 1)
                pe.wait_ge(y_copied, c)
                for k in range(CT):
                    mm = pe.transpose(ps_t[:, k * P:(k + 1) * P], mixed[:, u, k * P:(k + 1) * P], g["ident"][:, :])
                mm.then_inc(turned, 1)

            chunks(pe, chunk)

        @block.scalar
        def _(act):
            def chunk(c, u):
                for n in range(STEPS):
                    act.wait_ge(h_ready, (c * STEPS + n) * 2 + 1)
                    act.wait_ge(hid_ready, c * STEPS + n + 1)
                    act.activation(silu[:, n % 2, :], ps_h[:, n % 2, 0, :], ACT.Silu).then_inc(silu_ready, 1)
                    e = n // FB
                    if n % FB == 0 and e < E_:
                        act.wait_ge(gates_turned, c * E_ + e + 1)
                        act.wait_ge(scaled_ready, c * EXPERTS + e + 1)
                        act.activation(gates[:, e % 2, :], ps_g[:, :], ACT.Copy).then_inc(gates_ready, 1)
                act.wait_ge(turned, c + 1)
                act.activation(g["y_tok"][:, ds(c * CT, CT), :], ps_t[:, :].rearrange("p (k e) -> p k e", k=CT), ACT.Copy).then_inc(y_copied, 1)

            chunks(act, chunk)

        @block.vector
        def _(v):
            v.sem_inc(hid_ready, 2)
            v.sem_inc(scaled_ready, 2)

            def hidden(c, n):
                v.wait_ge(silu_ready, c * STEPS + n + 1)
                v.wait_ge(h_ready, (c * STEPS + n) * 2 + 2)
                if n >= 2:
                    v.wait_ge(down_done, c * STEPS + n - 1)
                v.tensor_tensor(hid[:, n % 2, :], silu[:, n % 2, :], ps_h[:, n % 2, 1, :], ALU.mult).then_inc(hid_ready, 1)

            def scale(c, u, e):
                v.wait_ge(down_done, c * STEPS + (e + 1) * FB)
                v.wait_ge(gates_ready, c * E_ + e + 1)
                v.wait_ge(added, c * (E_ - 1) + (max(e - 2, 1) if e >= 2 else 0))
                v.tensor_tensor(scaled[:, e % 2, :], ps_y[:, (u + e) % 2, :], gates[:, e % 2, :], ALU.mult).then_inc(scaled_ready, 1)

            def chunk(c, u):
                for n in range(STEPS):
                    if n < 2:
                        v.wait_ge(down_done, c * STEPS)
                    hidden(c, n)
                    if n % FB == 0 and n > 0:
                        scale(c, u, n // FB - 1)
                v.wait_ge(down_done, (c + 1) * STEPS)
                v.wait_ge(added, (c + 1) * (E_ - 1))
                v.wait_ge(turned, c)
                v.scalar_tensor_tensor(mixed[:, u, :], ps_y[:, (u + SHARED) % 2, :], 0.5 / E_, total[:, (E_ - 1) % 2, :],
                                       ALU.mult, ALU.add).then_inc(mixed_ready, 1)
                v.wait_ge(mixed_ready, c + 1)
                v.sem_inc(scaled_ready, 1)

            chunks(v, chunk)

        @block.gpsimd
        def _(pool):
            def chunk(c, u):
                for e in range(1, E_):
                    pool.wait_ge(scaled_ready, c * EXPERTS + 2 + e + 1)
                    if e == 1:
                        pool.wait_ge(mixed_ready, c)
                    else:
                        pool.wait_ge(added, c * (E_ - 1) + e - 1)
                    before = scaled[:, 0, :] if e == 1 else total[:, (e - 1) % 2, :]
                    pool.tensor_tensor(total[:, e % 2, :], before, scaled[:, e % 2, :], ALU.add).then_inc(added, 1)

            chunks(pool, chunk)


def moe0(nc, g, io):
    with ExitStack() as ctx:
        m = Mem(nc, ctx, "m0")
        w = {"up_t": m.sb("up_t", [P, 2, E_, P], bf16), "down_t": m.sb("down_t", [P, E_, P]), "gate_w": m.sb("gate_w", [P, E_], bf16),
             "b1_t": m.sb("b1_t", [P, 2, E_]), "b2_rows": m.sb("b2_rows", [P, P], bf16), "norm_w": m.sb("norm_w", [P, P]),
             "gate_b": m.sb("gate_b", [P, E_], bf16), "pick": g["pick"]}
        xc = m.sb("xc", [P, TILES, P], bf16)
        rms_inv = m.sb("rms_inv", [P, TILES])
        nf_t, gate_t = m.sb("nf_t", [P, NTOK], bf16), m.sb("gate_t", [P, NTOK], bf16)
        gate_parts = m.sb("gate_parts", [P, TILES, PARTS, E_], bf16)
        moe0_weights_stage(nc, g, io, w)
        moe0_norm_stage(nc, g, w, xc, rms_inv)
        moe0_route_stage(nc, g, w, xc, rms_inv, nf_t, gate_parts)
        gate_rows_stage(nc, g, gate_parts, gate_t, "m0g")
        moe0_experts_stage(nc, g, w, xc, nf_t, gate_t)


def attn1(nc, g, io, scratch):
    with ExitStack() as ctx:
        m = Mem(nc, ctx, "a1")
        q_t, kp_t = m.sb("q_t", [P, B, T]), m.sb("kp_t", [P, B, T])
        k_t, v_t = m.sb("k_t", [P, B, PAD + T]), m.sb("v_t", [P, B, PAD + T])
        z_t = m.sb("z_t", [P, NTOK])
        attn1_project_stage(nc, g, q_t, k_t, kp_t, v_t, scratch["v_rows"])
        attn1_windows_stage(nc, g, io, q_t, k_t, kp_t, v_t, scratch["v_rows"], z_t)
        attn1_output_stage(nc, g, io, z_t)


def moe1(nc, g, io):
    with ExitStack() as ctx:
        m = Mem(nc, ctx, "m1")
        w = {"w1": m.sb("w1", [P, EXPERTS, F1]), "w3": m.sb("w3", [P, EXPERTS, F1]), "w2": m.sb("w2", [P, EXPERTS, FB, P]),
             "gate_w": m.sb("gate_w", [P, P])}
        x_t, gate_t = m.sb("x_t", [P, NTOK]), m.sb("gate_t", [P, NTOK], bf16)
        gate_parts = m.sb("gate_parts", [P, TILES, PARTS, E_], bf16)
        moe1_weights_stage(nc, g, io, w)
        moe1_route_stage(nc, g, w, x_t, gate_parts)
        gate_rows_stage(nc, g, gate_parts, gate_t, "m1g")
        moe1_experts_stage(nc, g, w, x_t, gate_t)


def build_program(nc, io, out):
    scratch = {
        "qk_parts": nc.dram_tensor("qk_parts", [2, 3, P, NTOK], bf16, kind="Internal").ap(),
        "o_raw": nc.dram_tensor("o_raw", [H, DH + 1, NTOK], fp32, kind="Internal").ap(),
        "l_inv": nc.dram_tensor("l_inv", [H, NTOK], fp32, kind="Internal").ap(),
    }
    scratch["v_rows"] = nc.dram_tensor("v_rows", [NTOK, P], fp32, kind="Internal").ap()
    with ExitStack() as ctx:
        m = Mem(nc, ctx, "g")
        g = {
            "x_tok": m.sb("x_tok", [P, TILES, P]), "y_tok": m.sb("y_tok", [P, TILES, P]), 
            "mean": m.sb("mean", [P, TILES]), "rstd": m.sb("rstd", [P, TILES]),
            "ident": m.sb("ident", [P, P]), "ident_h": m.sb("ident_h", [P, P], bf16),
            "mask_qk": m.sb("mask_qk", [P, P], bf16), "mask_kq": m.sb("mask_kq", [P, P], bf16),
            "w_t": m.sb("w_t", [P, 9, P]), "place": m.sb("place", [P, E_]), "pick": m.sb("pick", [P, E_, P], bf16),
        }
        with semaphores_of(nc):
            load_stage(nc, io, g)
            first_norm_stage(nc, g)
            with ExitStack() as inner:
                g["v_tok"] = Mem(nc, inner, "attn0").sb("v_tok", [P, TILES, P])
                attn0_project_stage(nc, g, scratch)
                attn0_heads_stage(nc, g, scratch, io)
            attn0_output_stage(nc, g, scratch)
            residual_stage(nc, g, "res0")
        with semaphores_of(nc):
            moe0(nc, g, io)
            residual_stage(nc, g, "res1")
        with semaphores_of(nc):
            attn1(nc, g, io, scratch)
            residual_stage(nc, g, "res2")
        with semaphores_of(nc):
            moe1(nc, g, io)
            residual_stage(nc, g, "res3", out=out)


def kernel(**inputs):
    import numpy as np
    from concourse import bacc
    from concourse.bass_utils import run_bass_kernel_spmd

    half = inputs["L0_ffn_gate_weight"].dtype
    start = 2.0 ** -0.5
    slopes = np.array([start * start ** i for i in range(H)], np.float32)
    high = slopes.astype(half).astype(np.float32)
    middle = (slopes - high).astype(half).astype(np.float32)
    low = slopes - high - middle
    pos = np.arange(T)
    key_rows = np.zeros((P - 48, T), np.float32)
    key_rows[0:6:2], key_rows[1:6:2], key_rows[6:8] = pos // P * P, pos % P, 1.0
    slope_rows = np.zeros((H, 8, T), np.float32)
    for i, part in enumerate((high, middle, low)):
        slope_rows[:, 2 * i:2 * i + 2] = -part[:, None, None]
    arrays = {"key_rows": key_rows.astype(half), "slope_rows": slope_rows.astype(half),
              "query_rows": np.zeros((P - 48, T), half)}
    p = np.arange(P)
    head_mask = (p[:, None] // DH == np.arange(H)).astype(np.float32)
    key_mask = (p[:, None] % H == p[None, :] // DH).astype(np.float32)
    outside = np.ones((GK, 2, 3, BLK), bool)
    for q, (slot, lo, hi) in enumerate(GROUPS):
        for s in range(lo, hi):
            key = GK * q + np.arange(GK) - 2 * GK
            off = (key > s) | (key < s - WIN + 1)
            outside[:, 1, slot, s] = off
            outside[:, 0, slot, s] = off | (key < 0)
    window_mask = np.repeat(np.where(outside, NEG, 0.0), H, axis=0)
    m_pick = np.zeros((P, P), np.float32)
    m_pick[0:H] = m_pick[H:2 * H] = p[None, :] % H == np.arange(H)[:, None]
    m_pick[2 * H:2 * H + GK] = p[None, :] // H == np.arange(GK)[:, None]
    m_pick[2 * H + GK] = 1.0
    window_rows = np.zeros((P, 2, 3, BLK, WIN), np.float32)
    window_rows[2 * H:2 * H + GK] = np.where(outside, NEG, 0.0)[..., None]
    before = np.arange(BLK)[:, None] - (WIN - 1) + np.arange(WIN) < 0
    window_rows[2 * H + GK, 0] = np.where(before, NEG, 0.0)
    arrays.update(head_mask=head_mask, key_mask=key_mask, m_pick=m_pick.astype(half),
                  window_mask=window_mask.reshape(P, 2, 3 * BLK).astype(np.float32),
                  window_rows=window_rows.reshape(P, 2, 3 * BLK * WIN).astype(half))
    arrays.update({k: np.ascontiguousarray(v) for k, v in inputs.items()})

    nc = bacc.Bacc("TRN2", target_bir_lowering=False, num_devices=1)
    io = {k: nc.dram_tensor("in_" + k, a.shape, mybir.dt.from_np(a.dtype), kind="ExternalInput").ap() for k, a in arrays.items()}
    out = nc.dram_tensor("out", (B, T, P), fp32, kind="ExternalOutput").ap()
    build_program(nc, io, out)
    done = run_bass_kernel_spmd(nc, [{"in_" + k: a for k, a in arrays.items()}], core_ids=[0])
    return done.results[0]["out"]
```

```python
from contextlib import ExitStack, contextmanager

import concourse.bass as bass
from concourse import mybir

fp32 = mybir.dt.float32
bf16 = mybir.dt.bfloat16
ALU = mybir.AluOpType
ACT = mybir.ActivationFunctionType
AX = mybir.AxisListType

P = 128
B, T = 4, 1024
NTOK = B * T
TILES = NTOK // P
CH = 512
NCH = NTOK // CH
CT = CH // P
H, DH = 16, 8
EPS = 1e-5
NEG = -1e30


class Mem:

    def __init__(self, nc, ctx, stage):
        self.nc, self.ctx, self.stage = nc, ctx, stage + "_"

    def sb(self, name, shape, dt=fp32):
        return self.ctx.enter_context(self.nc.sbuf_tensor(self.stage + name, shape, dt))

    def ps(self, name, shape, dt=fp32):
        return self.ctx.enter_context(self.nc.psum_tensor(self.stage + name, shape, dt))

    def sem(self, name, free=0):
        handle = self.nc.alloc_semaphore(self.stage + name)
        self.nc.sync.sem_inc(handle, 1 + free)
        return handle


@contextmanager
def semaphores_of(nc):
    before = nc.snapshot_sems()
    yield
    nc.clear_and_free_semaphores(nc.allocated_since(before))
    nc.all_engine_barrier()


def ds(at, n):
    return bass.ds(at, n)


def view(ap, dims, offset=0):
    return bass.AP(ap.tensor, ap.offset + offset, [list(ap.ap[0]), *dims])


def load_stage(nc, io, g):
    with ExitStack() as ctx:
        m = Mem(nc, ctx, "load")
        names = ["L0_attn_Wq", "L0_attn_Wk", "L0_attn_Wv", "L0_attn_Wp",
                 "L1_attn_Wq", "L1_attn_Wk", "L1_attn_Wv", "L1_attn_Wkp", "L1_attn_Wo"]
        w_nat = m.sb("w_nat", [P, len(names), P])
        lora_a = m.sb("lora_a", [P, 3, DH])
        lora_b = m.sb("lora_b", [DH, 3, P])
        lora_at = m.sb("lora_at", [DH, 3, P])
        place_i = m.sb("place_i", [P, E_], mybir.dt.int32)
        ps_a = m.ps("ps_a", [P, 3, 512])
        ps_w = m.ps("ps_w", [P, 3, 512])
        loaded, x_loaded, consts, at_ready, at_copied, w_ready, w_copied = (
            m.sem(s) for s in ("loaded", "x_loaded", "consts", "at_ready", "at_copied", "w_ready", "w_copied"))
        N_LOADS = len(names) + 6
        nc.all_engine_barrier()
        block = ctx.enter_context(nc.Block())

        @block.sync
        def _(sp):
            for i, n in enumerate(names):
                sp.dma_start(w_nat[:, i, :], io[n]).then_inc(loaded, 16)
            for i, n in enumerate("qkv"):
                sp.dma_start(lora_a[:, i, :], io["L0_attn_A" + n]).then_inc(loaded, 16)
                sp.dma_start(lora_b[:, i, :], io["L0_attn_B" + n]).then_inc(loaded, 16)
            sp.dma_start(g["x_tok"][:, :, :], io["L0_attn_x"].rearrange("b (k p) e -> p (b k) e", p=P)).then_inc(x_loaded, 16)
            sp.wait_ge(x_loaded, 17)

        @block.gpsimd
        def _(pool):
            pool.memset(g["ident"][:, :], 0.0).then_inc(consts, 1)
            pool.memset(g["ident_h"][:, :], 0.0).then_inc(consts, 1)
            pool.memset(g["mask_qk"][:, :], 0.0).then_inc(consts, 1)
            pool.memset(g["mask_kq"][:, :], 0.0).then_inc(consts, 1)
            pool.wait_ge(consts, 5)
            for t in ("ident", "ident_h"):
                pool.affine_select(out=g[t][:, :], in_=g[t][:, :], compare_op=ALU.not_equal, fill=1.0,
                                   base=0, pattern=[[-1, P]], channel_multiplier=1).then_inc(consts, 1)
            pool.iota(place_i[:, :], pattern=[[1, E_]], base=-E_, channel_multiplier=0).then_inc(consts, 1)
            pool.wait_ge(consts, 8)
            pool.tensor_copy(g["place"][:, :], place_i[:, :]).then_inc(consts, 1)
            pool.memset(g["pick"][:, :, :], 0.0).then_inc(consts, 1)
            for s in range(PARTS):
                pool.wait_ge(consts, 1 + 9 + s)
                pool.affine_select(out=g["pick"][:, :, :], in_=g["pick"][:, :, :], compare_op=ALU.not_equal, fill=1.0,
                                   base=-s * E_, pattern=[[-1, E_], [0, P]], channel_multiplier=1).then_inc(consts, 1)
            pool.affine_select(out=g["mask_qk"][:, :], in_=g["mask_qk"][:, :], compare_op=ALU.is_ge, fill=NEG,
                               base=0, pattern=[[-1, P]], channel_multiplier=1).then_inc(consts, 1)
            pool.affine_select(out=g["mask_kq"][:, :], in_=g["mask_kq"][:, :], compare_op=ALU.is_ge, fill=NEG,
                               base=0, pattern=[[1, P]], channel_multiplier=-1).then_inc(consts, 1)

        @block.tensor
        def _(pe):
            pe.wait_ge(consts, 1 + 9 + PARTS + 2)
            pe.wait_ge(loaded, 1 + 16 * N_LOADS)
            for i in range(3):
                pe.matmul(ps_a[0:DH, i, 0:P], lora_a[:, i, :], g["ident"][:, :], start=True, stop=True).then_inc(at_ready, 1)
            pe.wait_ge(at_copied, 4)
            for i in range(len(names)):
                if i >= 3:
                    pe.wait_ge(w_copied, 1 + i - 2)
                mm = pe.matmul(ps_w[:, i % 3, 0:P], w_nat[:, i, :], g["ident"][:, :], start=True, stop=i >= 3)
                if i < 3:
                    mm = pe.matmul(ps_w[:, i % 3, 0:P], lora_b[:, i, :], lora_at[:, i, :], start=False, stop=True)
                mm.then_inc(w_ready, 1)

        @block.vector
        def _(v):
            v.wait_ge(at_ready, 4)
            for i in range(3):
                v.tensor_scalar(lora_at[:, i, :], ps_a[0:DH, i, 0:P], 2.0, None, ALU.mult).then_inc(at_copied, 1)
            for i, n in enumerate(names):
                v.wait_ge(w_ready, 1 + i + 1)
                scale = DH ** -0.5 if n.endswith("Wq") else 1.0
                v.tensor_scalar(g["w_t"][:, i, :], ps_w[:, i % 3, 0:P], scale, None, ALU.mult).then_inc(w_copied, 1)
            v.wait_ge(w_copied, 1 + len(names))


def stats_buffers(m):
    d = {n: m.sb("ln_" + n, [P, TILES]) for n in ("sum", "dif", "m2", "sq", "var", "std")}
    d["raw"] = m.sb("ln_raw", [P, TILES, 6])
    d["step"] = m.sem("ln_step")
    d["raw_done"] = m.sem("ln_raw_done")
    d["var_ready"] = m.sem("ln_var_ready")
    d["std_ready"] = m.sem("ln_std_ready")
    d["uses"] = 0
    return d


def raw_stats(v, src, s, tiles):
    for t in tiles:
        v.bn_stats(s["raw"][:, t:t + 1, :], src[:, t:t + 1, :]).then_inc(s["raw_done"], 1)


def vector_stats(v, s, mean, rstd, use):
    v.wait_ge(s["raw_done"], 1 + TILES * (use + 1))
    raw, n = s["raw"], 4 * use
    v.tensor_tensor(s["sum"][:, :], raw[:, :, 1], raw[:, :, 4], ALU.add).then_inc(s["step"], 1)
    v.tensor_tensor(s["dif"][:, :], raw[:, :, 1], raw[:, :, 4], ALU.subtract).then_inc(s["step"], 1)
    v.tensor_tensor(s["m2"][:, :], raw[:, :, 2], raw[:, :, 5], ALU.add).then_inc(s["step"], 1)
    v.wait_ge(s["step"], 1 + 8 * use + 3)
    v.tensor_scalar(mean[:, :], s["sum"][:, :], 0.5, None, ALU.mult).then_inc(s["step"], 1)
    v.tensor_tensor(s["sq"][:, :], s["dif"][:, :], s["dif"][:, :], ALU.mult).then_inc(s["step"], 1)
    v.tensor_scalar(s["var"][:, :], s["m2"][:, :], 1.0 / P, EPS, ALU.mult, ALU.add).then_inc(s["step"], 1)
    v.wait_ge(s["step"], 1 + 8 * use + 6)
    v.scalar_tensor_tensor(s["m2"][:, :], s["sq"][:, :], 0.25, s["var"][:, :], ALU.mult, ALU.add).then_inc(s["var_ready"], 1)
    v.wait_ge(s["std_ready"], 1 + use + 1)
    v.reciprocal(rstd[:, :], s["std"][:, :]).then_inc(s["step"], 2)
    v.wait_ge(s["step"], 1 + 8 * use + 8)


def scalar_stats(act, s, use):
    act.wait_ge(s["var_ready"], 1 + use + 1)
    act.activation(s["std"][:, :], s["m2"][:, :], ACT.Sqrt).then_inc(s["std_ready"], 1)


def first_norm_stage(nc, g):
    with ExitStack() as ctx:
        m = Mem(nc, ctx, "first")
        s = stats_buffers(m)
        nc.all_engine_barrier()
        block = ctx.enter_context(nc.Block())

        @block.vector
        def _(v):
            raw_stats(v, g["x_tok"], s, range(TILES))
            vector_stats(v, s, g["mean"], g["rstd"], 0)

        @block.scalar
        def _(act):
            scalar_stats(act, s, 0)


def residual_stage(nc, g, tag, out=None):
    with ExitStack() as ctx:
        m = Mem(nc, ctx, tag)
        s = stats_buffers(m)
        y_mean, y_rstd, y_shift = m.sb("y_mean", [P, TILES]), m.sb("y_rstd", [P, TILES]), m.sb("y_shift", [P, TILES])
        shift_ready, normed, stored = m.sem("shift_ready"), m.sem("normed"), m.sem("stored")
        added = [m.sem("added_by_vector"), m.sem("added_by_pool")]
        x, y = g["x_tok"], g["y_tok"]
        nc.all_engine_barrier()
        block = ctx.enter_context(nc.Block())

        def add(eng, c):
            eng.wait_ge(normed, 1 + (c + 1) * CT)
            at = slice(c * CT, (c + 1) * CT)
            eng.tensor_tensor(x[:, at, :], x[:, at, :], y[:, at, :], ALU.add).then_inc(added[c % 2], 1)

        @block.vector
        def _(v):
            raw_stats(v, y, s, range(TILES))
            vector_stats(v, s, y_mean, y_rstd, 0)
            v.scalar_tensor_tensor(y_shift[:, :], y_mean[:, :], -1.0, y_rstd[:, :], ALU.mult, ALU.mult).then_inc(shift_ready, 1)
            for c in range(NCH):
                if c % 2 == 0:
                    add(v, c)
                if out is None and c:
                    v.wait_ge(added[(c - 1) % 2], 1 + (c + 1) // 2)
                    raw_stats(v, x, s, range((c - 1) * CT, c * CT))
            if out is None:
                v.wait_ge(added[1], 1 + NCH // 2)
                raw_stats(v, x, s, range((NCH - 1) * CT, TILES))
                vector_stats(v, s, g["mean"], g["rstd"], 1)

        @block.gpsimd
        def _(pool):
            for c in range(1, NCH, 2):
                add(pool, c)
            pool.wait_ge(added[1], 1 + NCH // 2)

        @block.scalar
        def _(act):
            scalar_stats(act, s, 0)
            act.wait_ge(shift_ready, 2)
            for t in range(TILES):
                act.activation(y[:, t, :], y[:, t, :], ACT.Identity, bias=y_shift[:, t:t + 1], scale=y_rstd[:, t:t + 1]).then_inc(normed, 1)
            if out is None:
                scalar_stats(act, s, 1)

        @block.sync
        def _(sp):
            if out is not None:
                o = out.rearrange("b (k p) e -> p (b k) e", p=P)
                for c in range(NCH):
                    sp.wait_ge(added[c % 2], 1 + c // 2 + 1)
                    sp.dma_start(o[:, c * CT:(c + 1) * CT, :], x[:, c * CT:(c + 1) * CT, :]).then_inc(stored, 16)
                sp.wait_ge(stored, 1 + 16 * NCH)


def attn0_project_stage(nc, g, scratch):
    with ExitStack() as ctx:
        m = Mem(nc, ctx, "a0p")
        norm = m.sb("norm", [P, 2, CT, P])
        norm_t = m.sb("norm_t", [P, 2, CH])
        full = m.sb("full", [P, 2, 2, CH])
        rest = m.sb("rest", [P, 2, 2, 2, CH])
        parts = m.sb("parts", [P, 2, 2, 3, CH], bf16)
        ps_t = m.ps("ps_t", [P, 2, CH])
        ps_qk = m.ps("ps_qk", [P, 2, CH])
        ps_v = m.ps("ps_v", [P, CT, P])
        normed, turned, t_copied, qk_ready, full_ready, v_ready, v_copied, split = (
            m.sem(s) for s in ("normed", "turned", "t_copied", "qk_ready", "full_ready", "v_ready", "v_copied", "split"))
        stored = [m.sem("stored0"), m.sem("stored1")]
        SPLIT = 5 * 2
        nc.all_engine_barrier()
        block = ctx.enter_context(nc.Block())

        @block.vector
        def _(v):
            with v.Fori(0, NCH // 2) as pair:
                for u in range(2):
                    c = pair * 2 + u
                    v.wait_ge(turned, 1 + c * 1)
                    for k in range(CT):
                        t = c * CT + k
                        v.tensor_scalar(norm[:, u, k, :], g["x_tok"][:, ds(t, 1), :], g["mean"][:, ds(t, 1)], g["rstd"][:, ds(t, 1)],
                                        ALU.subtract, ALU.mult).then_inc(normed, 1)
                    v.wait_ge(stored[u], 1 + pair * 32)
                    v.wait_ge(full_ready, 1 + c * 2 + 2)
                    for i in range(2):
                        v.tensor_copy(parts[:, u, i, 0, :], full[:, u, i, :]).then_inc(split, 1)
                    v.wait_ge(split, 1 + c * SPLIT + 2)
                    for i in range(2):
                        v.tensor_tensor(rest[:, u, i, 0, :], full[:, u, i, :], parts[:, u, i, 0, :], ALU.subtract).then_inc(split, 1)
                    v.wait_ge(split, 1 + c * SPLIT + 4)
                    for i in range(2):
                        v.tensor_copy(parts[:, u, i, 1, :], rest[:, u, i, 0, :]).then_inc(split, 1)
                    v.wait_ge(split, 1 + c * SPLIT + 6)
                    for i in range(2):
                        v.tensor_tensor(parts[:, u, i, 2, :], rest[:, u, i, 0, :], parts[:, u, i, 1, :], ALU.subtract).then_inc(split, 2)

        @block.tensor
        def _(pe):
            with pe.Fori(0, NCH // 2) as pair:
                for u in range(2):
                    c = pair * 2 + u
                    pe.wait_ge(normed, 1 + c * CT + CT)
                    for k in range(CT):
                        mm = pe.transpose(ps_t[:, u, k * P:(k + 1) * P], norm[:, u, k, :], g["ident"][:, :])
                    mm.then_inc(turned, 1)
                    pe.wait_ge(t_copied, 1 + c + 1)
                    pe.wait_ge(full_ready, 1 + c * 2)
                    for i in range(2):
                        pe.matmul(ps_qk[:, i, :], g["w_t"][:, i, :], norm_t[:, u, :], start=True, stop=True).then_inc(qk_ready, 1)
                    pe.wait_ge(v_copied, 1 + c)
                    for k in range(CT):
                        mm = pe.matmul(ps_v[:, k, :], norm_t[:, u, k * P:(k + 1) * P], g["w_t"][:, 2, :], start=True, stop=True)
                    mm.then_inc(v_ready, 1)

        @block.scalar
        def _(act):
            with act.Fori(0, NCH // 2) as pair:
                for u in range(2):
                    c = pair * 2 + u
                    act.wait_ge(turned, 1 + c + 1)
                    act.wait_ge(v_ready, 1 + c)
                    act.activation(norm_t[:, u, :], ps_t[:, u, :], ACT.Copy).then_inc(t_copied, 1)
                    for i in range(2):
                        act.wait_ge(qk_ready, 1 + c * 2 + i + 1)
                        act.wait_ge(split, 1 + c * SPLIT)
                        act.activation(full[:, u, i, :], ps_qk[:, i, :], ACT.Copy).then_inc(full_ready, 1)
                    act.wait_ge(v_ready, 1 + c + 1)
                    act.activation(g["v_tok"][:, ds(c * CT, CT), :], ps_v[:, :, :], ACT.Copy).then_inc(v_copied, 1)

        @block.sync
        def _(sp):
            dst = scratch["qk_parts"].rearrange("i s f t -> f i s t")
            with sp.Fori(0, NCH // 2) as pair:
                for u in range(2):
                    c = pair * 2 + u
                    sp.wait_ge(split, 1 + c * SPLIT + SPLIT)
                    for i in range(2):
                        sp.dma_start(dst[:, i, :, ds(c * CH, CH)], parts[:, u, i, :, :]).then_inc(stored[u], 16)
            for u in range(2):
                sp.wait_ge(stored[u], 1 + 16 * NCH)


def attn0_heads_stage(nc, g, scratch, io):
    HEADS = B * H
    RING = 4
    STEPS = HEADS // RING
    KB = T // P
    HALF = T // 2
    ST = [(kb, 1, min(HALF, T - kb * P)) for kb in range(KB)] + [(kb, 0, HALF - kb * P) for kb in range(KB // 2)]
    S = []
    for qb in range(KB):
        w = (qb + 1) * P
        S.append((qb, 0, min(w, HALF)))
        if w > HALF:
            S.append((qb, 1, w - HALF))
    N = len(ST)
    assert len(S) == N
    LOADED = (3 + 3 + 1) * 16
    with ExitStack() as ctx:
        m = Mem(nc, ctx, "a0h")
        q_st = m.sb("q_st", [P, RING, T], bf16)
        k_st = m.sb("k_st", [P, RING, T], bf16)
        v_st = m.sb("v_st", [P, 2, KB, 32])
        probs = m.sb("probs", [P, N, HALF])
        group_sum = m.sb("group_sum", [P, 32])
        o_sb = m.sb("o_sb", [P, 2, HALF])
        o_sum = m.sb("o_sum", [64, HALF])
        mx = m.sb("mx", [P, 2, 2, KB])
        nm = m.sb("nm", [P, 2, 2 * KB], bf16)
        nm_t = m.sb("nm_t", [P, 2, P], bf16)
        ps_s = m.ps("ps_s", [P, 2, HALF])
        ps_st = m.ps("ps_st", [P, 3, HALF])
        ps_o = m.ps("ps_o", [P, 2, HALF])
        ps_misc = m.ps("ps_misc", [P, HALF])
        ps_nm = ps_misc[96:96 + 2 * KB, 0:P // 2].bitcast(bf16)
        init = m.sem("init")
        gs_init = m.sem("gs_init")
        consts = m.sem("consts")
        qk_loaded = [m.sem(f"qk_loaded{i}") for i in range(RING)]
        s_ready, s_used = m.sem("s_ready"), m.sem("s_used", free=2)
        st_ready, p_ready = m.sem("st_ready"), m.sem("p_ready", free=3)
        pv_done = m.sem("pv_done", free=3)
        max_done, nm_ready, nm_turned, nm_copied = m.sem("max_done"), m.sem("nm_ready"), m.sem("nm_turned"), m.sem("nm_copied")
        m_step = m.sem("m_step")
        m_loaded = [m.sem(f"m_loaded{i}") for i in range(RING)]
        v_ready = m.sem("v_ready")
        o_copied, summed, sum_copied, o_stored = m.sem("o_copied", free=2), m.sem("summed"), m.sem("sum_copied", free=1), m.sem("o_stored")
        nc.all_engine_barrier()
        block = ctx.enter_context(nc.Block())

        def at(i, u, k=0):
            r, slot = i + (u + k) // RING, (u + k) % RING
            return r * RING + slot, slot, r, r // (H // RING), (r % (H // RING)) * RING + slot

        parts = scratch["qk_parts"]

        @block.sync
        def _(sp):
            for u in range(RING):
                sp.dma_start(k_st[48:P, u, :], io["key_rows"]).then_inc(consts, 16)
                sp.dma_start(q_st[48:P, u, :], io["query_rows"]).then_inc(consts, 16)
            sp.wait_ge(consts, 1 + 2 * 16 * RING)

            def load_head(i, u, k=0):
                _, slot, _, b, h = at(i, u, k)
                tok = ds(b * T, T)
                for part, n, row in ((0, 3, 0), (1, 2, 24), (2, 1, 40)):
                    src = parts[0, part, ds(h * DH, DH), tok]
                    sp.dma_start(q_st[row:row + n * DH, slot, :],
                                 bass.AP(src.tensor, src.offset, [[0, n], [NTOK, DH], [1, T]])).then_inc(qk_loaded[slot], 16)
                for n, row in ((3, 0), (2, 24), (1, 40)):
                    sp.dma_start(k_st[row:row + n * DH, slot, :], parts[1, 0:n, ds(h * DH, DH), tok]).then_inc(qk_loaded[slot], 16)
                sp.dma_start(q_st[48:56, slot, :], io["slope_rows"][ds(h, 1), :, :].rearrange("a r t -> (a r) t")).then_inc(qk_loaded[slot], 16)

            def load_max(i, u, k=0):
                t, slot, _, _, _ = at(i, u, k)
                sp.wait_ge(nm_copied, 1 + t + 1)
                sp.dma_start(q_st[54:56, slot, :].rearrange("r (q c) -> r q c", c=P), nm_t[96:96 + 2 * KB, slot % 2, :]).then_inc(m_loaded[slot], 16)

            def store(i, u, k=0):
                t, _, _, b, h = at(i, u, k)
                sp.wait_ge(sum_copied, 1 + t + 2)
                for half in range(2):
                    sp.dma_start(scratch["o_raw"][ds(h, 1), :, ds(b * T + half * HALF, HALF)].rearrange("a r t -> (a r) t"),
                                 o_sum[32 * half:32 * half + DH + 1, :]).then_inc(o_stored, 16)

            def step(i, u, loads, maxes, prev):
                if loads:
                    sp.wait_ge(st_ready, 1 + (i * RING + u) * N)
                    load_head(i, u, 3)
                if maxes:
                    load_max(i, u, 1)
                if prev:
                    store(i, u, -1)

            for u in range(3):
                load_head(0, u)
            load_max(0, 0)
            for u in range(RING):
                step(0, u, True, True, u > 0)
            with sp.Fori(1, STEPS - 1) as i:
                for u in range(RING):
                    step(i, u, True, True, True)
            for u in range(RING):
                step(STEPS - 1, u, u + 3 < RING, u + 1 < RING, True)
            store(STEPS - 1, RING - 1)
            sp.wait_ge(o_stored, 1 + 2 * 16 * HEADS)

        @block.gpsimd
        def _(pool):
            pool.memset(group_sum[:, :], 0.0).then_inc(gs_init, 1)
            for gq in range(4):
                pool.wait_ge(gs_init, 1 + gq + 1)
                pool.affine_select(out=group_sum[:, 0:DH + 1], in_=group_sum[:, 0:DH + 1], compare_op=ALU.not_equal, fill=1.0,
                                   base=-32 * gq, pattern=[[-1, DH + 1]], channel_multiplier=1).then_inc(gs_init, 1)
            pool.memset(v_st[:, :, :, :], 0.0).then_inc(init, 1)
            pool.memset(mx[:, :, :, :], NEG).then_inc(init, 1)
            pool.wait_ge(init, 3)
            pool.memset(v_st[:, :, :, DH:DH + 1], 1.0).then_inc(init, 1)
            pool.memset(probs[:, KB:N, :], 0.0).then_inc(init, 1)
            pool.wait_ge(init, 4)
            with pool.Fori(0, STEPS) as i:
                for u in range(RING):
                    t, _, _, b, h = at(i, u)
                    pool.wait_ge(pv_done, 1 + t * 3)
                    pool.tensor_copy(v_st[:, u % 2, :, 0:DH], g["v_tok"][:, ds(b * KB, KB), ds(h * DH, DH)]).then_inc(v_ready, 1)

        @block.tensor
        def _(pe):
            def s_unit(i, u, k, n):
                t, slot, r, _, _ = at(i, u, k)
                qb, half, w = S[n]
                bank, k0 = n % 2, half * HALF
                if n == 0:
                    pe.wait_ge(qk_loaded[slot], 1 + (r + 1) * LOADED)
                pe.wait_ge(s_used, 1 + t * N + n + 1)
                diag = qb * P - k0
                masked = 0 <= diag < w
                mm = pe.matmul(ps_s[:, bank, 0:w], q_st[:, slot, qb * P:(qb + 1) * P], k_st[:, slot, k0:k0 + w],
                               start=True, stop=not masked)
                if masked:
                    mm = pe.matmul(ps_s[:, bank, diag:diag + P], g["ident_h"][:, :], g["mask_qk"][:, :], start=False, stop=True)
                mm.then_inc(s_ready, 1)

            def st_unit(i, u, n):
                t, slot, r, _, _ = at(i, u)
                kb, half, w = ST[n]
                bank, q0 = n % 3, (half + 1) * HALF - w
                if n == 0:
                    pe.wait_ge(m_loaded[slot], 1 + (r + 1) * 16)
                pe.wait_ge(p_ready, 1 + t * N + n + 1)
                masked = q0 == kb * P
                mm = pe.matmul(ps_st[:, bank, 0:w], k_st[:, slot, kb * P:(kb + 1) * P], q_st[:, slot, q0:q0 + w],
                               start=True, stop=not masked)
                if masked:
                    mm = pe.matmul(ps_st[:, bank, 0:P], g["ident_h"][:, :], g["mask_kq"][:, :], start=False, stop=True)
                mm.then_inc(st_ready, 1)

            def times_v(i, u, k, first, half):
                t, slot, _, _, _ = at(i, u, k)
                if first != KB:
                    pe.wait_ge(v_ready, 1 + t + 1)
                pe.wait_ge(p_ready, 1 + 3 + t * N + first + 4)
                if first != 4:
                    pe.wait_ge(o_copied, 1 + (t * 2 + (1 if half else 2)))
                for q in range(4):
                    kb, _, w = ST[first + q]
                    w = w if half else HALF
                    mm = pe.matmul(ps_o[32 * q:32 * q + 32, half, HALF - w:HALF], v_st[:, slot % 2, kb, :], probs[:, first + q, 0:w],
                                   start=first != 4, stop=first != 0)
                mm.then_inc(pv_done, 1)

            def group_sums(i, u, k=0):
                t, _, _, _, _ = at(i, u, k)
                pe.wait_ge(o_copied, 1 + t * 2 + 4)
                pe.wait_ge(sum_copied, 1 + t + 1)
                for half in range(2):
                    mm = pe.matmul(ps_misc[32 * half:32 * half + 32, :], group_sum[:, :], o_sb[:, half, :], start=True, stop=True)
                mm.then_inc(summed, 1)

            def turn_max(i, u, k=0):
                t, slot, _, _, _ = at(i, u, k)
                pe.wait_ge(nm_ready, 1 + t + 1)
                pe.wait_ge(nm_copied, 1 + t)
                pe.transpose(ps_nm, nm[:, slot % 2, :], g["ident_h"][:, :]).then_inc(nm_turned, 1)

            def step(i, u, ahead, prev, turn):
                for n in range(N):
                    st_unit(i, u, n)
                    if ahead:
                        s_unit(i, u, 2, n)
                    if n == 2 and turn:
                        turn_max(i, u, 1)
                    if n == 2 and prev:
                        times_v(i, u, -1, KB, 0)
                    if n == 5 and prev:
                        group_sums(i, u, -1)
                    if n == 7:
                        times_v(i, u, 0, 0, 1)
                times_v(i, u, 0, 4, 1)

            pe.wait_ge(consts, 1 + 2 * 16 * RING)
            pe.wait_ge(gs_init, 6)
            pe.wait_ge(init, 5)
            for u in range(2):
                for n in range(N):
                    s_unit(0, u, 0, n)
                    if u == 1 and n == 2:
                        turn_max(0, 0)
            for u in range(RING):
                step(0, u, True, u > 0, True)
            with pe.Fori(1, STEPS - 1) as i:
                for u in range(RING):
                    step(i, u, True, True, True)
            for u in range(RING):
                step(STEPS - 1, u, u + 2 < RING, True, u + 1 < RING)
            times_v(STEPS - 1, RING - 1, 0, KB, 0)
            group_sums(STEPS - 1, RING - 1)

        @block.vector
        def _(v):
            v.wait_ge(init, 4)

            def copy_max(i, u, k):
                t, slot, r, _, _ = at(i, u, k)
                v.wait_ge(nm_turned, 1 + t + 1)
                if k or not isinstance(i, int) or i:
                    v.wait_ge(m_loaded[(slot + 2) % RING], 1 + (r + slot // 2) * 16)
                v.tensor_copy(nm_t[96:96 + 2 * KB, slot % 2, :], ps_nm).then_inc(nm_copied, 1)

            def step(i, u, prev):
                t, _, _, _, _ = at(i, u)
                b2 = u % 2
                for n, (qb, half, w) in enumerate(S):
                    v.wait_ge(s_ready, 1 + t * N + n + 1)
                    v.reduce_max(mx[:, b2, half, qb:qb + 1], ps_s[:, n % 2, 0:w], AX.X).then_inc(s_used, 1)
                    if n == 4 and prev:
                        copy_max(i, u, -1)
                v.wait_ge(s_used, 1 + t * N + N + 2)
                v.tensor_tensor(mx[:, b2, 0, :], mx[:, b2, 0, :], mx[:, b2, 1, :], ALU.max).then_inc(m_step, 1)
                v.wait_ge(m_step, 1 + t * 2 + 1)
                v.tensor_scalar(nm[:, b2, 0:KB], mx[:, b2, 0, :], -1.0, None, ALU.mult).then_inc(m_step, 1)
                v.wait_ge(m_step, 1 + t * 2 + 2)
                v.scalar_tensor_tensor(nm[:, b2, KB:2 * KB], mx[:, b2, 0, :], -1.0, nm[:, b2, 0:KB],
                                       ALU.mult, ALU.subtract).then_inc(nm_ready, 1)

            for u in range(RING):
                step(0, u, u > 0)
            with v.Fori(1, STEPS) as i:
                for u in range(RING):
                    step(i, u, True)
            copy_max(STEPS - 1, RING - 1, 0)

        @block.scalar
        def _(act):
            act.wait_ge(init, 5)

            def exps(i, u, lo, hi):
                t, _, _, _, _ = at(i, u)
                for n in range(lo, hi):
                    kb, half, w = ST[n]
                    if n % 4 == 0:
                        act.wait_ge(pv_done, 1 + t * 3 + 1 + n // 4)
                    act.wait_ge(st_ready, 1 + t * N + n + 1)
                    o = HALF - w if n >= KB else 0
                    act.activation(probs[:, n, o:o + w], ps_st[:, n % 3, 0:w], ACT.Exp).then_inc(p_ready, 1)

            def outputs(i, u, k, half):
                t, _, _, _, _ = at(i, u, k)
                act.wait_ge(pv_done, 1 + (t * 3 + (5 if half else 6)))
                act.wait_ge(summed, 1 + t)
                act.activation(o_sb[:, half, :], ps_o[:, half, :], ACT.Copy).then_inc(o_copied, 1)

            def sums(i, u, k=0):
                t, _, _, _, _ = at(i, u, k)
                act.wait_ge(summed, 1 + t + 1)
                act.wait_ge(o_stored, 1 + t * 32)
                act.activation(o_sum[:, :], ps_misc[0:64, :], ACT.Copy).then_inc(sum_copied, 1)

            def step(i, u, prev):
                exps(i, u, 0, 5)
                if prev:
                    outputs(i, u, -1, 0)
                exps(i, u, 5, 9)
                if prev:
                    sums(i, u, -1)
                exps(i, u, 9, N)
                outputs(i, u, 0, 1)

            for u in range(RING):
                step(0, u, u > 0)
            with act.Fori(1, STEPS) as i:
                for u in range(RING):
                    step(i, u, True)
            outputs(STEPS - 1, RING - 1, 0, 0)
            sums(STEPS - 1, RING - 1)


def attn0_output_stage(nc, g, scratch):
    with ExitStack() as ctx:
        m = Mem(nc, ctx, "a0o")
        l_sum = m.sb("l_sum", [P, CH])
        l_inv = m.sb("l_inv", [P, CH])
        o_t = m.sb("o_t", [P, 2, CH])
        inv_t = m.sb("inv_t", [P, 2, CH])
        on_t = m.sb("on_t", [P, 2, CH])
        ps_y = m.ps("ps_y", [P, 2, CT, P])
        l_loaded, inverted, inv_stored, loaded, divided, projected, copied = (
            m.sem(s) for s in ("l_loaded", "inverted", "inv_stored", "loaded", "divided", "projected", "copied"))
        loaded = [m.sem("loaded0"), m.sem("loaded1")]
        nc.all_engine_barrier()
        block = ctx.enter_context(nc.Block())

        @block.sync
        def _(sp):
            o_raw, row = scratch["o_raw"], NTOK
            head = (DH + 1) * row
            sp.dma_start(l_sum[:, :], bass.AP(o_raw.tensor, DH * row, [[head, H], [CH, NCH], [1, CH]])).then_inc(l_loaded, 16)
            sp.wait_ge(inverted, 2)
            sp.dma_start(scratch["l_inv"].rearrange("h (c t) -> (h c) t", t=CH), l_inv[:, :]).then_inc(inv_stored, 16)
            sp.wait_ge(inv_stored, 17)
            with sp.Fori(0, NCH // 2) as pair:
                for u in range(2):
                    c = pair * 2 + u
                    sp.wait_ge(divided, 1 + c)
                    at = scratch["l_inv"][0:1, ds(c * CH, CH)]
                    sp.dma_start(o_t[:, u, :], bass.AP(o_raw.tensor, at.offset, [[head, H], [row, DH], [1, CH]])).then_inc(loaded[u], 16)
                    sp.dma_start(inv_t[:, u, :], bass.AP(at.tensor, at.offset, [[row, H], [0, DH], [1, CH]])).then_inc(loaded[u], 16)

        @block.vector
        def _(v):
            v.wait_ge(l_loaded, 17)
            v.reciprocal(l_inv[:, :], l_sum[:, :]).then_inc(inverted, 1)
            with v.Fori(0, NCH // 2) as pair:
                for u in range(2):
                    c = pair * 2 + u
                    v.wait_ge(loaded[u], 1 + (pair + 1) * 32)
                    v.wait_ge(projected, 1 + c)
                    v.tensor_tensor(on_t[:, u, :], o_t[:, u, :], inv_t[:, u, :], ALU.mult).then_inc(divided, 1)

        @block.tensor
        def _(pe):
            with pe.Fori(0, NCH // 2) as pair:
                for u in range(2):
                    c = pair * 2 + u
                    pe.wait_ge(divided, 1 + c + 1)
                    pe.wait_ge(copied, 1 + c)
                    for k in range(CT):
                        mm = pe.matmul(ps_y[:, u, k, :], on_t[:, u, k * P:(k + 1) * P], g["w_t"][:, 3, :], start=True, stop=True)
                    mm.then_inc(projected, 1)

        @block.scalar
        def _(act):
            with act.Fori(0, NCH // 2) as pair:
                for u in range(2):
                    c = pair * 2 + u
                    act.wait_ge(projected, 1 + c + 1)
                    act.activation(g["y_tok"][:, ds(c * CT, CT), :], ps_y[:, u, :, :], ACT.Copy).then_inc(copied, 1)


E_ = 8
PARTS = 3


def route_buffers(m):
    d = {n: m.sb("route_" + n, [P, TILES, E_]) for n in ("eq", "sel1", "sel2", "rest", "gate", "tmp")}
    d.update({n: m.sb("route_" + n, [P, TILES]) for n in ("first", "v1", "v2", "w1", "w2")})
    d["step"] = m.sem("route_step")
    return d


class Chain:

    def __init__(self, v, sem):
        self.v, self.sem, self.n = v, sem, 0

    def __call__(self, instruction):
        self.n += 1
        instruction.then_inc(self.sem, 1)
        self.v.wait_ge(self.sem, 1 + self.n)


def per_tile(ap):
    return ap[:, :].unsqueeze(2).to_broadcast([P, TILES, E_])


def top_two(v, step, r, scores, g):
    place = g["place"][:, :].unsqueeze(1).to_broadcast([P, TILES, E_])
    for value, sel, src in (("v1", "sel1", scores), ("v2", "sel2", r["rest"])):
        step(v.reduce_max(r[value][:, :], src[:, :, :], AX.X))
        step(v.tensor_tensor(r["eq"][:, :, :], src[:, :, :], per_tile(r[value]), ALU.is_equal))
        step(v.tensor_tensor(r["eq"][:, :, :], r["eq"][:, :, :], place, ALU.mult))
        step(v.tensor_reduce(r["first"][:, :], r["eq"][:, :, :], AX.X, ALU.min))
        step(v.tensor_tensor(r[sel][:, :, :], per_tile(r["first"]), place, ALU.is_equal))
        if sel == "sel1":
            step(v.scalar_tensor_tensor(r["rest"][:, :, :], r["sel1"][:, :, :], NEG, scores[:, :, :], ALU.mult, ALU.add))


def split_gates(v, step, r, parts):
    step(v.tensor_copy(parts[:, :, 0, :], r["gate"][:, :, :]))
    step(v.tensor_tensor(r["rest"][:, :, :], r["gate"][:, :, :], parts[:, :, 0, :], ALU.subtract))
    step(v.tensor_copy(parts[:, :, 1, :], r["rest"][:, :, :]))
    step(v.tensor_tensor(parts[:, :, 2, :], r["rest"][:, :, :], parts[:, :, 1, :], ALU.subtract))


def gate_rows_stage(nc, g, parts, gate_t, tag):
    with ExitStack() as ctx:
        m = Mem(nc, ctx, tag)
        held = m.sb("held", [P, 2, CT, PARTS * E_], bf16)
        ps_g = m.ps("ps_g", [P, 2, 2 * CH], bf16)
        zeroed, picked, turned, copied = (m.sem(s) for s in ("zeroed", "picked", "turned", "copied"))
        nc.all_engine_barrier()
        block = ctx.enter_context(nc.Block())

        @block.gpsimd
        def _(pool):
            pool.memset(gate_t[:, :], 0.0).then_inc(zeroed, 1)
            pool.wait_ge(zeroed, 2)

        @block.vector
        def _(v):
            with v.Fori(0, NCH // 2) as pair:
                for u in range(2):
                    c = pair * 2 + u
                    v.wait_ge(turned, 1 + c)
                    v.tensor_copy(held[:, u, :, :], parts[:, ds(c * CT, CT), :, :].rearrange("p k s e -> p k (s e)")).then_inc(picked, 1)

        @block.tensor
        def _(pe):
            with pe.Fori(0, NCH // 2) as pair:
                for u in range(2):
                    c = pair * 2 + u
                    pe.wait_ge(picked, 1 + c + 1)
                    pe.wait_ge(copied, 1 + c)
                    for k in range(CT):
                        mm = pe.transpose(ps_g[0:PARTS * E_, u, k * P:(k + 1) * P], held[:, u, k, :], g["ident_h"][:, :])
                    mm.then_inc(turned, 1)

        @block.scalar
        def _(act):
            act.wait_ge(zeroed, 2)
            with act.Fori(0, NCH // 2) as pair:
                for u in range(2):
                    c = pair * 2 + u
                    act.wait_ge(turned, 1 + c + 1)
                    act.activation(gate_t[0:PARTS * E_, ds(c * CH, CH)], ps_g[0:PARTS * E_, u, 0:CH], ACT.Copy).then_inc(copied, 1)
            act.wait_ge(copied, 1 + NCH)


LIMIT, ALPHA = 7.0, 1.702


def moe0_weights_stage(nc, g, io, w):
    with ExitStack() as ctx:
        m = Mem(nc, ctx, "m0w")
        up = m.sb("up", [P, E_, 2, P], bf16)
        down = m.sb("down", [P, E_, P], bf16)
        gate = m.sb("gate", [E_, P], bf16)
        b1 = m.sb("b1", [E_, P, 2], bf16)
        ps_w = m.ps("ps_w", [P, 4, E_, P], bf16)
        loaded, b2_loaded, rows_loaded, turned, copied, zeroed = (
            m.sem(s) for s in ("loaded", "b2_loaded", "rows_loaded", "turned", "copied", "zeroed"))
        nc.all_engine_barrier()
        block = ctx.enter_context(nc.Block())

        @block.sync
        def _(sp):
            sp.dma_start(up[:, :, :, :], io["L0_ffn_mlp1_weight"].rearrange("e (i s) h -> i e s h", s=2)).then_inc(loaded, 16)
            sp.dma_start(down[:, :, :], io["L0_ffn_mlp2_weight"].rearrange("e h i -> h e i")).then_inc(loaded, 16)
            sp.dma_start(gate[:, :], io["L0_ffn_gate_weight"]).then_inc(loaded, 16)
            sp.dma_start(b1[:, :, :], io["L0_ffn_mlp1_bias"].rearrange("e (i s) -> e i s", s=2)).then_inc(loaded, 16)
            sp.dma_start(w["norm_w"][:, :], io["L0_ffn_norm_weight"].partition_broadcast(P)).then_inc(rows_loaded, 16)
            sp.dma_start(w["gate_b"][:, :], io["L0_ffn_gate_bias"].partition_broadcast(P)).then_inc(rows_loaded, 16)
            sp.wait_ge(zeroed, 2)
            for s in range(PARTS):
                sp.dma_start(w["b2_rows"][s * E_:(s + 1) * E_, :], io["L0_ffn_mlp2_bias"]).then_inc(b2_loaded, 16)
            sp.wait_ge(b2_loaded, 1 + 16 * PARTS)
            sp.wait_ge(rows_loaded, 33)

        @block.gpsimd
        def _(pool):
            pool.memset(w["b2_rows"][:, :], 0.0).then_inc(zeroed, 1)

        @block.tensor
        def _(pe):
            pe.wait_ge(loaded, 65)
            for s in range(2):
                for e in range(E_):
                    mm = pe.transpose(ps_w[:, s, e, :], up[:, e, s, :], g["ident_h"][:, :])
            for e in range(E_):
                mm = pe.transpose(ps_w[:, 2, e, :], down[:, e, :], g["ident_h"][:, :])
            for s in range(2):
                mm = pe.transpose(ps_w[:, 3, s, 0:E_], b1[:, :, s], g["ident_h"][0:E_, 0:E_])
            mm = pe.transpose(ps_w[:, 3, 2, 0:E_], gate[:, :], g["ident_h"][0:E_, 0:E_])
            mm.then_inc(turned, 1)

        @block.vector
        def _(v):
            v.wait_ge(turned, 2)
            for s in range(2):
                v.tensor_copy(w["up_t"][:, s, :, :], ps_w[:, s, :, :]).then_inc(copied, 1)
                v.tensor_copy(w["b1_t"][:, s, :], ps_w[:, 3, s, 0:E_]).then_inc(copied, 1)
            v.tensor_copy(w["down_t"][:, :, :], ps_w[:, 2, :, :]).then_inc(copied, 1)
            v.tensor_copy(w["gate_w"][:, :], ps_w[:, 3, 2, 0:E_]).then_inc(copied, 1)
            v.wait_ge(copied, 7)


def moe0_norm_stage(nc, g, w, xc, rms_inv):
    with ExitStack() as ctx:
        m = Mem(nc, ctx, "m0n")
        sq = m.sb("sq", [P, 2, CT, P])
        ss, root = m.sb("ss", [P, TILES]), m.sb("root", [P, TILES])
        normed, squared, mean_ready, rooted, inverted = (m.sem(s) for s in ("normed", "squared", "mean_ready", "rooted", "inverted"))
        nc.all_engine_barrier()
        block = ctx.enter_context(nc.Block())

        @block.vector
        def _(v):
            with v.Fori(0, NCH) as c:
                for k in range(CT):
                    t = c * CT + k
                    v.tensor_scalar(xc[:, ds(t, 1), :], g["x_tok"][:, ds(t, 1), :], g["mean"][:, ds(t, 1)], g["rstd"][:, ds(t, 1)],
                                    ALU.subtract, ALU.mult).then_inc(normed, 1)
            v.wait_ge(squared, 1 + TILES)
            v.tensor_scalar(ss[:, :], ss[:, :], 1.0 / P, EPS, ALU.mult, ALU.add).then_inc(mean_ready, 1)
            v.wait_ge(rooted, 2)
            v.reciprocal(rms_inv[:, :], root[:, :]).then_inc(inverted, 1)
            v.wait_ge(inverted, 2)

        @block.scalar
        def _(act):
            with act.Fori(0, NCH // 2) as pair:
                for u in range(2):
                    for k in range(CT):
                        t = (pair * 2 + u) * CT + k
                        act.wait_ge(normed, 1 + t + 1)
                        act.wait_ge(squared, 1 + (pair * 2) * CT)
                        act.activation(sq[:, u, k, :], xc[:, ds(t, 1), :], ACT.Square, accum_out=ss[:, ds(t, 1)]).then_inc(squared, 1)
            act.wait_ge(mean_ready, 2)
            act.activation(root[:, :], ss[:, :], ACT.Sqrt).then_inc(rooted, 1)


def moe0_route_stage(nc, g, w, xc, rms_inv, nf_t, gate_parts):
    with ExitStack() as ctx:
        m = Mem(nc, ctx, "m0r")
        nf = m.sb("nf", [P, 2, CT, P], bf16)
        nf_c = m.sb("nf_c", [P, 2, CH], bf16)
        logits = m.sb("logits", [P, TILES, E_])
        rounded = m.sb("rounded", [P, TILES, E_], bf16)
        r = route_buffers(m)
        ps_t = m.ps("ps_t", [P, 2, 2 * CH], bf16)
        ps_l = m.ps("ps_l", [P, 2, CT, P])
        scaled, turned, t_copied, c_copied, scored, l_copied, diff_ready, weights_ready = (
            m.sem(s) for s in ("scaled", "turned", "t_copied", "c_copied", "scored", "l_copied", "diff_ready", "weights_ready"))
        nc.all_engine_barrier()
        block = ctx.enter_context(nc.Block())

        @block.vector
        def _(v):
            with v.Fori(0, NCH // 2) as pair:
                for u in range(2):
                    c = pair * 2 + u
                    v.wait_ge(turned, 1 + c)
                    for k in range(CT):
                        t = c * CT + k
                        v.scalar_tensor_tensor(nf[:, u, k, :], xc[:, ds(t, 1), :].rearrange("p a e -> p (a e)"), rms_inv[:, ds(t, 1)], w["norm_w"][:, :],
                                               ALU.mult, ALU.mult).then_inc(scaled, 1)
            v.wait_ge(l_copied, 1 + NCH)
            step = Chain(v, r["step"])
            bias = w["gate_b"][:, :].unsqueeze(1).to_broadcast([P, TILES, E_])
            step(v.tensor_tensor(rounded[:, :, :], logits[:, :, :], bias, ALU.add))
            step(v.tensor_copy(logits[:, :, :], rounded[:, :, :]))
            top_two(v, step, r, logits, g)
            v.tensor_tensor(r["first"][:, :], r["v1"][:, :], r["v2"][:, :], ALU.subtract).then_inc(diff_ready, 1)
            v.wait_ge(weights_ready, 3)
            step(v.tensor_tensor(r["gate"][:, :, :], r["sel1"][:, :, :], per_tile(r["w1"]), ALU.mult))
            step(v.tensor_tensor(r["tmp"][:, :, :], r["sel2"][:, :, :], per_tile(r["w2"]), ALU.mult))
            step(v.tensor_tensor(r["gate"][:, :, :], r["gate"][:, :, :], r["tmp"][:, :, :], ALU.add))
            split_gates(v, step, r, gate_parts)

        @block.tensor
        def _(pe):
            with pe.Fori(0, NCH // 2) as pair:
                for u in range(2):
                    c = pair * 2 + u
                    pe.wait_ge(scaled, 1 + c * CT + CT)
                    pe.wait_ge(t_copied, 1 + c)
                    for k in range(CT):
                        mm = pe.transpose(ps_t[:, u, k * P:(k + 1) * P], nf[:, u, k, :], g["ident_h"][:, :])
                    mm.then_inc(turned, 1)
                    pe.wait_ge(t_copied, 1 + c + 1)
                    pe.wait_ge(l_copied, 1 + c)
                    for k in range(CT):
                        mm = pe.matmul(ps_l[:, u, k, 0:E_], nf_c[:, u, k * P:(k + 1) * P], w["gate_w"][:, :], start=True, stop=True)
                    mm.then_inc(scored, 1)

        @block.scalar
        def _(act):
            with act.Fori(0, NCH // 2) as pair:
                for u in range(2):
                    c = pair * 2 + u
                    act.wait_ge(turned, 1 + c + 1)
                    act.wait_ge(scored, 1 + c)
                    act.activation(nf_c[:, u, :], ps_t[:, u, 0:CH], ACT.Copy).then_inc(t_copied, 1)
                    act.wait_ge(t_copied, 1 + c + 1)
                    act.activation(nf_t[:, ds(c * CH, CH)], nf_c[:, u, :], ACT.Copy).then_inc(c_copied, 1)
                    act.wait_ge(scored, 1 + c + 1)
                    act.activation(logits[:, ds(c * CT, CT), :], ps_l[:, u, :, 0:E_], ACT.Copy).then_inc(l_copied, 1)
            act.wait_ge(diff_ready, 2)
            act.activation(r["w1"][:, :], r["first"][:, :], ACT.Sigmoid).then_inc(weights_ready, 1)
            act.activation(r["w2"][:, :], r["first"][:, :], ACT.Sigmoid, scale=-1.0).then_inc(weights_ready, 1)
            act.wait_ge(c_copied, 1 + NCH)


def moe0_experts_stage(nc, g, w, xc, nf_t, gate_t):
    with ExitStack() as ctx:
        m = Mem(nc, ctx, "m0e")
        glu0, glu, sig, lin0, lin = (m.sb(n, [P, 2, CH]) for n in ("glu0", "glu", "sig", "lin0", "lin"))
        prod, gated, hid = (m.sb(n, [P, 2, CH]) for n in ("prod", "gated", "hid"))
        comb = m.sb("comb", [P, 2, CH], bf16)
        summed = m.sb("summed", [P, 2, CT, P], bf16)
        ps_up = m.ps("ps_up", [P, 2, 2, CH])
        ps_g = m.ps("ps_g", [P, 2, CH])
        ps_y = m.ps("ps_y", [P, CH])
        ps_c = m.ps("ps_c", [P, 2 * CH], bf16)
        FREE = 2
        biased = m.sem("biased", 2 * FREE)
        lin_ready, sig_ready, prod_ready, gated_ready, hid_ready, down_done = (
            m.sem(s, FREE) for s in ("lin_ready", "sig_ready", "prod_ready", "gated_ready", "hid_ready", "down_done"))
        up_ready, glu_ready, gates_ready, y_ready, comb_ready, turned, sum_ready, y_copied = (
            m.sem(s) for s in ("up_ready", "glu_ready", "gates_ready", "y_ready", "comb_ready", "turned", "sum_ready", "y_copied"))
        STEPS = 2 * E_
        nc.all_engine_barrier()
        block = ctx.enter_context(nc.Block())

        def at(pair, s):
            return pair * STEPS + s, pair * 2 + s // E_, s // E_, s % E_

        @block.tensor
        def _(pe):
            def up(pair, s):
                n, c, u, e = at(pair, s)
                pe.wait_ge(biased, 1 + n * 2 + 2)
                for half in range(2):
                    pe.matmul(ps_up[:, s % 2, half, :], w["up_t"][:, half, e, :], nf_t[:, ds(c * CH, CH)],
                              start=True, stop=True).then_inc(up_ready, 1)

            def gates(pair, s):
                n, c, u, e = at(pair, s)
                pe.wait_ge(hid_ready, 1 + n + 1)
                pe.matmul(ps_g[:, s % 2, :], w["pick"][:, e, :], gate_t[:, ds(c * CH, CH)], start=True, stop=True).then_inc(gates_ready, 1)

            def down(pair, s):
                n, c, u, e = at(pair, s)
                pe.wait_ge(hid_ready, 1 + FREE + n + 1)
                if e == 0:
                    pe.wait_ge(comb_ready, 1 + c)
                pe.matmul(ps_y[:, :], w["down_t"][:, e, :], hid[:, s % 2, :], start=e == 0, stop=False).then_inc(down_done, 1)
                if e == E_ - 1:
                    pe.matmul(ps_y[:, :], w["b2_rows"][:, :], gate_t[:, ds(c * CH, CH)], start=False, stop=True).then_inc(y_ready, 1)

            def turn(pair, u):
                c = pair * 2 + u
                pe.wait_ge(comb_ready, 1 + c + 1)
                pe.wait_ge(sum_ready, 1 + c)
                for k in range(CT):
                    mm = pe.transpose(ps_c[:, k * P:(k + 1) * P], comb[:, u, k * P:(k + 1) * P], g["ident_h"][:, :])
                mm.then_inc(turned, 1)

            with pe.Fori(0, NCH // 2) as pair:
                up(pair, 0)
                for s in range(STEPS + 2):
                    if s + 1 < STEPS:
                        up(pair, s + 1)
                    if s < STEPS:
                        gates(pair, s)
                    if s == E_ + 3:
                        turn(pair, 0)
                    if s >= 2:
                        down(pair, s - 2)
                turn(pair, 1)

        @block.scalar
        def _(act):
            def biases(pair, s):
                n, c, u, e = at(pair, s)
                act.wait_ge(up_ready, 1 + n * 2 + 1)
                act.wait_ge(lin_ready, 1 + n + 1)
                act.activation(glu0[:, s % 2, :], ps_up[:, s % 2, 0, :], ACT.Identity, bias=w["b1_t"][:, 0, e:e + 1]).then_inc(biased, 1)
                act.wait_ge(up_ready, 1 + n * 2 + 2)
                act.activation(lin0[:, s % 2, :], ps_up[:, s % 2, 1, :], ACT.Identity, bias=w["b1_t"][:, 1, e:e + 1]).then_inc(biased, 1)

            def sigmoid(pair, s):
                n, c, u, e = at(pair, s)
                act.wait_ge(glu_ready, 1 + n + 1)
                act.wait_ge(gated_ready, 1 + n + 1)
                act.activation(sig[:, s % 2, :], glu[:, s % 2, :], ACT.Sigmoid, scale=ALPHA).then_inc(sig_ready, 1)

            def combine(pair, u):
                c = pair * 2 + u
                act.wait_ge(y_ready, 1 + c + 1)
                act.wait_ge(turned, 1 + c)
                act.activation(comb[:, u, :], ps_y[:, :], ACT.Copy).then_inc(comb_ready, 1)

            def keep(pair, u):
                c = pair * 2 + u
                act.wait_ge(sum_ready, 1 + c + 1)
                act.activation(g["y_tok"][:, ds(c * CT, CT), :], summed[:, u, :, :], ACT.Copy).then_inc(y_copied, 1)

            with act.Fori(0, NCH // 2) as pair:
                for s in range(STEPS + 1):
                    if s == E_ + 2:
                        combine(pair, 0)
                    if s == E_ + 5:
                        keep(pair, 0)
                    if s < STEPS:
                        biases(pair, s)
                    if s >= 1:
                        sigmoid(pair, s - 1)
                combine(pair, 1)
                keep(pair, 1)

        @block.vector
        def _(v):
            def product(pair, s):
                n, c, u, e = at(pair, s)
                q = s % 2
                v.wait_ge(biased, 1 + 2 * FREE + n * 2 + 1)
                v.wait_ge(sig_ready, 1 + n + 1)
                v.wait_ge(prod_ready, 1 + n + 1)
                v.tensor_scalar(glu[:, q, :], glu0[:, q, :], LIMIT, None, ALU.min).then_inc(glu_ready, 1)
                v.wait_ge(biased, 1 + 2 * FREE + n * 2 + 2)
                v.tensor_scalar(lin[:, q, :], lin0[:, q, :], LIMIT, -LIMIT, ALU.min, ALU.max).then_inc(lin_ready, 1)
                v.wait_ge(glu_ready, 1 + n + 1)
                v.wait_ge(lin_ready, 1 + FREE + n + 1)
                v.wait_ge(gated_ready, 1 + n + 1)
                v.scalar_tensor_tensor(prod[:, q, :], lin[:, q, :], 1.0, glu[:, q, :], ALU.add, ALU.mult).then_inc(prod_ready, 1)

            def hidden(pair, s):
                n, c, u, e = at(pair, s)
                v.wait_ge(gated_ready, 1 + FREE + n + 1)
                v.wait_ge(gates_ready, 1 + n + 1)
                v.wait_ge(down_done, 1 + n + 1)
                v.tensor_tensor(hid[:, s % 2, :], gated[:, s % 2, :], ps_g[:, s % 2, :], ALU.mult).then_inc(hid_ready, 1)

            def add_input(pair, u):
                c = pair * 2 + u
                v.wait_ge(turned, 1 + c + 1)
                v.wait_ge(y_copied, 1 + c)
                v.tensor_tensor(summed[:, u, :, :].rearrange("p k e -> p (k e)"), xc[:, ds(c * CT, CT), :].rearrange("p k e -> p (k e)"),
                                ps_c[:, 0:CH], ALU.add).then_inc(sum_ready, 1)

            with v.Fori(0, NCH // 2) as pair:
                for s in range(STEPS + 2):
                    if s < STEPS:
                        product(pair, s)
                    if s == E_ + 4:
                        add_input(pair, 0)
                    if s >= 2:
                        hidden(pair, s - 2)
                add_input(pair, 1)

        @block.gpsimd
        def _(pool):
            with pool.Fori(0, NCH // 2) as pair:
                for s in range(STEPS):
                    n, c, u, e = at(pair, s)
                    pool.wait_ge(sig_ready, 1 + FREE + n + 1)
                    pool.wait_ge(prod_ready, 1 + FREE + n + 1)
                    pool.wait_ge(hid_ready, 1 + n + 1)
                    pool.tensor_tensor(gated[:, s % 2, :], prod[:, s % 2, :], sig[:, s % 2, :], ALU.mult).then_inc(gated_ready, 1)


WIN = 16
PAD = 16


def attn1_project_stage(nc, g, q_t, k_t, kp_t, v_t, v_rows):
    with ExitStack() as ctx:
        m = Mem(nc, ctx, "a1p")
        norm = m.sb("norm", [P, 2, CT, P])
        norm_t = m.sb("norm_t", [P, 2, CH])
        v_c = m.sb("v_c", [P, 2, CT, P])
        ps_t = m.ps("ps_t", [P, 2, CH])
        ps_p = m.ps("ps_p", [P, 4, CH])
        ps_v = m.ps("ps_v", [P, CT, P])
        normed, turned, t_copied, projected, p_copied, v_ready, v_copied, padded = (
            m.sem(s) for s in ("normed", "turned", "t_copied", "projected", "p_copied", "v_ready", "v_copied", "padded"))
        stored = [m.sem("stored0"), m.sem("stored1")]
        nc.all_engine_barrier()
        block = ctx.enter_context(nc.Block())
        weights = (4, 5, 7, 6)

        @block.vector
        def _(v):
            with v.Fori(0, B) as b:
                for u in range(2):
                    c = b * 2 + u
                    v.wait_ge(turned, 1 + c)
                    for k in range(CT):
                        t = c * CT + k
                        v.tensor_scalar(norm[:, u, k, :], g["x_tok"][:, ds(t, 1), :], g["mean"][:, ds(t, 1)], g["rstd"][:, ds(t, 1)],
                                        ALU.subtract, ALU.mult).then_inc(normed, 1)
                    v.wait_ge(v_ready, 1 + c + 1)
                    v.wait_ge(stored[u], 1 + b * 16)
                    v.tensor_copy(v_c[:, u, :, :], ps_v[:, :, :]).then_inc(v_copied, 1)

        @block.tensor
        def _(pe):
            with pe.Fori(0, B) as b:
                for u in range(2):
                    c = b * 2 + u
                    pe.wait_ge(normed, 1 + c * CT + CT)
                    for k in range(CT):
                        mm = pe.transpose(ps_t[:, u, k * P:(k + 1) * P], norm[:, u, k, :], g["ident"][:, :])
                    mm.then_inc(turned, 1)
                    pe.wait_ge(t_copied, 1 + c + 1)
                    for i in range(4):
                        pe.wait_ge(p_copied, 1 + c * 4 + 0)
                        pe.matmul(ps_p[:, i, :], g["w_t"][:, weights[i], :], norm_t[:, u, :], start=True, stop=True).then_inc(projected, 1)
                    pe.wait_ge(v_copied, 1 + c)
                    for k in range(CT):
                        mm = pe.matmul(ps_v[:, k, :], norm_t[:, u, k * P:(k + 1) * P], g["w_t"][:, 6, :], start=True, stop=True)
                    mm.then_inc(v_ready, 1)

        @block.scalar
        def _(act):
            with act.Fori(0, B) as b:
                for u in range(2):
                    c = b * 2 + u
                    act.wait_ge(turned, 1 + c + 1)
                    act.wait_ge(v_ready, 1 + c)
                    act.activation(norm_t[:, u, :], ps_t[:, u, :], ACT.Copy).then_inc(t_copied, 1)
                    for i, (dst, pad) in enumerate(((q_t, 0), (k_t, PAD), (kp_t, 0), (v_t, PAD))):
                        act.wait_ge(projected, 1 + c * 4 + i + 1)
                        act.activation(dst[:, ds(b, 1), pad + u * CH:pad + (u + 1) * CH].rearrange("p a t -> p (a t)"),
                                       ps_p[:, i, :], ACT.Copy).then_inc(p_copied, 1)
            act.wait_ge(p_copied, 1 + 4 * NCH)

        @block.gpsimd
        def _(pool):
            pool.memset(v_t[:, :, 0:PAD], 0.0).then_inc(padded, 1)
            pool.wait_ge(p_copied, 1 + 4 * NCH)
            pool.tensor_copy(k_t[:, :, 0:PAD], k_t[:, :, PAD:PAD + 1].to_broadcast([P, B, PAD])).then_inc(padded, 1)
            pool.wait_ge(padded, 3)

        @block.sync
        def _(sp):
            dst = v_rows.rearrange("(k p) e -> p k e", p=P)
            with sp.Fori(0, B) as b:
                for u in range(2):
                    c = b * 2 + u
                    sp.wait_ge(v_copied, 1 + c + 1)
                    sp.dma_start(dst[:, ds(c * CT, CT), :], v_c[:, u, :, :]).then_inc(stored[u], 16)
            for u in range(2):
                sp.wait_ge(stored[u], 1 + 16 * B)


BLK = 32
GK = 8
BLOCKS = NTOK // BLK
PER_SEQ = T // BLK
GROUPS = [(0, 0, 8), (1, 0, 16), (2, 0, 24), (0, 8, 32), (1, 16, 32), (2, 24, 32)]


def attn1_windows_stage(nc, g, io, q_t, k_t, kp_t, v_t, v_rows, z_t, l_inv):
    with ExitStack() as ctx:
        m = Mem(nc, ctx, "a1w")
        head_mask = m.sb("head_mask", [P, H])
        key_mask = m.sb("key_mask", [P, P])
        m_pick = m.sb("m_pick", [P, P], bf16)
        mask_rows = m.sb("mask_rows", [P, 2, 3, BLK, WIN], bf16)
        max_rows = m.sb("max_rows", [P, 2, BLK], bf16)
        qk = m.sb("qk", [P, 2, BLK, WIN])
        bd_k = m.sb("bd_k", [P, 2, BLK, H])
        v_raw = m.sb("v_raw", [P, 2, 4, P])
        bd_v = m.sb("bd_v", [P, 2, 4, P])
        probs = m.sb("probs", [P, 2, 3, BLK, WIN])
        p_sum = m.sb("p_sum", [P, 2, BLK])
        r_max = m.sb("r_max", [P, 2, BLK])
        max_h = m.sb("max_h", [BLK, H])
        nm = m.sb("nm", [P, 2, H], bf16)
        uv = m.sb("uv", [P, BLK, WIN])
        ps_a = m.ps("ps_a", [P, 2, 3, BLK, WIN])
        ps_u = m.ps("ps_u", [P, BLK, WIN])
        ps_m = m.ps("ps_m", [P, CH])
        ps_max = ps_m[0:BLK, 0:P]
        ps_nm = ps_m[0:BLK, P:P + P // 2].bitcast(bf16)
        ps_l = ps_m[:, 2 * P:2 * P + BLK]
        (const_loaded, zeroed, qk_built, k_built, v_built, prior_done, logits_ready, r_ready, max_turned, max_ready, nm_ready,
         nm_split, nm_turned, rows_ready, max_taken, p_ready, p_summed, v_prior_done, u_ready, l_ready, u_read, l_read, z_ready) = (
            m.sem(s) for s in ("const_loaded", "zeroed", "qk_built", "k_built", "v_built", "prior_done", "logits_ready", "r_ready",
                               "max_turned", "max_ready", "nm_ready", "nm_split", "nm_turned", "rows_ready", "max_taken", "p_ready",
                               "p_summed", "v_prior_done", "u_ready", "l_ready", "u_read", "l_read", "z_ready"))
        v_loaded = [m.sem("v_loaded0"), m.sem("v_loaded1")]
        N_CONST = 4 * 16
        N_ZERO = 4
        PAIRS = BLOCKS // 2
        nc.all_engine_barrier()
        block = ctx.enter_context(nc.Block())

        def at(i, u, k=0):
            i, p = i + (u + k) // 2, (u + k) % 2
            half = PER_SEQ // 2
            later = 1 if p else ((i % half) + half - 1) // half
            return i * 2 + p, p, i, i // half, (i % half) * 2 * BLK + p * BLK, later

        def pairs(eng, step):
            for u in range(2):
                step(0, u, u > 0, True, True)
            with eng.Fori(1, PAIRS - 1) as i:
                for u in range(2):
                    step(i, u, True, True, True)
            for u in range(2):
                step(PAIRS - 1, u, True, u == 0, False)

        @block.sync
        def _(sp):
            sp.dma_start(head_mask[:, :], io["head_mask"]).then_inc(const_loaded, 16)
            sp.dma_start(key_mask[:, :], io["key_mask"]).then_inc(const_loaded, 16)
            sp.dma_start(m_pick[:, :], io["m_pick"]).then_inc(const_loaded, 16)
            sp.dma_start(mask_rows[:, :, :, :, :].rearrange("p a b c d -> p a (b c d)"), io["window_rows"]).then_inc(const_loaded, 16)

            def load(i, u):
                n, p, i, b, s0, _ = at(i, u)
                if not isinstance(n, int) or n >= 2:
                    sp.wait_ge(v_built, 1 + n - 1)
                rows = v_rows[ds(n * BLK, BLK), :]
                for k in range(GK):
                    src = bass.AP(rows.tensor, rows.offset + k * P, [[0, H], [GK * P, 4], [1, P]])
                    sp.dma_start(v_raw[k * H:(k + 1) * H, p, :, :], src).then_inc(v_loaded[p], 16)

            for u in range(2):
                load(0, u)
            with sp.Fori(1, PAIRS) as i:
                for u in range(2):
                    load(i, u)

        @block.gpsimd
        def _(pool):
            pool.memset(max_rows[:, :, :], 0.0).then_inc(zeroed, 1)
            pool.memset(bd_k[:, :, :, :], 0.0).then_inc(zeroed, 1)
            pool.memset(bd_v[:, :, :, :], 0.0).then_inc(zeroed, 1)
            pool.memset(nm[:, :, :], 0.0).then_inc(zeroed, 1)
            pool.wait_ge(const_loaded, 1 + N_CONST)
            pool.wait_ge(zeroed, 1 + N_ZERO)

            def build_keys(i, u, k=0, first=False):
                n, p, i, b, s0, _ = at(i, u, k)
                if not first:
                    pool.wait_ge(prior_done, 1 + n)
                keys = kp_t[:, ds(b, 1), ds(s0, BLK)].rearrange("p a t -> p (a t)").unsqueeze(2).to_broadcast([P, BLK, H])
                pool.tensor_tensor(bd_k[:, p, :, :], keys, head_mask[:, :].unsqueeze(1).to_broadcast([P, BLK, H]), ALU.mult).then_inc(k_built, 1)
                if not first:
                    pool.wait_ge(logits_ready, 1 + (n - 1 if not isinstance(n, int) else max(n - 1, 0)))
                queries = q_t[:, ds(b, 1), ds(s0, BLK)].rearrange("p a t -> p (a t)").unsqueeze(2).to_broadcast([P, BLK, WIN])
                window = view(k_t[:, ds(b, 1), ds(s0 + PAD - WIN + 1, 1)], [[1, BLK], [1, WIN]])
                pool.tensor_tensor(qk[:, p, :, :], queries, window, ALU.mult).then_inc(qk_built, 1)

            def build_values(i, u, first=False):
                n, p, i, b, s0, _ = at(i, u)
                pool.wait_ge(v_loaded[p], 1 + (i + 1) * 16 * GK)
                if not first:
                    pool.wait_ge(v_prior_done, 1 + n)
                pool.tensor_tensor(bd_v[:, p, :, :], v_raw[:, p, :, :], key_mask[:, :].unsqueeze(1).to_broadcast([P, 4, P]), ALU.mult).then_inc(v_built, 1)

            build_keys(0, 0, 0, True)
            build_keys(0, 1)

            def step(i, u, prev, ahead, ahead2):
                build_values(i, u, not prev)
                if ahead2:
                    build_keys(i, u, 2)

            pairs(pool, step)

        @block.tensor
        def _(pe):
            def group_keys(ring, p, q):
                return ring[:, p, q - 2] if q >= 2 else ring[:, 1 - p, q + 2]

            k_ring = bd_k[:, :, :, :].rearrange("p a (q k) h -> p a q (k h)", q=4)

            def masks(i, u, k):
                n, p, _, _, _, later = at(i, u, k)
                if not isinstance(n, int) or n >= 2:
                    pe.wait_ge(p_ready, 1 + n - 1)
                for slot in range(3):
                    rows = mask_rows[:, ds(later, 1), slot, :, :].rearrange("p a s j -> p (a s) j")
                    pe.matmul(ps_a[:, p, slot, :, :], m_pick[:, :], rows, start=True, stop=False, skip_group_check=True)

            def logits(i, u, k, groups):
                n, p, _, _, _, _ = at(i, u, k)
                if 0 in groups:
                    pe.wait_ge(k_built, 1 + n + 1)
                    pe.wait_ge(qk_built, 1 + n + 1)
                for q in groups:
                    slot, lo, hi = GROUPS[q]
                    mm = pe.matmul(ps_a[:, p, slot, lo:hi, :], group_keys(k_ring, p, q), qk[:, p, lo:hi, :],
                                   start=False, stop=False, skip_group_check=True)
                    if q == 1:
                        mm.then_inc(prior_done, 1)
                    if q == 5:
                        mm.then_inc(logits_ready, 1)

            def turn_max(i, u):
                n, p, _, _, _, _ = at(i, u)
                pe.wait_ge(r_ready, 1 + n + 1)
                if not isinstance(n, int) or n >= 2:
                    pe.wait_ge(l_read, 1 + n - 1)
                pe.transpose(ps_max, r_max[:, p, :], g["ident"][:, :]).then_inc(max_turned, 1)

            def turn_back(i, u):
                n, _, _, _, _, _ = at(i, u)
                pe.wait_ge(nm_ready, 1 + n + 1)
                pe.transpose(ps_nm, nm[:, :, :].rearrange("p a h -> p (a h)"), g["ident_h"][:, :]).then_inc(nm_turned, 1)

            def add_max(i, u):
                n, p, _, _, _, _ = at(i, u)
                pe.wait_ge(rows_ready, 1 + n + 1)
                rows = max_rows[:, p, :].unsqueeze(2).to_broadcast([P, BLK, WIN])
                for slot in range(3):
                    mm = pe.matmul(ps_a[:, p, slot, :, :], m_pick[:, :], rows, start=False, stop=True, skip_group_check=True)
                mm.then_inc(max_taken, 1)

            def times_v(i, u, k, groups):
                n, p, _, _, _, _ = at(i, u, k)
                if 2 in groups:
                    pe.wait_ge(v_built, 1 + n + 1)
                    pe.wait_ge(p_ready, 1 + n + 1)
                    pe.wait_ge(u_read, 1 + n)
                for q in groups:
                    slot, lo, hi = GROUPS[q]
                    mm = pe.matmul(ps_u[:, lo:hi, :], group_keys(bd_v, p, q), probs[:, p, slot, lo:hi, :],
                                   start=q == 2, stop=q == 4, skip_group_check=True)
                    if q == 1:
                        mm.then_inc(v_prior_done, 1)
                    if q == 4:
                        mm.then_inc(u_ready, 1)

            def sums(i, u, k=0):
                n, p, _, _, _, _ = at(i, u, k)
                pe.wait_ge(p_summed, 1 + n + 1)
                pe.matmul(ps_l, key_mask[:, :], p_sum[:, p, :], start=True, stop=True).then_inc(l_ready, 1)

            pe.wait_ge(const_loaded, 1 + N_CONST)
            pe.wait_ge(zeroed, 1 + N_ZERO)
            masks(0, 0, 0)
            logits(0, 0, 0, range(6))

            def step(i, u, prev, ahead, ahead2):
                if prev:
                    times_v(i, u, -1, (2, 5, 0, 1, 3))
                turn_max(i, u)
                if prev:
                    times_v(i, u, -1, (4,))
                if ahead:
                    masks(i, u, 1)
                turn_back(i, u)
                if ahead:
                    logits(i, u, 1, (0, 1))
                add_max(i, u)
                if ahead:
                    logits(i, u, 1, (2, 3))
                if prev:
                    sums(i, u, -1)
                if ahead:
                    logits(i, u, 1, (4, 5))

            pairs(pe, step)
            times_v(PAIRS - 1, 1, 0, (2, 5, 0, 1, 3, 4))
            sums(PAIRS - 1, 1)

        @block.vector
        def _(v):
            def finish(i, u, k):
                n, p, _, b, s0, _ = at(i, u, k)
                window = view(v_t[:, ds(b, 1), ds(s0 + PAD - WIN + 1, 1)], [[1, BLK], [1, WIN]])
                v.wait_ge(u_ready, 1 + n + 1)
                v.wait_ge(z_ready, 1 + n)
                v.tensor_tensor(uv[:, :, :], ps_u[:, :, :], window, ALU.mult).then_inc(u_read, 1)
                v.wait_ge(u_read, 1 + n + 1)
                v.tensor_reduce(z_t[:, ds(n * BLK, BLK)], uv[:, :, :], AX.X, ALU.add).then_inc(z_ready, 1)
                v.wait_ge(l_ready, 1 + n + 1)
                v.reciprocal(l_inv[:, ds(n * BLK, BLK)], ps_l).then_inc(l_read, 1)

            def sum_pairs(i, u, k):
                n, p, _, _, _, _ = at(i, u, k)
                v.wait_ge(p_ready, 1 + n + 1)
                if not isinstance(n, int) or n >= 2:
                    v.wait_ge(l_ready, 1 + n - 1)
                v.tensor_reduce(p_sum[:, p, :], probs[:, p, :, :, :].rearrange("p a s j -> p s a j"), AX.XY, ALU.add).then_inc(p_summed, 1)

            def negate(i, u):
                n, _, _, _, _, _ = at(i, u)
                v.wait_ge(max_turned, 1 + n + 1)
                v.tensor_reduce(max_h[:, :], ps_max.rearrange("s (k h) -> s h k", h=H), AX.X, ALU.max).then_inc(max_ready, 1)
                v.wait_ge(nm_turned, 1 + n)
                v.wait_ge(max_ready, 1 + n + 1)
                v.tensor_scalar(nm[0:BLK, 0, :], max_h[:, :], -1.0, None, ALU.mult).then_inc(nm_split, 1)
                v.wait_ge(nm_split, 1 + n + 1)
                v.scalar_tensor_tensor(nm[0:BLK, 1, :], max_h[:, :], -1.0, nm[0:BLK, 0, :], ALU.mult, ALU.subtract).then_inc(nm_ready, 1)

            def maximum(i, u, k=0):
                n, p, _, _, _, _ = at(i, u, k)
                v.wait_ge(logits_ready, 1 + n + 1)
                if not isinstance(n, int) or n >= 2:
                    v.wait_ge(max_turned, 1 + n - 1)
                v.tensor_reduce(r_max[:, p, :], ps_a[:, p, :, :, :].rearrange("p a s j -> p s a j"), AX.XY, ALU.max).then_inc(r_ready, 1)

            v.wait_ge(zeroed, 1 + N_ZERO)

            def step(i, u, prev, ahead, ahead2):
                maximum(i, u)
                negate(i, u)
                if prev:
                    sum_pairs(i, u, -1)
                    finish(i, u, -1)

            pairs(v, step)
            sum_pairs(PAIRS - 1, 1, 0)
            finish(PAIRS - 1, 1, 0)
            v.wait_ge(z_ready, 1 + BLOCKS)
            v.wait_ge(l_read, 1 + BLOCKS)

        @block.scalar
        def _(act):
            act.wait_ge(zeroed, 1 + N_ZERO)

            def step(i, u, prev, ahead, ahead2):
                n, p, _, _, _, _ = at(i, u)
                act.wait_ge(nm_turned, 1 + n + 1)
                if not isinstance(n, int) or n >= 2:
                    act.wait_ge(max_taken, 1 + n - 1)
                act.activation(max_rows[0:BLK, p, :], ps_nm[:, 0:BLK], ACT.Copy).then_inc(rows_ready, 1)
                if not isinstance(n, int) or n >= 2:
                    act.wait_ge(u_ready, 1 + n - 1)
                    act.wait_ge(p_summed, 1 + n - 1)
                act.wait_ge(max_taken, 1 + n + 1)
                act.activation(probs[:, p, :, :, :], ps_a[:, p, :, :, :], ACT.Exp).then_inc(p_ready, 1)

            pairs(act, step)


def attn1_output_stage(nc, g, io, z_t, l_inv):
    with ExitStack() as ctx:
        m = Mem(nc, ctx, "a1o")
        s = stats_buffers(m)
        z_c = m.sb("z_c", [P, 2, CH])
        norm = m.sb("norm", [P, 2, CT, P])
        gamma, beta = m.sb("gamma", [P, P]), m.sb("beta", [P, P])
        y_mean, y_rstd = m.sb("y_mean", [P, TILES]), m.sb("y_rstd", [P, TILES])
        ps_y = m.ps("ps_y", [P, 2, CT, P])
        loaded, picked, projected, normed, added, y_normed, scaled, shifted = (
            m.sem(x) for x in ("loaded", "picked", "projected", "normed", "added", "y_normed", "scaled", "shifted"))
        y = g["y_tok"]
        nc.all_engine_barrier()
        block = ctx.enter_context(nc.Block())

        @block.sync
        def _(sp):
            sp.dma_start(gamma[:, :], io["L1_attn_gamma"].partition_broadcast(P)).then_inc(loaded, 16)
            sp.dma_start(beta[:, :], io["L1_attn_beta"].partition_broadcast(P)).then_inc(loaded, 16)
            sp.wait_ge(loaded, 33)

        @block.scalar
        def _(act):
            scalar_stats(act, s, 0)

        @block.tensor
        def _(pe):
            with pe.Fori(0, NCH // 2) as pair:
                for u in range(2):
                    c = pair * 2 + u
                    pe.wait_ge(picked, 1 + c + 1)
                    pe.wait_ge(added, 1 + c)
                    for k in range(CT):
                        mm = pe.matmul(ps_y[:, u, k, :], z_c[:, u, k * P:(k + 1) * P], g["w_t"][:, 8, :], start=True, stop=True)
                    mm.then_inc(projected, 1)

        @block.vector
        def _(v):
            with v.Fori(0, NCH // 2) as pair:
                for u in range(2):
                    c = pair * 2 + u
                    for k in range(CT):
                        t = c * CT + k
                        v.tensor_scalar(norm[:, u, k, :], g["x_tok"][:, ds(t, 1), :], g["mean"][:, ds(t, 1)], g["rstd"][:, ds(t, 1)],
                                        ALU.subtract, ALU.mult).then_inc(normed, 1)
                    v.wait_ge(normed, 1 + c * CT + CT)
                    v.wait_ge(projected, 1 + c + 1)
                    v.tensor_tensor(y[:, ds(c * CT, CT), :], ps_y[:, u, :, :], norm[:, u, :, :], ALU.add).then_inc(added, 1)
            v.wait_ge(added, 1 + NCH)
            raw_stats(v, y, s, range(TILES))
            vector_stats(v, s, y_mean, y_rstd, 0)
            v.wait_ge(loaded, 33)
            with v.Fori(0, NCH) as c:
                for k in range(CT):
                    t = c * CT + k
                    v.tensor_scalar(y[:, ds(t, 1), :], y[:, ds(t, 1), :], y_mean[:, ds(t, 1)], y_rstd[:, ds(t, 1)],
                                    ALU.subtract, ALU.mult).then_inc(y_normed, 1)
                v.wait_ge(y_normed, 1 + c * CT + CT)
                yc = y[:, ds(c * CT, CT), :]
                v.tensor_tensor(yc, yc, gamma[:, :].unsqueeze(1).to_broadcast([P, CT, P]), ALU.mult).then_inc(scaled, 1)

        @block.gpsimd
        def _(pool):
            with pool.Fori(0, NCH // 2) as pair:
                for u in range(2):
                    c = pair * 2 + u
                    pool.wait_ge(projected, 1 + c)
                    pool.tensor_tensor(z_c[:, u, :], z_t[:, ds(c * CH, CH)], l_inv[:, ds(c * CH, CH)], ALU.mult).then_inc(picked, 1)
            pool.wait_ge(loaded, 33)
            with pool.Fori(0, NCH) as c:
                pool.wait_ge(scaled, 1 + c + 1)
                yc = y[:, ds(c * CT, CT), :]
                pool.tensor_tensor(yc, yc, beta[:, :].unsqueeze(1).to_broadcast([P, CT, P]), ALU.add).then_inc(shifted, 1)
            pool.wait_ge(shifted, 1 + NCH)


F1 = 512
FB = F1 // P
SHARED = E_
EXPERTS = E_ + 1


def moe1_weights_stage(nc, g, io, w):
    with ExitStack() as ctx:
        m = Mem(nc, ctx, "m1w")
        gate = m.sb("gate", [P, P])
        ps_w = m.ps("ps_w", [P, P])
        loaded, gate_loaded, zeroed, turned, copied = (m.sem(s) for s in ("loaded", "gate_loaded", "zeroed", "turned", "copied"))
        nc.all_engine_barrier()
        block = ctx.enter_context(nc.Block())

        @block.sync
        def _(sp):
            sp.wait_ge(zeroed, 2)
            sp.dma_start(gate[0:E_, :], io["L1_ffn_gate_W"]).then_inc(gate_loaded, 16)
            for dst, name in ((w["w1"], "w1"), (w["w3"], "w3")):
                sp.dma_start(dst[:, 0:E_, :], io[f"L1_ffn_{name}_e"].rearrange("e d f -> d e f")).then_inc(loaded, 16)
                shared = dst[:, SHARED, :].rearrange("d (n f) -> d n f", n=E_)
                sp.dma_start(shared, io[f"L1_ffn_{name}_s"].rearrange("n d f -> d n f")).then_inc(loaded, 16)
            sp.dma_start(w["w2"][:, 0:E_, :, :].rearrange("p e b d -> p (e b) d"),
                         io["L1_ffn_w2_e"].rearrange("e (b p) d -> p (e b) d", p=P)).then_inc(loaded, 16)
            sp.dma_start(w["w2"][:, SHARED, :, :], io["L1_ffn_w2_s"].rearrange("n f d -> (n f) d").rearrange("(b p) d -> p b d", p=P)).then_inc(loaded, 16)
            sp.wait_ge(loaded, 1 + 16 * 6)

        @block.gpsimd
        def _(pool):
            pool.memset(gate[:, :], 0.0).then_inc(zeroed, 1)

        @block.tensor
        def _(pe):
            pe.wait_ge(gate_loaded, 17)
            pe.matmul(ps_w[:, :], gate[:, :], g["ident"][:, :], start=True, stop=True).then_inc(turned, 1)

        @block.vector
        def _(v):
            v.wait_ge(turned, 2)
            v.tensor_copy(w["gate_w"][:, :], ps_w[:, :]).then_inc(copied, 1)
            v.wait_ge(copied, 2)


def moe1_route_stage(nc, g, w, x_t, gate_parts):
    with ExitStack() as ctx:
        m = Mem(nc, ctx, "m1r")
        norm = m.sb("norm", [P, 2, CT, P])
        x_c = m.sb("x_c", [P, 2, CH])
        logits = m.sb("logits", [P, TILES, E_])
        exps = m.sb("exps", [P, TILES, E_])
        r = route_buffers(m)
        ps_t = m.ps("ps_t", [P, 2, CH])
        ps_l = m.ps("ps_l", [P, 2, CT, P])
        normed, turned, t_copied, c_copied, scored, l_copied, exps_ready = (
            m.sem(s) for s in ("normed", "turned", "t_copied", "c_copied", "scored", "l_copied", "exps_ready"))
        nc.all_engine_barrier()
        block = ctx.enter_context(nc.Block())

        @block.vector
        def _(v):
            with v.Fori(0, NCH // 2) as pair:
                for u in range(2):
                    c = pair * 2 + u
                    v.wait_ge(turned, 1 + c)
                    for k in range(CT):
                        t = c * CT + k
                        v.tensor_scalar(norm[:, u, k, :], g["x_tok"][:, ds(t, 1), :], g["mean"][:, ds(t, 1)], g["rstd"][:, ds(t, 1)],
                                        ALU.subtract, ALU.mult).then_inc(normed, 1)
            v.wait_ge(l_copied, 1 + NCH)
            step = Chain(v, r["step"])
            step(v.reduce_max(r["v1"][:, :], logits[:, :, :], AX.X))
            step(v.tensor_tensor(logits[:, :, :], logits[:, :, :], per_tile(r["v1"]), ALU.subtract))
            v.wait_ge(exps_ready, 2)
            step(v.tensor_reduce(r["w1"][:, :], exps[:, :, :], AX.X, ALU.add))
            step(v.reciprocal(r["w2"][:, :], r["w1"][:, :]))
            step(v.tensor_tensor(logits[:, :, :], exps[:, :, :], per_tile(r["w2"]), ALU.mult))
            top_two(v, step, r, logits, g)
            step(v.tensor_tensor(r["eq"][:, :, :], r["sel1"][:, :, :], r["sel2"][:, :, :], ALU.add))
            step(v.scalar_tensor_tensor(r["gate"][:, :, :], r["eq"][:, :, :], 0.5, logits[:, :, :], ALU.mult, ALU.mult))
            split_gates(v, step, r, gate_parts)

        @block.tensor
        def _(pe):
            with pe.Fori(0, NCH // 2) as pair:
                for u in range(2):
                    c = pair * 2 + u
                    pe.wait_ge(normed, 1 + c * CT + CT)
                    pe.wait_ge(t_copied, 1 + c)
                    for k in range(CT):
                        mm = pe.transpose(ps_t[:, u, k * P:(k + 1) * P], norm[:, u, k, :], g["ident"][:, :])
                    mm.then_inc(turned, 1)
                    pe.wait_ge(t_copied, 1 + c + 1)
                    pe.wait_ge(l_copied, 1 + c)
                    for k in range(CT):
                        mm = pe.matmul(ps_l[:, u, k, :], x_c[:, u, k * P:(k + 1) * P], w["gate_w"][:, :], start=True, stop=True)
                    mm.then_inc(scored, 1)

        @block.scalar
        def _(act):
            with act.Fori(0, NCH // 2) as pair:
                for u in range(2):
                    c = pair * 2 + u
                    act.wait_ge(turned, 1 + c + 1)
                    act.wait_ge(scored, 1 + c)
                    act.wait_ge(c_copied, 1 + c)
                    act.activation(x_c[:, u, :], ps_t[:, u, :], ACT.Copy).then_inc(t_copied, 1)
                    act.wait_ge(scored, 1 + c + 1)
                    act.activation(logits[:, ds(c * CT, CT), :], ps_l[:, u, :, 0:E_], ACT.Copy).then_inc(l_copied, 1)
            act.wait_ge(r["step"], 3)
            act.activation(exps[:, :, :], logits[:, :, :], ACT.Exp).then_inc(exps_ready, 1)

        @block.gpsimd
        def _(pool):
            with pool.Fori(0, NCH // 2) as pair:
                for u in range(2):
                    c = pair * 2 + u
                    pool.wait_ge(t_copied, 1 + c + 1)
                    pool.tensor_copy(x_t[:, ds(c * CH, CH)], x_c[:, u, :]).then_inc(c_copied, 1)
            pool.wait_ge(c_copied, 1 + NCH)


def moe1_experts_stage(nc, g, w, x_t, gate_t):
    with ExitStack() as ctx:
        m = Mem(nc, ctx, "m1e")
        silu, hid = m.sb("silu", [P, 2, CH]), m.sb("hid", [P, 2, CH])
        gates, scaled = m.sb("gates", [P, 2, CH]), m.sb("scaled", [P, 2, CH])
        total, mixed = m.sb("total", [P, 2, CH]), m.sb("mixed", [P, 2, CH])
        ps_h = m.ps("ps_h", [P, 2, 2, CH])
        ps_y = m.ps("ps_y", [P, 2, CH])
        ps_g = m.ps("ps_g", [P, CH])
        ps_t = m.ps("ps_t", [P, CH])
        h_ready, silu_ready, hid_ready, down_done, gates_turned, gates_ready, scaled_ready, added, mixed_ready, turned, y_copied = (
            m.sem(s, 2 * (s in ("hid_ready", "scaled_ready"))) for s in ("h_ready", "silu_ready", "hid_ready", "down_done", "gates_turned", "gates_ready", "scaled_ready",
                               "added", "mixed_ready", "turned", "y_copied"))
        STEPS = EXPERTS * FB
        nc.all_engine_barrier()
        block = ctx.enter_context(nc.Block())

        def chunks(eng, body):
            with eng.Fori(0, NCH // 2) as pair:
                for u in range(2):
                    body(pair * 2 + u, u)

        @block.tensor
        def _(pe):
            def up(c, u, n):
                e, b = n // FB, n % FB
                pe.wait_ge(hid_ready, 1 + c * STEPS + n + 1)
                for s, name in ((0, "w1"), (1, "w3")):
                    pe.matmul(ps_h[:, n % 2, s, :], w[name][:, e, b * P:(b + 1) * P], x_t[:, ds(c * CH, CH)],
                              start=True, stop=True).then_inc(h_ready, 1)

            def down(c, u, n):
                e, b = n // FB, n % FB
                pe.wait_ge(hid_ready, 1 + c * STEPS + n + 3)
                if b == 0:
                    pe.wait_ge(scaled_ready, 1 + c * EXPERTS + e + 1)
                pe.matmul(ps_y[:, (u + e) % 2, :], w["w2"][:, e, b, :], hid[:, n % 2, :], start=b == 0, stop=b == FB - 1).then_inc(down_done, 1)

            def spread(c, e):
                pe.wait_ge(gates_ready, 1 + c * E_ + e)
                pe.matmul(ps_g[:, :], g["pick"][:, e, :], gate_t[:, ds(c * CH, CH)], start=True, stop=True).then_inc(gates_turned, 1)

            def chunk(c, u):
                up(c, u, 0)
                for n in range(STEPS):
                    if n + 1 < STEPS:
                        up(c, u, n + 1)
                    if n % FB == 0 and n // FB < E_:
                        spread(c, n // FB)
                    down(c, u, n)
                pe.wait_ge(mixed_ready, 1 + c + 1)
                pe.wait_ge(y_copied, 1 + c)
                for k in range(CT):
                    mm = pe.transpose(ps_t[:, k * P:(k + 1) * P], mixed[:, u, k * P:(k + 1) * P], g["ident"][:, :])
                mm.then_inc(turned, 1)

            chunks(pe, chunk)

        @block.scalar
        def _(act):
            def chunk(c, u):
                for n in range(STEPS):
                    act.wait_ge(h_ready, 1 + (c * STEPS + n) * 2 + 1)
                    act.wait_ge(hid_ready, 1 + c * STEPS + n + 1)
                    act.activation(silu[:, n % 2, :], ps_h[:, n % 2, 0, :], ACT.Silu).then_inc(silu_ready, 1)
                    e = n // FB
                    if n % FB == 0 and e < E_:
                        act.wait_ge(gates_turned, 1 + c * E_ + e + 1)
                        act.wait_ge(scaled_ready, 1 + c * EXPERTS + e + 1)
                        act.activation(gates[:, e % 2, :], ps_g[:, :], ACT.Copy).then_inc(gates_ready, 1)
                act.wait_ge(turned, 1 + c + 1)
                act.activation(g["y_tok"][:, ds(c * CT, CT), :], ps_t[:, :].rearrange("p (k e) -> p k e", k=CT), ACT.Copy).then_inc(y_copied, 1)

            chunks(act, chunk)

        @block.vector
        def _(v):
            def hidden(c, n):
                v.wait_ge(silu_ready, 1 + c * STEPS + n + 1)
                v.wait_ge(h_ready, 1 + (c * STEPS + n) * 2 + 2)
                if n >= 2:
                    v.wait_ge(down_done, 1 + c * STEPS + n - 1)
                v.tensor_tensor(hid[:, n % 2, :], silu[:, n % 2, :], ps_h[:, n % 2, 1, :], ALU.mult).then_inc(hid_ready, 1)

            def scale(c, u, e):
                v.wait_ge(down_done, 1 + c * STEPS + (e + 1) * FB)
                v.wait_ge(gates_ready, 1 + c * E_ + e + 1)
                v.wait_ge(added, 1 + (c * (E_ - 1) + (max(e - 2, 1) if e >= 2 else 0)))
                v.tensor_tensor(scaled[:, e % 2, :], ps_y[:, (u + e) % 2, :], gates[:, e % 2, :], ALU.mult).then_inc(scaled_ready, 1)

            def chunk(c, u):
                for n in range(STEPS):
                    if n < 2:
                        v.wait_ge(down_done, 1 + c * STEPS)
                    hidden(c, n)
                    if n % FB == 0 and n > 0:
                        scale(c, u, n // FB - 1)
                v.wait_ge(down_done, 1 + (c + 1) * STEPS)
                v.wait_ge(added, 1 + (c + 1) * (E_ - 1))
                v.wait_ge(turned, 1 + c)
                v.scalar_tensor_tensor(mixed[:, u, :], ps_y[:, (u + SHARED) % 2, :], 0.5 / E_, total[:, (E_ - 1) % 2, :],
                                       ALU.mult, ALU.add).then_inc(mixed_ready, 1)
                v.wait_ge(mixed_ready, 1 + c + 1)
                v.sem_inc(scaled_ready, 1)

            chunks(v, chunk)

        @block.gpsimd
        def _(pool):
            def chunk(c, u):
                for e in range(1, E_):
                    pool.wait_ge(scaled_ready, 1 + c * EXPERTS + 2 + e + 1)
                    if e == 1:
                        pool.wait_ge(mixed_ready, 1 + c)
                    else:
                        pool.wait_ge(added, 1 + c * (E_ - 1) + e - 1)
                    before = scaled[:, 0, :] if e == 1 else total[:, (e - 1) % 2, :]
                    pool.tensor_tensor(total[:, e % 2, :], before, scaled[:, e % 2, :], ALU.add).then_inc(added, 1)

            chunks(pool, chunk)


def moe0(nc, g, io):
    with ExitStack() as ctx:
        m = Mem(nc, ctx, "m0")
        w = {"up_t": m.sb("up_t", [P, 2, E_, P], bf16), "down_t": m.sb("down_t", [P, E_, P]), "gate_w": m.sb("gate_w", [P, E_], bf16),
             "b1_t": m.sb("b1_t", [P, 2, E_]), "b2_rows": m.sb("b2_rows", [P, P], bf16), "norm_w": m.sb("norm_w", [P, P]),
             "gate_b": m.sb("gate_b", [P, E_], bf16), "pick": g["pick"]}
        xc = m.sb("xc", [P, TILES, P], bf16)
        rms_inv = m.sb("rms_inv", [P, TILES])
        nf_t, gate_t = m.sb("nf_t", [P, NTOK], bf16), m.sb("gate_t", [P, NTOK], bf16)
        gate_parts = m.sb("gate_parts", [P, TILES, PARTS, E_], bf16)
        moe0_weights_stage(nc, g, io, w)
        moe0_norm_stage(nc, g, w, xc, rms_inv)
        moe0_route_stage(nc, g, w, xc, rms_inv, nf_t, gate_parts)
        gate_rows_stage(nc, g, gate_parts, gate_t, "m0g")
        moe0_experts_stage(nc, g, w, xc, nf_t, gate_t)


def attn1(nc, g, io, scratch):
    with ExitStack() as ctx:
        m = Mem(nc, ctx, "a1")
        q_t, kp_t = m.sb("q_t", [P, B, T]), m.sb("kp_t", [P, B, T])
        k_t, v_t = m.sb("k_t", [P, B, PAD + T]), m.sb("v_t", [P, B, PAD + T])
        z_t, l_inv = m.sb("z_t", [P, NTOK]), m.sb("l_inv", [P, NTOK])
        attn1_project_stage(nc, g, q_t, k_t, kp_t, v_t, scratch["v_rows"])
        attn1_windows_stage(nc, g, io, q_t, k_t, kp_t, v_t, scratch["v_rows"], z_t, l_inv)
        attn1_output_stage(nc, g, io, z_t, l_inv)


def moe1(nc, g, io):
    with ExitStack() as ctx:
        m = Mem(nc, ctx, "m1")
        w = {"w1": m.sb("w1", [P, EXPERTS, F1]), "w3": m.sb("w3", [P, EXPERTS, F1]), "w2": m.sb("w2", [P, EXPERTS, FB, P]),
             "gate_w": m.sb("gate_w", [P, P])}
        x_t, gate_t = m.sb("x_t", [P, NTOK]), m.sb("gate_t", [P, NTOK], bf16)
        gate_parts = m.sb("gate_parts", [P, TILES, PARTS, E_], bf16)
        moe1_weights_stage(nc, g, io, w)
        moe1_route_stage(nc, g, w, x_t, gate_parts)
        gate_rows_stage(nc, g, gate_parts, gate_t, "m1g")
        moe1_experts_stage(nc, g, w, x_t, gate_t)


def build_program(nc, io, out):
    scratch = {
        "qk_parts": nc.dram_tensor("qk_parts", [2, 3, P, NTOK], bf16, kind="Internal").ap(),
        "o_raw": nc.dram_tensor("o_raw", [H, DH + 1, NTOK], fp32, kind="Internal").ap(),
        "l_inv": nc.dram_tensor("l_inv", [H, NTOK], fp32, kind="Internal").ap(),
    }
    scratch["v_rows"] = nc.dram_tensor("v_rows", [NTOK, P], fp32, kind="Internal").ap()
    with ExitStack() as ctx:
        m = Mem(nc, ctx, "g")
        g = {
            "x_tok": m.sb("x_tok", [P, TILES, P]), "y_tok": m.sb("y_tok", [P, TILES, P]), 
            "mean": m.sb("mean", [P, TILES]), "rstd": m.sb("rstd", [P, TILES]),
            "ident": m.sb("ident", [P, P]), "ident_h": m.sb("ident_h", [P, P], bf16),
            "mask_qk": m.sb("mask_qk", [P, P], bf16), "mask_kq": m.sb("mask_kq", [P, P], bf16),
            "w_t": m.sb("w_t", [P, 9, P]), "place": m.sb("place", [P, E_]), "pick": m.sb("pick", [P, E_, P], bf16),
        }
        with semaphores_of(nc):
            load_stage(nc, io, g)
            first_norm_stage(nc, g)
            with ExitStack() as inner:
                g["v_tok"] = Mem(nc, inner, "attn0").sb("v_tok", [P, TILES, P])
                attn0_project_stage(nc, g, scratch)
                attn0_heads_stage(nc, g, scratch, io)
            attn0_output_stage(nc, g, scratch)
            residual_stage(nc, g, "res0")
        with semaphores_of(nc):
            moe0(nc, g, io)
            residual_stage(nc, g, "res1")
        with semaphores_of(nc):
            attn1(nc, g, io, scratch)
            residual_stage(nc, g, "res2")
        with semaphores_of(nc):
            moe1(nc, g, io)
            residual_stage(nc, g, "res3", out=out)


def kernel(**inputs):
    import numpy as np
    from concourse import bacc
    from concourse.bass_utils import run_bass_kernel_spmd

    half = inputs["L0_ffn_gate_weight"].dtype
    start = 2.0 ** -0.5
    slopes = np.array([start * start ** i for i in range(H)], np.float32)
    high = slopes.astype(half).astype(np.float32)
    middle = (slopes - high).astype(half).astype(np.float32)
    low = slopes - high - middle
    pos = np.arange(T)
    key_rows = np.zeros((P - 48, T), np.float32)
    key_rows[0:6:2], key_rows[1:6:2], key_rows[6:8] = pos // P * P, pos % P, 1.0
    slope_rows = np.zeros((H, 8, T), np.float32)
    for i, part in enumerate((high, middle, low)):
        slope_rows[:, 2 * i:2 * i + 2] = -part[:, None, None]
    arrays = {"key_rows": key_rows.astype(half), "slope_rows": slope_rows.astype(half),
              "query_rows": np.zeros((P - 48, T), half)}
    p = np.arange(P)
    head_mask = (p[:, None] // DH == np.arange(H)).astype(np.float32)
    key_mask = (p[:, None] % H == p[None, :] // DH).astype(np.float32)
    outside = np.ones((GK, 2, 3, BLK), bool)
    for q, (slot, lo, hi) in enumerate(GROUPS):
        for s in range(lo, hi):
            key = GK * q + np.arange(GK) - 2 * GK
            off = (key > s) | (key < s - WIN + 1)
            outside[:, 1, slot, s] = off
            outside[:, 0, slot, s] = off | (key < 0)
    m_pick = np.zeros((P, P), np.float32)
    m_pick[0:H] = m_pick[H:2 * H] = p[None, :] % H == np.arange(H)[:, None]
    m_pick[2 * H:2 * H + GK] = p[None, :] // H == np.arange(GK)[:, None]
    m_pick[2 * H + GK] = 1.0
    window_rows = np.zeros((P, 2, 3, BLK, WIN), np.float32)
    window_rows[2 * H:2 * H + GK] = np.where(outside, NEG, 0.0)[..., None]
    before = np.arange(BLK)[:, None] - (WIN - 1) + np.arange(WIN) < 0
    window_rows[2 * H + GK, 0] = np.where(before, NEG, 0.0)
    arrays.update(head_mask=head_mask, key_mask=key_mask, m_pick=m_pick.astype(half),
                  window_rows=window_rows.reshape(P, 2, 3 * BLK * WIN).astype(half))
    arrays.update({k: np.ascontiguousarray(v) for k, v in inputs.items()})

    nc = bacc.Bacc("TRN2", target_bir_lowering=False, num_devices=1)
    io = {k: nc.dram_tensor("in_" + k, a.shape, mybir.dt.from_np(a.dtype), kind="ExternalInput").ap() for k, a in arrays.items()}
    out = nc.dram_tensor("out", (B, T, P), fp32, kind="ExternalOutput").ap()
    build_program(nc, io, out)
    done = run_bass_kernel_spmd(nc, [{"in_" + k: a for k, a in arrays.items()}], core_ids=[0])
    return done.results[0]["out"]
```

```python
from contextlib import ExitStack, contextmanager

import concourse.bass as bass
from concourse import mybir

fp32 = mybir.dt.float32
bf16 = mybir.dt.bfloat16
ALU = mybir.AluOpType
ACT = mybir.ActivationFunctionType
AX = mybir.AxisListType

P = 128
B, T = 4, 1024
NTOK = B * T
TILES = NTOK // P
CH = 512
NCH = NTOK // CH
CT = CH // P
H, DH = 16, 8
EPS = 1e-5
NEG = -1e30


class Mem:

    def __init__(self, nc, ctx, stage):
        self.nc, self.ctx, self.stage = nc, ctx, stage + "_"

    def sb(self, name, shape, dt=fp32):
        return self.ctx.enter_context(self.nc.sbuf_tensor(self.stage + name, shape, dt))

    def ps(self, name, shape, dt=fp32):
        return self.ctx.enter_context(self.nc.psum_tensor(self.stage + name, shape, dt))

    def sem(self, name, free=0):
        handle = self.nc.alloc_semaphore(self.stage + name)
        self.nc.sync.sem_inc(handle, 1 + free)
        return handle

    def pool_dma_sem(self, name):
        return self.nc.alloc_semaphore(self.stage + name)


@contextmanager
def semaphores_of(nc):
    before = nc.snapshot_sems()
    yield
    nc.clear_and_free_semaphores(nc.allocated_since(before))
    nc.all_engine_barrier()


def ds(at, n):
    return bass.ds(at, n)


def view(ap, dims, offset=0):
    return bass.AP(ap.tensor, ap.offset + offset, [list(ap.ap[0]), *dims])


def load_stage(nc, io, g, w1, weights_loaded):
    with ExitStack() as ctx:
        m = Mem(nc, ctx, "load")
        names = ["L0_attn_Wq", "L0_attn_Wk", "L0_attn_Wv", "L0_attn_Wp",
                 "L1_attn_Wq", "L1_attn_Wk", "L1_attn_Wv", "L1_attn_Wkp", "L1_attn_Wo"]
        w_nat = m.sb("w_nat", [P, len(names), P])
        lora_a = m.sb("lora_a", [P, 3, DH])
        lora_b = m.sb("lora_b", [DH, 3, P])
        lora_at = m.sb("lora_at", [DH, 3, P])
        place_i = m.sb("place_i", [P, E_], mybir.dt.int32)
        s = stats_buffers(m)
        ps_a = m.ps("ps_a", [P, 3, 512])
        ps_w = m.ps("ps_w", [P, 3, 512])
        loaded, x_loaded, consts, at_ready, at_copied, w_ready, w_copied = (
            m.sem(s) for s in ("loaded", "x_loaded", "consts", "at_ready", "at_copied", "w_ready", "w_copied"))
        N_LOADS = len(names) + 6
        nc.all_engine_barrier()
        block = ctx.enter_context(nc.Block())

        @block.sync
        def _(sp):
            sp.dma_start(g["x_tok"][:, :, :], io["L0_attn_x"].rearrange("b (k p) e -> p (b k) e", p=P)).then_inc(x_loaded, 16)
            for i, n in enumerate(names):
                sp.dma_start(w_nat[:, i, :], io[n]).then_inc(loaded, 16)
            for i, n in enumerate("qkv"):
                sp.dma_start(lora_a[:, i, :], io["L0_attn_A" + n]).then_inc(loaded, 16)
                sp.dma_start(lora_b[:, i, :], io["L0_attn_B" + n]).then_inc(loaded, 16)
            start_moe1_loads(sp, io, w1, weights_loaded)
            sp.wait_ge(x_loaded, 17)

        @block.gpsimd
        def _(pool):
            pool.memset(g["ident"][:, :], 0.0).then_inc(consts, 1)
            pool.memset(g["ident_h"][:, :], 0.0).then_inc(consts, 1)
            pool.memset(g["mask_qk"][:, :], 0.0).then_inc(consts, 1)
            pool.memset(g["mask_kq"][:, :], 0.0).then_inc(consts, 1)
            pool.wait_ge(consts, 5)
            for t in ("ident", "ident_h"):
                pool.affine_select(out=g[t][:, :], in_=g[t][:, :], compare_op=ALU.not_equal, fill=1.0,
                                   base=0, pattern=[[-1, P]], channel_multiplier=1).then_inc(consts, 1)
            pool.iota(place_i[:, :], pattern=[[1, E_]], base=-E_, channel_multiplier=0).then_inc(consts, 1)
            pool.wait_ge(consts, 8)
            pool.tensor_copy(g["place"][:, :], place_i[:, :]).then_inc(consts, 1)
            pool.memset(g["pick"][:, :, :], 0.0).then_inc(consts, 1)
            for s in range(PARTS):
                pool.wait_ge(consts, 1 + 9 + s)
                pool.affine_select(out=g["pick"][:, :, :], in_=g["pick"][:, :, :], compare_op=ALU.not_equal, fill=1.0,
                                   base=-s * E_, pattern=[[-1, E_], [0, P]], channel_multiplier=1).then_inc(consts, 1)
            pool.affine_select(out=g["mask_qk"][:, :], in_=g["mask_qk"][:, :], compare_op=ALU.is_ge, fill=NEG,
                               base=0, pattern=[[-1, P]], channel_multiplier=1).then_inc(consts, 1)
            pool.affine_select(out=g["mask_kq"][:, :], in_=g["mask_kq"][:, :], compare_op=ALU.is_ge, fill=NEG,
                               base=0, pattern=[[1, P]], channel_multiplier=-1).then_inc(consts, 1)

        @block.tensor
        def _(pe):
            pe.wait_ge(consts, 1 + 9 + PARTS + 2)
            pe.wait_ge(loaded, 1 + 16 * N_LOADS)
            for i in range(3):
                pe.matmul(ps_a[0:DH, i, 0:P], lora_a[:, i, :], g["ident"][:, :], start=True, stop=True).then_inc(at_ready, 1)
            pe.wait_ge(at_copied, 4)
            for i in range(len(names)):
                if i >= 3:
                    pe.wait_ge(w_copied, 1 + i - 2)
                mm = pe.matmul(ps_w[:, i % 3, 0:P], w_nat[:, i, :], g["ident"][:, :], start=True, stop=i >= 3)
                if i < 3:
                    mm = pe.matmul(ps_w[:, i % 3, 0:P], lora_b[:, i, :], lora_at[:, i, :], start=False, stop=True)
                mm.then_inc(w_ready, 1)

        @block.vector
        def _(v):
            v.wait_ge(x_loaded, 17)
            raw_stats(v, g["x_tok"], s, range(TILES))
            vector_stats(v, s, g["mean"], g["rstd"], 0)
            v.wait_ge(at_ready, 4)
            for i in range(3):
                v.tensor_scalar(lora_at[:, i, :], ps_a[0:DH, i, 0:P], 2.0, None, ALU.mult).then_inc(at_copied, 1)
            for i, n in enumerate(names):
                v.wait_ge(w_ready, 1 + i + 1)
                scale = DH ** -0.5 if n.endswith("Wq") else 1.0
                v.tensor_scalar(g["w_t"][:, i, :], ps_w[:, i % 3, 0:P], scale, None, ALU.mult).then_inc(w_copied, 1)
            v.wait_ge(w_copied, 1 + len(names))

        @block.scalar
        def _(act):
            scalar_stats(act, s, 0)


def stats_buffers(m):
    d = {n: m.sb("ln_" + n, [P, TILES]) for n in ("sum", "dif", "m2", "sq", "var", "std")}
    d["raw"] = m.sb("ln_raw", [P, TILES, 6])
    d["step"] = m.sem("ln_step")
    d["raw_done"] = m.sem("ln_raw_done")
    d["var_ready"] = m.sem("ln_var_ready")
    d["std_ready"] = m.sem("ln_std_ready")
    d["uses"] = 0
    return d


def raw_stats(v, src, s, tiles):
    for t in tiles:
        v.bn_stats(s["raw"][:, t:t + 1, :], src[:, t:t + 1, :]).then_inc(s["raw_done"], 1)


def vector_stats(v, s, mean, rstd, use):
    v.wait_ge(s["raw_done"], 1 + TILES * (use + 1))
    raw, n = s["raw"], 4 * use
    v.tensor_tensor(s["sum"][:, :], raw[:, :, 1], raw[:, :, 4], ALU.add).then_inc(s["step"], 1)
    v.tensor_tensor(s["dif"][:, :], raw[:, :, 1], raw[:, :, 4], ALU.subtract).then_inc(s["step"], 1)
    v.tensor_tensor(s["m2"][:, :], raw[:, :, 2], raw[:, :, 5], ALU.add).then_inc(s["step"], 1)
    v.wait_ge(s["step"], 1 + 8 * use + 3)
    v.tensor_scalar(mean[:, :], s["sum"][:, :], 0.5, None, ALU.mult).then_inc(s["step"], 1)
    v.tensor_tensor(s["sq"][:, :], s["dif"][:, :], s["dif"][:, :], ALU.mult).then_inc(s["step"], 1)
    v.tensor_scalar(s["var"][:, :], s["m2"][:, :], 1.0 / P, EPS, ALU.mult, ALU.add).then_inc(s["step"], 1)
    v.wait_ge(s["step"], 1 + 8 * use + 6)
    v.scalar_tensor_tensor(s["m2"][:, :], s["sq"][:, :], 0.25, s["var"][:, :], ALU.mult, ALU.add).then_inc(s["var_ready"], 1)
    v.wait_ge(s["std_ready"], 1 + use + 1)
    v.reciprocal(rstd[:, :], s["std"][:, :]).then_inc(s["step"], 2)
    v.wait_ge(s["step"], 1 + 8 * use + 8)


def scalar_stats(act, s, use):
    act.wait_ge(s["var_ready"], 1 + use + 1)
    act.activation(s["std"][:, :], s["m2"][:, :], ACT.Sqrt).then_inc(s["std_ready"], 1)


def residual_stage(nc, g, tag):
    with ExitStack() as ctx:
        m = Mem(nc, ctx, tag)
        s = stats_buffers(m)
        y_mean, y_rstd, y_shift = m.sb("y_mean", [P, TILES]), m.sb("y_rstd", [P, TILES]), m.sb("y_shift", [P, TILES])
        shift_ready = m.sem("shift_ready")
        normed = [m.sem("normed_by_vector"), m.sem("normed_by_scalar")]
        added = [m.sem("added_by_pool"), m.sem("added_by_vector")]
        x, y = g["x_tok"], g["y_tok"]
        nc.all_engine_barrier()
        block = ctx.enter_context(nc.Block())

        def add(eng, c):
            eng.wait_ge(normed[c % 2], 1 + (c // 2 + 1) * CT)
            at = slice(c * CT, (c + 1) * CT)
            eng.tensor_tensor(x[:, at, :], x[:, at, :], y[:, at, :], ALU.add).then_inc(added[c % 2], 1)

        @block.vector
        def _(v):
            raw_stats(v, y, s, range(TILES))
            vector_stats(v, s, y_mean, y_rstd, 0)
            v.scalar_tensor_tensor(y_shift[:, :], y_mean[:, :], -1.0, y_rstd[:, :], ALU.mult, ALU.mult).then_inc(shift_ready, 1)
            for c in range(0, NCH, 2):
                for t in range(c * CT, (c + 1) * CT):
                    v.tensor_scalar(y[:, t, :], y[:, t, :], y_mean[:, t:t + 1], y_rstd[:, t:t + 1],
                                    ALU.subtract, ALU.mult).then_inc(normed[0], 1)
            for c in range(1, NCH, 2):
                add(v, c)
                for done in (c - 1, c):
                    v.wait_ge(added[done % 2], 1 + done // 2 + 1)
                    raw_stats(v, x, s, range(done * CT, (done + 1) * CT))
            vector_stats(v, s, g["mean"], g["rstd"], 1)

        @block.gpsimd
        def _(pool):
            for c in range(0, NCH, 2):
                add(pool, c)
            pool.wait_ge(added[0], 1 + NCH // 2)

        @block.scalar
        def _(act):
            scalar_stats(act, s, 0)
            act.wait_ge(shift_ready, 2)
            for c in range(1, NCH, 2):
                for t in range(c * CT, (c + 1) * CT):
                    act.activation(y[:, t, :], y[:, t, :], ACT.Identity, bias=y_shift[:, t:t + 1], scale=y_rstd[:, t:t + 1]).then_inc(normed[1], 1)
            scalar_stats(act, s, 1)


def chunks_ahead(eng, first, body):
    def step(c, u, ahead):
        if ahead:
            first(c + 1, 1 - u)
        body(c, u)

    first(0, 0)
    step(0, 0, True)
    step(1, 1, True)
    with eng.Fori(1, NCH // 2 - 1) as pair:
        for u in range(2):
            step(pair * 2 + u, u, True)
    step(NCH - 2, 0, True)
    step(NCH - 1, 1, False)


def chunks_in_turn(eng, first, body):
    for u in range(2):
        first(u, u)
        body(u, u)
    with eng.Fori(1, NCH // 2) as pair:
        for u in range(2):
            first(pair * 2 + u, u)
            body(pair * 2 + u, u)


def later_than(c, n=2):
    return not isinstance(c, int) or c >= n


def normalise(v, g, norm, normed, turned, c, u):
    if later_than(c):
        v.wait_ge(turned, 1 + c - 1)
    for k in range(CT):
        t = c * CT + k
        v.tensor_scalar(norm[:, u, k, :], g["x_tok"][:, ds(t, 1), :], g["mean"][:, ds(t, 1)], g["rstd"][:, ds(t, 1)],
                        ALU.subtract, ALU.mult).then_inc(normed, 1)


def turn(pe, ident, norm, normed, ps_t, t_copied, turned, c, u):
    pe.wait_ge(normed, 1 + c * CT + CT)
    if later_than(c):
        pe.wait_ge(t_copied, 1 + c - 1)
    for k in range(CT):
        mm = pe.transpose(ps_t[:, u, k * P:(k + 1) * P], norm[:, u, k, :], ident[:, :])
    mm.then_inc(turned, 1)


def attn0_project_stage(nc, g, scratch):
    with ExitStack() as ctx:
        m = Mem(nc, ctx, "a0p")
        norm = m.sb("norm", [P, 2, CT, P])
        norm_t = m.sb("norm_t", [P, 2, CH])
        full = m.sb("full", [P, 2, 2, CH])
        rest = m.sb("rest", [P, 2, 2, 2, CH])
        parts = m.sb("parts", [P, 2, 2, 3, CH], bf16)
        ps_t = m.ps("ps_t", [P, 2, CH])
        ps_qk = m.ps("ps_qk", [P, 2, CH])
        ps_v = m.ps("ps_v", [P, CT, P])
        normed, turned, t_copied, qk_ready, full_ready, v_ready, v_copied, split = (
            m.sem(s) for s in ("normed", "turned", "t_copied", "qk_ready", "full_ready", "v_ready", "v_copied", "split"))
        stored = [m.sem("stored0"), m.sem("stored1")]
        SPLIT = 5 * 2
        nc.all_engine_barrier()
        block = ctx.enter_context(nc.Block())

        @block.vector
        def _(v):
            def norm_chunk(c, u):
                normalise(v, g, norm, normed, turned, c, u)

            def split_chunk(c, u):
                v.wait_ge(stored[u], 1 + c // 2 * 32)
                v.wait_ge(full_ready, 1 + c * 2 + 2)
                for i in range(2):
                    v.tensor_copy(parts[:, u, i, 0, :], full[:, u, i, :]).then_inc(split, 1)
                v.wait_ge(split, 1 + c * SPLIT + 2)
                for i in range(2):
                    v.tensor_tensor(rest[:, u, i, 0, :], full[:, u, i, :], parts[:, u, i, 0, :], ALU.subtract).then_inc(split, 1)
                v.wait_ge(split, 1 + c * SPLIT + 4)
                for i in range(2):
                    v.tensor_copy(parts[:, u, i, 1, :], rest[:, u, i, 0, :]).then_inc(split, 1)
                v.wait_ge(split, 1 + c * SPLIT + 6)
                for i in range(2):
                    v.tensor_tensor(parts[:, u, i, 2, :], rest[:, u, i, 0, :], parts[:, u, i, 1, :], ALU.subtract).then_inc(split, 2)

            chunks_ahead(v, norm_chunk, split_chunk)

        @block.tensor
        def _(pe):
            def turn_chunk(c, u):
                turn(pe, g["ident"], norm, normed, ps_t, t_copied, turned, c, u)

            def project(c, u):
                pe.wait_ge(t_copied, 1 + c + 1)
                pe.wait_ge(full_ready, 1 + c * 2)
                for i in range(2):
                    pe.matmul(ps_qk[:, i, :], g["w_t"][:, i, :], norm_t[:, u, :], start=True, stop=True).then_inc(qk_ready, 1)
                pe.wait_ge(v_copied, 1 + c)
                for k in range(CT):
                    mm = pe.matmul(ps_v[:, k, :], norm_t[:, u, k * P:(k + 1) * P], g["w_t"][:, 2, :], start=True, stop=True)
                mm.then_inc(v_ready, 1)

            chunks_in_turn(pe, turn_chunk, project)

        @block.scalar
        def _(act):
            def copy_turned(c, u):
                act.wait_ge(turned, 1 + c + 1)
                if later_than(c):
                    act.wait_ge(v_ready, 1 + c - 1)
                act.activation(norm_t[:, u, :], ps_t[:, u, :], ACT.Copy).then_inc(t_copied, 1)

            def copy_projected(c, u):
                for i in range(2):
                    act.wait_ge(qk_ready, 1 + c * 2 + i + 1)
                    if later_than(c):
                        act.wait_ge(split, 1 + (c - 1) * SPLIT)
                    act.activation(full[:, u, i, :], ps_qk[:, i, :], ACT.Copy).then_inc(full_ready, 1)
                act.wait_ge(v_ready, 1 + c + 1)
                act.activation(g["v_tok"][:, ds(c * CT, CT), :], ps_v[:, :, :], ACT.Copy).then_inc(v_copied, 1)

            chunks_in_turn(act, copy_turned, copy_projected)

        @block.sync
        def _(sp):
            dst = scratch["qk_parts"].rearrange("i s f t -> f i s t")
            with sp.Fori(0, NCH // 2) as pair:
                for u in range(2):
                    c = pair * 2 + u
                    sp.wait_ge(split, 1 + c * SPLIT + SPLIT)
                    for i in range(2):
                        sp.dma_start(dst[:, i, :, ds(c * CH, CH)], parts[:, u, i, :, :]).then_inc(stored[u], 16)
            for u in range(2):
                sp.wait_ge(stored[u], 1 + 16 * NCH)


def attn0_heads_stage(nc, g, scratch, io):
    HEADS = B * H
    RING = 4
    STEPS = HEADS // RING
    KB = T // P
    HALF = T // 2
    ST = [(kb, 1, min(HALF, T - kb * P)) for kb in range(KB)] + [(kb, 0, HALF - kb * P) for kb in range(KB // 2)]
    S = []
    for qb in range(KB):
        w = (qb + 1) * P
        S.append((qb, 0, min(w, HALF)))
        if w > HALF:
            S.append((qb, 1, w - HALF))
    widths = [1, 1, 2, 2, 3, 4, 4, 4, 3, 4, 4, 4]
    S = [S.pop(next(i for i, unit in enumerate(S) if unit[2] == w * P)) for w in widths]
    N = len(ST)
    assert len(S) == N
    LOADED = (3 + 3 + 1) * 16
    with ExitStack() as ctx:
        m = Mem(nc, ctx, "a0h")
        q_st = m.sb("q_st", [P, RING, T], bf16)
        k_st = m.sb("k_st", [P, RING, T], bf16)
        v_st = m.sb("v_st", [P, 2, KB, 32])
        probs = m.sb("probs", [P, N, HALF])
        group_sum = m.sb("group_sum", [P, 32])
        o_sb = m.sb("o_sb", [P, 2, HALF])
        o_sum = m.sb("o_sum", [64, HALF])
        mx = m.sb("mx", [P, 2, 2, KB])
        nm = m.sb("nm", [P, 2, 2 * KB], bf16)
        nm_t = m.sb("nm_t", [P, 2, P], bf16)
        ps_s = m.ps("ps_s", [P, 2, HALF])
        ps_st = m.ps("ps_st", [P, 3, HALF])
        ps_o = m.ps("ps_o", [P, 2, HALF])
        ps_misc = m.ps("ps_misc", [P, HALF])
        ps_nm = ps_misc[96:96 + 2 * KB, 0:P // 2].bitcast(bf16)
        init = m.sem("init")
        gs_init = m.sem("gs_init")
        consts = m.sem("consts")
        qk_loaded = [m.sem(f"qk_loaded{i}") for i in range(RING)]
        s_ready, s_used = m.sem("s_ready"), m.sem("s_used", free=2)
        st_ready, p_ready = m.sem("st_ready"), m.sem("p_ready", free=3)
        pv_done = m.sem("pv_done", free=3)
        nm_ready, nm_turned, nm_copied = m.sem("nm_ready"), m.sem("nm_turned"), m.sem("nm_copied")
        m_step = m.sem("m_step")
        m_loaded = [m.sem(f"m_loaded{i}") for i in range(RING)]
        v_ready = m.sem("v_ready")
        o_copied, summed, sum_copied, o_stored = m.sem("o_copied", free=2), m.sem("summed"), m.sem("sum_copied", free=1), m.sem("o_stored")
        nc.all_engine_barrier()
        block = ctx.enter_context(nc.Block())

        def at(i, u, k=0):
            r, slot = i + (u + k) // RING, (u + k) % RING
            return r * RING + slot, slot, r, r // (H // RING), (r % (H // RING)) * RING + slot

        parts = scratch["qk_parts"]

        @block.sync
        def _(sp):
            for u in range(RING):
                sp.dma_start(k_st[48:P, u, :], io["key_rows"]).then_inc(consts, 16)
                sp.dma_start(q_st[48:P, u, :], io["query_rows"]).then_inc(consts, 16)
            sp.wait_ge(consts, 1 + 2 * 16 * RING)

            def load_head(i, u, k=0):
                _, slot, _, b, h = at(i, u, k)
                tok = ds(b * T, T)
                for part, n, row in ((0, 3, 0), (1, 2, 24), (2, 1, 40)):
                    src = parts[0, part, ds(h * DH, DH), tok]
                    sp.dma_start(q_st[row:row + n * DH, slot, :],
                                 bass.AP(src.tensor, src.offset, [[0, n], [NTOK, DH], [1, T]])).then_inc(qk_loaded[slot], 16)
                for n, row in ((3, 0), (2, 24), (1, 40)):
                    sp.dma_start(k_st[row:row + n * DH, slot, :], parts[1, 0:n, ds(h * DH, DH), tok]).then_inc(qk_loaded[slot], 16)
                sp.dma_start(q_st[48:56, slot, :], io["slope_rows"][ds(h, 1), :, :].rearrange("a r t -> (a r) t")).then_inc(qk_loaded[slot], 16)

            def load_max(i, u, k=0):
                t, slot, _, _, _ = at(i, u, k)
                sp.wait_ge(nm_copied, 1 + t + 1)
                sp.dma_start(q_st[54:56, slot, :].rearrange("r (q c) -> r q c", c=P), nm_t[96:96 + 2 * KB, slot % 2, :]).then_inc(m_loaded[slot], 16)

            def store(i, u, k=0):
                t, _, _, b, h = at(i, u, k)
                sp.wait_ge(sum_copied, 1 + t + 2)
                for half in range(2):
                    sp.dma_start(scratch["o_raw"][ds(h, 1), :, ds(b * T + half * HALF, HALF)].rearrange("a r t -> (a r) t"),
                                 o_sum[32 * half:32 * half + DH + 1, :]).then_inc(o_stored, 16)

            def step(i, u, loads, maxes, prev):
                if loads:
                    sp.wait_ge(st_ready, 1 + (i * RING + u) * N)
                    load_head(i, u, 3)
                if maxes:
                    load_max(i, u, 1)
                if prev:
                    store(i, u, -1)

            for u in range(3):
                load_head(0, u)
            load_max(0, 0)
            for u in range(RING):
                step(0, u, True, True, u > 0)
            with sp.Fori(1, STEPS - 1) as i:
                for u in range(RING):
                    step(i, u, True, True, True)
            for u in range(RING):
                step(STEPS - 1, u, u + 3 < RING, u + 1 < RING, True)
            store(STEPS - 1, RING - 1)
            sp.wait_ge(o_stored, 1 + 2 * 16 * HEADS)

        @block.gpsimd
        def _(pool):
            pool.memset(group_sum[:, :], 0.0).then_inc(gs_init, 1)
            for gq in range(4):
                pool.wait_ge(gs_init, 1 + gq + 1)
                pool.affine_select(out=group_sum[:, 0:DH + 1], in_=group_sum[:, 0:DH + 1], compare_op=ALU.not_equal, fill=1.0,
                                   base=-32 * gq, pattern=[[-1, DH + 1]], channel_multiplier=1).then_inc(gs_init, 1)
            pool.memset(v_st[:, :, :, :], 0.0).then_inc(init, 1)
            pool.memset(mx[:, :, :, :], NEG).then_inc(init, 1)
            pool.wait_ge(init, 3)
            pool.memset(v_st[:, :, :, DH:DH + 1], 1.0).then_inc(init, 1)
            pool.memset(probs[:, KB:N, :], 0.0).then_inc(init, 1)
            pool.wait_ge(init, 4)
            with pool.Fori(0, STEPS) as i:
                for u in range(RING):
                    t, _, _, b, h = at(i, u)
                    pool.wait_ge(pv_done, 1 + t * 3)
                    pool.tensor_copy(v_st[:, u % 2, :, 0:DH], g["v_tok"][:, ds(b * KB, KB), ds(h * DH, DH)]).then_inc(v_ready, 1)

        @block.tensor
        def _(pe):
            def s_unit(i, u, k, n):
                t, slot, r, _, _ = at(i, u, k)
                qb, half, w = S[n]
                bank, k0 = n % 2, half * HALF
                if n == 0:
                    pe.wait_ge(qk_loaded[slot], 1 + (r + 1) * LOADED)
                pe.wait_ge(s_used, 1 + t * N + n + 1)
                diag = qb * P - k0
                masked = 0 <= diag < w
                mm = pe.matmul(ps_s[:, bank, 0:w], q_st[:, slot, qb * P:(qb + 1) * P], k_st[:, slot, k0:k0 + w],
                               start=True, stop=not masked)
                if masked:
                    mm = pe.matmul(ps_s[:, bank, diag:diag + P], g["ident_h"][:, :], g["mask_qk"][:, :], start=False, stop=True)
                mm.then_inc(s_ready, 1)

            def st_unit(i, u, n):
                t, slot, r, _, _ = at(i, u)
                kb, half, w = ST[n]
                bank, q0 = n % 3, (half + 1) * HALF - w
                if n == 0:
                    pe.wait_ge(m_loaded[slot], 1 + (r + 1) * 16)
                pe.wait_ge(p_ready, 1 + t * N + n + 1)
                masked = q0 == kb * P
                mm = pe.matmul(ps_st[:, bank, 0:w], k_st[:, slot, kb * P:(kb + 1) * P], q_st[:, slot, q0:q0 + w],
                               start=True, stop=not masked)
                if masked:
                    mm = pe.matmul(ps_st[:, bank, 0:P], g["ident_h"][:, :], g["mask_kq"][:, :], start=False, stop=True)
                mm.then_inc(st_ready, 1)

            def times_v(i, u, k, first, half):
                t, slot, _, _, _ = at(i, u, k)
                if first != KB:
                    pe.wait_ge(v_ready, 1 + t + 1)
                pe.wait_ge(p_ready, 1 + 3 + t * N + first + 4)
                if first != 4:
                    pe.wait_ge(o_copied, 1 + (t * 2 + (1 if half else 2)))
                for q in range(4):
                    kb, _, w = ST[first + q]
                    w = w if half else HALF
                    mm = pe.matmul(ps_o[32 * q:32 * q + 32, half, HALF - w:HALF], v_st[:, slot % 2, kb, :], probs[:, first + q, 0:w],
                                   start=first != 4, stop=first != 0)
                mm.then_inc(pv_done, 1)

            def group_sums(i, u, k=0):
                t, _, _, _, _ = at(i, u, k)
                pe.wait_ge(o_copied, 1 + t * 2 + 4)
                pe.wait_ge(sum_copied, 1 + t + 1)
                for half in range(2):
                    mm = pe.matmul(ps_misc[32 * half:32 * half + 32, :], group_sum[:, :], o_sb[:, half, :], start=True, stop=True)
                mm.then_inc(summed, 1)

            def turn_max(i, u, k=0):
                t, slot, _, _, _ = at(i, u, k)
                pe.wait_ge(nm_ready, 1 + t + 1)
                pe.wait_ge(nm_copied, 1 + t)
                pe.transpose(ps_nm, nm[:, slot % 2, :], g["ident_h"][:, :]).then_inc(nm_turned, 1)

            def step(i, u, ahead, prev, turn):
                for n in range(N):
                    st_unit(i, u, n)
                    if ahead:
                        s_unit(i, u, 2, n)
                    if n == 2 and turn:
                        turn_max(i, u, 1)
                    if n == 1 and prev:
                        times_v(i, u, -1, KB, 0)
                    if n == 6 and prev:
                        group_sums(i, u, -1)
                    if n == 8:
                        times_v(i, u, 0, 0, 1)
                times_v(i, u, 0, 4, 1)

            pe.wait_ge(consts, 1 + 2 * 16 * RING)
            pe.wait_ge(gs_init, 6)
            pe.wait_ge(init, 5)
            for u in range(2):
                for n in range(N):
                    s_unit(0, u, 0, n)
                    if u == 1 and n == 2:
                        turn_max(0, 0)
            for u in range(RING):
                step(0, u, True, u > 0, True)
            with pe.Fori(1, STEPS - 1) as i:
                for u in range(RING):
                    step(i, u, True, True, True)
            for u in range(RING):
                step(STEPS - 1, u, u + 2 < RING, True, u + 1 < RING)
            times_v(STEPS - 1, RING - 1, 0, KB, 0)
            group_sums(STEPS - 1, RING - 1)

        @block.vector
        def _(v):
            v.wait_ge(init, 4)

            def copy_max(i, u, k):
                t, slot, r, _, _ = at(i, u, k)
                v.wait_ge(nm_turned, 1 + t + 1)
                if later_than(t):
                    v.wait_ge(m_loaded[(slot + 2) % RING], 1 + (r + slot // 2) * 16)
                v.tensor_copy(nm_t[96:96 + 2 * KB, slot % 2, :], ps_nm).then_inc(nm_copied, 1)

            def step(i, u, prev):
                t, _, _, _, _ = at(i, u)
                b2 = u % 2
                for n, (qb, half, w) in enumerate(S):
                    v.wait_ge(s_ready, 1 + t * N + n + 1)
                    v.reduce_max(mx[:, b2, half, qb:qb + 1], ps_s[:, n % 2, 0:w], AX.X).then_inc(s_used, 1)
                    if n == 4 and prev:
                        copy_max(i, u, -1)
                v.wait_ge(s_used, 1 + t * N + N + 2)
                v.tensor_tensor(mx[:, b2, 0, :], mx[:, b2, 0, :], mx[:, b2, 1, :], ALU.max).then_inc(m_step, 1)
                v.wait_ge(m_step, 1 + t * 2 + 1)
                v.tensor_scalar(nm[:, b2, 0:KB], mx[:, b2, 0, :], -1.0, None, ALU.mult).then_inc(m_step, 1)
                v.wait_ge(m_step, 1 + t * 2 + 2)
                v.scalar_tensor_tensor(nm[:, b2, KB:2 * KB], mx[:, b2, 0, :], -1.0, nm[:, b2, 0:KB],
                                       ALU.mult, ALU.subtract).then_inc(nm_ready, 1)

            for u in range(RING):
                step(0, u, u > 0)
            with v.Fori(1, STEPS) as i:
                for u in range(RING):
                    step(i, u, True)
            copy_max(STEPS - 1, RING - 1, 0)

        @block.scalar
        def _(act):
            act.wait_ge(init, 5)

            def exps(i, u, lo, hi):
                t, _, _, _, _ = at(i, u)
                for n in range(lo, hi):
                    kb, half, w = ST[n]
                    if n % 4 == 0:
                        act.wait_ge(pv_done, 1 + t * 3 + 1 + n // 4)
                    act.wait_ge(st_ready, 1 + t * N + n + 1)
                    o = HALF - w if n >= KB else 0
                    act.activation(probs[:, n, o:o + w], ps_st[:, n % 3, 0:w], ACT.Exp).then_inc(p_ready, 1)

            def outputs(i, u, k, half):
                t, _, _, _, _ = at(i, u, k)
                act.wait_ge(pv_done, 1 + (t * 3 + (5 if half else 6)))
                act.wait_ge(summed, 1 + t)
                act.activation(o_sb[:, half, :], ps_o[:, half, :], ACT.Copy).then_inc(o_copied, 1)

            def sums(i, u, k=0):
                t, _, _, _, _ = at(i, u, k)
                act.wait_ge(summed, 1 + t + 1)
                act.wait_ge(o_stored, 1 + t * 32)
                act.activation(o_sum[:, :], ps_misc[0:64, :], ACT.Copy).then_inc(sum_copied, 1)

            def step(i, u, prev):
                exps(i, u, 0, 4)
                if prev:
                    outputs(i, u, -1, 0)
                exps(i, u, 4, 9)
                if prev:
                    sums(i, u, -1)
                exps(i, u, 9, N)
                outputs(i, u, 0, 1)

            for u in range(RING):
                step(0, u, u > 0)
            with act.Fori(1, STEPS) as i:
                for u in range(RING):
                    step(i, u, True)
            outputs(STEPS - 1, RING - 1, 0, 0)
            sums(STEPS - 1, RING - 1)


def attn0_output_stage(nc, g, scratch):
    with ExitStack() as ctx:
        m = Mem(nc, ctx, "a0o")
        l_sum = m.sb("l_sum", [P, CH])
        l_inv = m.sb("l_inv", [P, CH])
        PIECES = 4
        PIECE = NTOK // PIECES
        o_t = m.sb("o_t", [P, PIECES, PIECE])
        inv_t = m.sb("inv_t", [P, PIECES, PIECE])
        on_t = m.sb("on_t", [P, 2, CH])
        ps_y = m.ps("ps_y", [P, 2, CT, P])
        l_loaded, inverted, inv_stored, divided, projected, copied = (
            m.sem(s) for s in ("l_loaded", "inverted", "inv_stored", "divided", "projected", "copied"))
        loaded = [m.sem(f"loaded{n}") for n in range(PIECES)]
        nc.all_engine_barrier()
        block = ctx.enter_context(nc.Block())

        @block.sync
        def _(sp):
            o_raw, row = scratch["o_raw"], NTOK
            head = (DH + 1) * row
            sp.dma_start(l_sum[:, :], bass.AP(o_raw.tensor, DH * row, [[head, H], [CH, NCH], [1, CH]])).then_inc(l_loaded, 16)
            for n in range(PIECES):
                sp.dma_start(o_t[:, n, :], bass.AP(o_raw.tensor, n * PIECE, [[head, H], [row, DH], [1, PIECE]])).then_inc(loaded[n], 16)
            sp.wait_ge(inverted, 2)
            sp.dma_start(scratch["l_inv"].rearrange("h (c t) -> (h c) t", t=CH), l_inv[:, :]).then_inc(inv_stored, 16)
            sp.wait_ge(inv_stored, 17)
            for n in range(PIECES):
                sp.dma_start(inv_t[:, n, :], bass.AP(scratch["l_inv"].tensor, n * PIECE, [[row, H], [0, DH], [1, PIECE]])).then_inc(loaded[n], 16)

        @block.vector
        def _(v):
            v.wait_ge(l_loaded, 17)
            v.reciprocal(l_inv[:, :], l_sum[:, :]).then_inc(inverted, 1)
            for c in range(NCH):
                n, at = c // 2, slice(c % 2 * CH, (c % 2 + 1) * CH)
                v.wait_ge(loaded[n], 33)
                if c >= 2:
                    v.wait_ge(projected, 1 + c - 1)
                v.tensor_tensor(on_t[:, c % 2, :], o_t[:, n, at], inv_t[:, n, at], ALU.mult).then_inc(divided, 1)

        @block.tensor
        def _(pe):
            with pe.Fori(0, NCH // 2) as pair:
                for u in range(2):
                    c = pair * 2 + u
                    pe.wait_ge(divided, 1 + c + 1)
                    pe.wait_ge(copied, 1 + c)
                    for k in range(CT):
                        mm = pe.matmul(ps_y[:, u, k, :], on_t[:, u, k * P:(k + 1) * P], g["w_t"][:, 3, :], start=True, stop=True)
                    mm.then_inc(projected, 1)

        @block.scalar
        def _(act):
            with act.Fori(0, NCH // 2) as pair:
                for u in range(2):
                    c = pair * 2 + u
                    act.wait_ge(projected, 1 + c + 1)
                    act.activation(g["y_tok"][:, ds(c * CT, CT), :], ps_y[:, u, :, :], ACT.Copy).then_inc(copied, 1)


E_ = 8
PARTS = 3


def route_buffers(m):
    d = {n: m.sb("route_" + n, [P, TILES, E_]) for n in ("eq", "sel1", "sel2", "rest", "gate", "tmp")}
    d.update({n: m.sb("route_" + n, [P, TILES]) for n in ("first", "v1", "v2", "w1", "w2")})
    return d


class Chain:

    def __init__(self, v, sem):
        self.v, self.sem, self.n = v, sem, 0

    def __call__(self, instruction):
        self.n += 1
        instruction.then_inc(self.sem, 1)
        self.v.wait_ge(self.sem, 1 + self.n)


def per_tile(ap):
    return ap[:, :].unsqueeze(2).to_broadcast([P, TILES, E_])


def top_two(v, step, r, scores, g):
    place = g["place"][:, :].unsqueeze(1).to_broadcast([P, TILES, E_])
    for value, sel, src in (("v1", "sel1", scores), ("v2", "sel2", r["rest"])):
        step(v.reduce_max(r[value][:, :], src[:, :, :], AX.X))
        step(v.tensor_tensor(r["eq"][:, :, :], src[:, :, :], per_tile(r[value]), ALU.is_equal))
        step(v.tensor_tensor(r["eq"][:, :, :], r["eq"][:, :, :], place, ALU.mult))
        step(v.tensor_reduce(r["first"][:, :], r["eq"][:, :, :], AX.X, ALU.min))
        step(v.tensor_tensor(r[sel][:, :, :], per_tile(r["first"]), place, ALU.is_equal))
        if sel == "sel1":
            step(v.scalar_tensor_tensor(r["rest"][:, :, :], r["sel1"][:, :, :], NEG, scores[:, :, :], ALU.mult, ALU.add))


def split_gates(v, step, r, parts):
    step(v.tensor_copy(parts[:, :, 0, :], r["gate"][:, :, :]))
    step(v.tensor_tensor(r["rest"][:, :, :], r["gate"][:, :, :], parts[:, :, 0, :], ALU.subtract))
    step(v.tensor_copy(parts[:, :, 1, :], r["rest"][:, :, :]))
    step(v.tensor_tensor(parts[:, :, 2, :], r["rest"][:, :, :], parts[:, :, 1, :], ALU.subtract))


def gate_rows_stage(nc, g, parts, gate_t, tag):
    with ExitStack() as ctx:
        m = Mem(nc, ctx, tag)
        held = m.sb("held", [P, 2, CT, PARTS * E_], bf16)
        ps_g = m.ps("ps_g", [P, 2, 2 * CH], bf16)
        zeroed, picked, turned, copied = (m.sem(s) for s in ("zeroed", "picked", "turned", "copied"))
        nc.all_engine_barrier()
        block = ctx.enter_context(nc.Block())

        @block.gpsimd
        def _(pool):
            pool.memset(gate_t[:, :], 0.0).then_inc(zeroed, 1)
            pool.wait_ge(zeroed, 2)

        @block.vector
        def _(v):
            with v.Fori(0, NCH // 2) as pair:
                for u in range(2):
                    c = pair * 2 + u
                    v.wait_ge(turned, 1 + c)
                    v.tensor_copy(held[:, u, :, :], parts[:, ds(c * CT, CT), :, :].rearrange("p k s e -> p k (s e)")).then_inc(picked, 1)

        @block.tensor
        def _(pe):
            with pe.Fori(0, NCH // 2) as pair:
                for u in range(2):
                    c = pair * 2 + u
                    pe.wait_ge(picked, 1 + c + 1)
                    pe.wait_ge(copied, 1 + c)
                    for k in range(CT):
                        mm = pe.transpose(ps_g[0:PARTS * E_, u, k * P:(k + 1) * P], held[:, u, k, :], g["ident_h"][:, :])
                    mm.then_inc(turned, 1)

        @block.scalar
        def _(act):
            act.wait_ge(zeroed, 2)
            with act.Fori(0, NCH // 2) as pair:
                for u in range(2):
                    c = pair * 2 + u
                    act.wait_ge(turned, 1 + c + 1)
                    act.activation(gate_t[0:PARTS * E_, ds(c * CH, CH)], ps_g[0:PARTS * E_, u, 0:CH], ACT.Copy).then_inc(copied, 1)
            act.wait_ge(copied, 1 + NCH)


LIMIT, ALPHA = 7.0, 1.702


def moe0_weights_stage(nc, g, io, w):
    with ExitStack() as ctx:
        m = Mem(nc, ctx, "m0w")
        up = m.sb("up", [P, E_, 2, P], bf16)
        down = m.sb("down", [P, E_, P], bf16)
        gate = m.sb("gate", [E_, P], bf16)
        b1 = m.sb("b1", [E_, P, 2], bf16)
        ps_w = m.ps("ps_w", [P, 4, E_, P], bf16)
        loaded, b2_loaded, rows_loaded, turned, copied, zeroed = (
            m.sem(s) for s in ("loaded", "b2_loaded", "rows_loaded", "turned", "copied", "zeroed"))
        nc.all_engine_barrier()
        block = ctx.enter_context(nc.Block())

        @block.sync
        def _(sp):
            sp.dma_start(up[:, :, :, :], io["L0_ffn_mlp1_weight"].rearrange("e (i s) h -> i e s h", s=2)).then_inc(loaded, 16)
            sp.dma_start(down[:, :, :], io["L0_ffn_mlp2_weight"].rearrange("e h i -> h e i")).then_inc(loaded, 16)
            sp.dma_start(gate[:, :], io["L0_ffn_gate_weight"]).then_inc(loaded, 16)
            sp.dma_start(b1[:, :, :], io["L0_ffn_mlp1_bias"].rearrange("e (i s) -> e i s", s=2)).then_inc(loaded, 16)
            sp.dma_start(w["norm_w"][:, :], io["L0_ffn_norm_weight"].partition_broadcast(P)).then_inc(rows_loaded, 16)
            sp.dma_start(w["gate_b"][:, :], io["L0_ffn_gate_bias"].partition_broadcast(P)).then_inc(rows_loaded, 16)
            sp.wait_ge(zeroed, 2)
            for s in range(PARTS):
                sp.dma_start(w["b2_rows"][s * E_:(s + 1) * E_, :], io["L0_ffn_mlp2_bias"]).then_inc(b2_loaded, 16)
            sp.wait_ge(b2_loaded, 1 + 16 * PARTS)
            sp.wait_ge(rows_loaded, 33)

        @block.gpsimd
        def _(pool):
            pool.memset(w["b2_rows"][:, :], 0.0).then_inc(zeroed, 1)

        @block.tensor
        def _(pe):
            pe.wait_ge(loaded, 65)
            for s in range(2):
                for e in range(E_):
                    mm = pe.transpose(ps_w[:, s, e, :], up[:, e, s, :], g["ident_h"][:, :])
            for e in range(E_):
                mm = pe.transpose(ps_w[:, 2, e, :], down[:, e, :], g["ident_h"][:, :])
            for s in range(2):
                mm = pe.transpose(ps_w[:, 3, s, 0:E_], b1[:, :, s], g["ident_h"][0:E_, 0:E_])
            mm = pe.transpose(ps_w[:, 3, 2, 0:E_], gate[:, :], g["ident_h"][0:E_, 0:E_])
            mm.then_inc(turned, 1)

        @block.vector
        def _(v):
            v.wait_ge(turned, 2)
            for s in range(2):
                v.tensor_copy(w["up_t"][:, s, :, :], ps_w[:, s, :, :]).then_inc(copied, 1)
                v.tensor_copy(w["b1_t"][:, s, :], ps_w[:, 3, s, 0:E_]).then_inc(copied, 1)
            v.tensor_copy(w["down_t"][:, :, :], ps_w[:, 2, :, :]).then_inc(copied, 1)
            v.tensor_copy(w["gate_w"][:, :], ps_w[:, 3, 2, 0:E_]).then_inc(copied, 1)
            v.wait_ge(copied, 7)


def moe0_norm_stage(nc, g, w, xc, rms_inv):
    with ExitStack() as ctx:
        m = Mem(nc, ctx, "m0n")
        sq = m.sb("sq", [P, TILES, P])
        ss, root = m.sb("ss", [P, TILES]), m.sb("root", [P, TILES])
        normed, squared, mean_ready, rooted, inverted = (m.sem(s) for s in ("normed", "squared", "mean_ready", "rooted", "inverted"))
        nc.all_engine_barrier()
        block = ctx.enter_context(nc.Block())

        @block.vector
        def _(v):
            for t in range(TILES):
                v.tensor_scalar(xc[:, t, :], g["x_tok"][:, t, :], g["mean"][:, t:t + 1], g["rstd"][:, t:t + 1],
                                ALU.subtract, ALU.mult).then_inc(normed, 1)
            v.wait_ge(squared, 1 + TILES)
            v.tensor_scalar(ss[:, :], ss[:, :], 1.0 / P, EPS, ALU.mult, ALU.add).then_inc(mean_ready, 1)
            v.wait_ge(rooted, 2)
            v.reciprocal(rms_inv[:, :], root[:, :]).then_inc(inverted, 1)
            v.wait_ge(inverted, 2)

        @block.scalar
        def _(act):
            for t in range(TILES):
                act.wait_ge(normed, 1 + t + 1)
                act.activation(sq[:, t, :], xc[:, t, :], ACT.Square, accum_out=ss[:, t:t + 1]).then_inc(squared, 1)
            act.wait_ge(mean_ready, 2)
            act.activation(root[:, :], ss[:, :], ACT.Sqrt).then_inc(rooted, 1)


def moe0_route_stage(nc, g, w, xc, rms_inv, nf_t, gate_parts):
    with ExitStack() as ctx:
        m = Mem(nc, ctx, "m0r")
        nf = m.sb("nf", [P, 2, CT, P], bf16)
        nf_c = m.sb("nf_c", [P, 2, CH], bf16)
        logits = m.sb("logits", [P, TILES, E_])
        rounded = m.sb("rounded", [P, TILES, E_], bf16)
        r = route_buffers(m)
        r["step"] = m.sem("route_step")
        ps_t = m.ps("ps_t", [P, 2, 2 * CH], bf16)
        ps_l = m.ps("ps_l", [P, 2, CT, P])
        scaled, turned, t_copied, c_copied, scored, l_copied, diff_ready, weights_ready = (
            m.sem(s) for s in ("scaled", "turned", "t_copied", "c_copied", "scored", "l_copied", "diff_ready", "weights_ready"))
        nc.all_engine_barrier()
        block = ctx.enter_context(nc.Block())

        @block.vector
        def _(v):
            with v.Fori(0, NCH // 2) as pair:
                for u in range(2):
                    c = pair * 2 + u
                    v.wait_ge(turned, 1 + c)
                    for k in range(CT):
                        t = c * CT + k
                        v.scalar_tensor_tensor(nf[:, u, k, :], xc[:, ds(t, 1), :].rearrange("p a e -> p (a e)"), rms_inv[:, ds(t, 1)], w["norm_w"][:, :],
                                               ALU.mult, ALU.mult).then_inc(scaled, 1)
            v.wait_ge(l_copied, 1 + NCH)
            step = Chain(v, r["step"])
            bias = w["gate_b"][:, :].unsqueeze(1).to_broadcast([P, TILES, E_])
            step(v.tensor_tensor(rounded[:, :, :], logits[:, :, :], bias, ALU.add))
            step(v.tensor_copy(logits[:, :, :], rounded[:, :, :]))
            top_two(v, step, r, logits, g)
            v.tensor_tensor(r["first"][:, :], r["v1"][:, :], r["v2"][:, :], ALU.subtract).then_inc(diff_ready, 1)
            v.wait_ge(weights_ready, 3)
            step(v.tensor_tensor(r["gate"][:, :, :], r["sel1"][:, :, :], per_tile(r["w1"]), ALU.mult))
            step(v.tensor_tensor(r["tmp"][:, :, :], r["sel2"][:, :, :], per_tile(r["w2"]), ALU.mult))
            step(v.tensor_tensor(r["gate"][:, :, :], r["gate"][:, :, :], r["tmp"][:, :, :], ALU.add))
            split_gates(v, step, r, gate_parts)

        @block.tensor
        def _(pe):
            def turn_chunk(c, u):
                turn(pe, g["ident_h"], nf, scaled, ps_t, t_copied, turned, c, u)

            def score(c, u):
                pe.wait_ge(t_copied, 1 + c + 1)
                if later_than(c):
                    pe.wait_ge(l_copied, 1 + c - 1)
                for k in range(CT):
                    mm = pe.matmul(ps_l[:, u, k, 0:E_], nf_c[:, u, k * P:(k + 1) * P], w["gate_w"][:, :], start=True, stop=True)
                mm.then_inc(scored, 1)

            chunks_ahead(pe, turn_chunk, score)

        @block.scalar
        def _(act):
            def copy_turned(c, u):
                act.wait_ge(turned, 1 + c + 1)
                if later_than(c):
                    act.wait_ge(scored, 1 + c - 1)
                    act.wait_ge(c_copied, 1 + c - 1)
                act.activation(nf_c[:, u, :], ps_t[:, u, 0:CH], ACT.Copy).then_inc(t_copied, 1)

            def copy_logits(c, u):
                act.wait_ge(scored, 1 + c + 1)
                act.activation(logits[:, ds(c * CT, CT), :], ps_l[:, u, :, 0:E_], ACT.Copy).then_inc(l_copied, 1)

            chunks_ahead(act, copy_turned, copy_logits)
            act.wait_ge(diff_ready, 2)
            act.activation(r["w1"][:, :], r["first"][:, :], ACT.Sigmoid).then_inc(weights_ready, 1)
            act.activation(r["w2"][:, :], r["first"][:, :], ACT.Sigmoid, scale=-1.0).then_inc(weights_ready, 1)

        @block.gpsimd
        def _(pool):
            with pool.Fori(0, NCH // 2) as pair:
                for u in range(2):
                    c = pair * 2 + u
                    pool.wait_ge(t_copied, 1 + c + 1)
                    pool.tensor_copy(nf_t[:, ds(c * CH, CH)], nf_c[:, u, :]).then_inc(c_copied, 1)
            pool.wait_ge(c_copied, 1 + NCH)


def moe0_experts_stage(nc, g, w, xc, nf_t, gate_t):
    with ExitStack() as ctx:
        m = Mem(nc, ctx, "m0e")
        glu0, glu, sig, lin0, lin = (m.sb(n, [P, 2, CH]) for n in ("glu0", "glu", "sig", "lin0", "lin"))
        prod, gated, hid = (m.sb(n, [P, 2, CH]) for n in ("prod", "gated", "hid"))
        comb = m.sb("comb", [P, 2, CH], bf16)
        summed = m.sb("summed", [P, 2, CT, P], bf16)
        ps_up = m.ps("ps_up", [P, 2, 2, CH])
        ps_g = m.ps("ps_g", [P, 2, CH])
        ps_y = m.ps("ps_y", [P, CH])
        ps_c = m.ps("ps_c", [P, 2 * CH], bf16)
        FREE = 2
        biased = m.sem("biased", 2 * FREE)
        lin_ready, sig_ready, prod_ready, gated_ready, hid_ready, down_done = (
            m.sem(s, FREE) for s in ("lin_ready", "sig_ready", "prod_ready", "gated_ready", "hid_ready", "down_done"))
        up_ready, glu_ready, gates_ready, y_ready, comb_ready, turned, sum_ready, y_copied = (
            m.sem(s) for s in ("up_ready", "glu_ready", "gates_ready", "y_ready", "comb_ready", "turned", "sum_ready", "y_copied"))
        STEPS = 2 * E_
        nc.all_engine_barrier()
        block = ctx.enter_context(nc.Block())

        def at(pair, s):
            return pair * STEPS + s, pair * 2 + s // E_, s // E_, s % E_

        @block.tensor
        def _(pe):
            def up(pair, s, half):
                n, c, u, e = at(pair, s)
                pe.wait_ge(biased, 1 + n * 2 + 1 + half)
                pe.matmul(ps_up[:, s % 2, half, :], w["up_t"][:, half, e, :], nf_t[:, ds(c * CH, CH)],
                          start=True, stop=True).then_inc(up_ready, 1)

            def gates(pair, s):
                n, c, u, e = at(pair, s)
                pe.wait_ge(hid_ready, 1 + n + 1)
                pe.matmul(ps_g[:, s % 2, :], w["pick"][:, e, :], gate_t[:, ds(c * CH, CH)], start=True, stop=True).then_inc(gates_ready, 1)

            def down(pair, s):
                n, c, u, e = at(pair, s)
                pe.wait_ge(hid_ready, 1 + FREE + n + 1)
                if e == 0:
                    pe.wait_ge(comb_ready, 1 + c)
                pe.matmul(ps_y[:, :], w["down_t"][:, e, :], hid[:, s % 2, :], start=e == 0, stop=False).then_inc(down_done, 1)
                if e == E_ - 1:
                    pe.matmul(ps_y[:, :], w["b2_rows"][:, :], gate_t[:, ds(c * CH, CH)], start=False, stop=True).then_inc(y_ready, 1)

            def turn(pair, u):
                c = pair * 2 + u
                pe.wait_ge(comb_ready, 1 + c + 1)
                pe.wait_ge(sum_ready, 1 + c)
                for k in range(CT):
                    mm = pe.transpose(ps_c[:, k * P:(k + 1) * P], comb[:, u, k * P:(k + 1) * P], g["ident_h"][:, :])
                mm.then_inc(turned, 1)

            with pe.Fori(0, NCH // 2) as pair:
                up(pair, 0, 0)
                up(pair, 0, 1)
                for s in range(STEPS + 2):
                    if s + 1 < STEPS:
                        up(pair, s + 1, 0)
                        up(pair, s + 1, 1)
                    if s < STEPS:
                        gates(pair, s)
                    if s == E_ + 3:
                        turn(pair, 0)
                    if s >= 2:
                        down(pair, s - 2)
                turn(pair, 1)

        @block.scalar
        def _(act):
            def biases(pair, s):
                n, c, u, e = at(pair, s)
                act.wait_ge(up_ready, 1 + n * 2 + 1)
                act.wait_ge(lin_ready, 1 + n + 1)
                act.activation(glu0[:, s % 2, :], ps_up[:, s % 2, 0, :], ACT.Identity, bias=w["b1_t"][:, 0, e:e + 1]).then_inc(biased, 1)
                act.wait_ge(up_ready, 1 + n * 2 + 2)
                act.activation(lin0[:, s % 2, :], ps_up[:, s % 2, 1, :], ACT.Identity, bias=w["b1_t"][:, 1, e:e + 1]).then_inc(biased, 1)

            def sigmoid(pair, s):
                n, c, u, e = at(pair, s)
                act.wait_ge(glu_ready, 1 + n + 1)
                act.wait_ge(gated_ready, 1 + n + 1)
                act.activation(sig[:, s % 2, :], glu[:, s % 2, :], ACT.Sigmoid, scale=ALPHA).then_inc(sig_ready, 1)

            def combine(pair, u):
                c = pair * 2 + u
                act.wait_ge(y_ready, 1 + c + 1)
                act.wait_ge(turned, 1 + c)
                act.activation(comb[:, u, :], ps_y[:, :], ACT.Copy).then_inc(comb_ready, 1)

            def keep(pair, u):
                c = pair * 2 + u
                act.wait_ge(sum_ready, 1 + c + 1)
                act.activation(g["y_tok"][:, ds(c * CT, CT), :], summed[:, u, :, :], ACT.Copy).then_inc(y_copied, 1)

            with act.Fori(0, NCH // 2) as pair:
                for s in range(STEPS + 1):
                    if s == E_ + 2:
                        combine(pair, 0)
                    if s == E_ + 5:
                        keep(pair, 0)
                    if s < STEPS:
                        biases(pair, s)
                    if s >= 1:
                        sigmoid(pair, s - 1)
                combine(pair, 1)
                keep(pair, 1)

        @block.vector
        def _(v):
            def product(pair, s):
                n, c, u, e = at(pair, s)
                q = s % 2
                v.wait_ge(biased, 1 + 2 * FREE + n * 2 + 1)
                v.wait_ge(sig_ready, 1 + n + 1)
                v.wait_ge(prod_ready, 1 + n + 1)
                v.tensor_scalar(glu[:, q, :], glu0[:, q, :], LIMIT, None, ALU.min).then_inc(glu_ready, 1)
                v.wait_ge(biased, 1 + 2 * FREE + n * 2 + 2)
                v.tensor_scalar(lin[:, q, :], lin0[:, q, :], LIMIT, -LIMIT, ALU.min, ALU.max).then_inc(lin_ready, 1)
                v.wait_ge(glu_ready, 1 + n + 1)
                v.wait_ge(lin_ready, 1 + FREE + n + 1)
                v.wait_ge(gated_ready, 1 + n + 1)
                v.scalar_tensor_tensor(prod[:, q, :], lin[:, q, :], 1.0, glu[:, q, :], ALU.add, ALU.mult).then_inc(prod_ready, 1)

            def hidden(pair, s):
                n, c, u, e = at(pair, s)
                v.wait_ge(gated_ready, 1 + FREE + n + 1)
                v.wait_ge(gates_ready, 1 + n + 1)
                v.wait_ge(down_done, 1 + n + 1)
                v.tensor_tensor(hid[:, s % 2, :], gated[:, s % 2, :], ps_g[:, s % 2, :], ALU.mult).then_inc(hid_ready, 1)

            def add_input(pair, u):
                c = pair * 2 + u
                v.wait_ge(turned, 1 + c + 1)
                v.wait_ge(y_copied, 1 + c)
                v.tensor_tensor(summed[:, u, :, :].rearrange("p k e -> p (k e)"), xc[:, ds(c * CT, CT), :].rearrange("p k e -> p (k e)"),
                                ps_c[:, 0:CH], ALU.add).then_inc(sum_ready, 1)

            with v.Fori(0, NCH // 2) as pair:
                for s in range(STEPS + 2):
                    if s < STEPS:
                        product(pair, s)
                    if s == E_ + 4:
                        add_input(pair, 0)
                    if s >= 2:
                        hidden(pair, s - 2)
                add_input(pair, 1)

        @block.gpsimd
        def _(pool):
            with pool.Fori(0, NCH // 2) as pair:
                for s in range(STEPS):
                    n, c, u, e = at(pair, s)
                    pool.wait_ge(sig_ready, 1 + FREE + n + 1)
                    pool.wait_ge(prod_ready, 1 + FREE + n + 1)
                    pool.wait_ge(hid_ready, 1 + n + 1)
                    pool.tensor_tensor(gated[:, s % 2, :], prod[:, s % 2, :], sig[:, s % 2, :], ALU.mult).then_inc(gated_ready, 1)


WIN = 16
PAD = 16


def attn1_project_stage(nc, g, q_t, k_t, kp_t, v_t, v_rows):
    with ExitStack() as ctx:
        m = Mem(nc, ctx, "a1p")
        norm = m.sb("norm", [P, 2, CT, P])
        norm_t = m.sb("norm_t", [P, 2, CH])
        v_c = m.sb("v_c", [P, 2, CT, P])
        ps_t = m.ps("ps_t", [P, 2, CH])
        ps_p = m.ps("ps_p", [P, 4, CH])
        ps_v = m.ps("ps_v", [P, CT, P])
        normed, turned, t_copied, projected, p_copied, v_ready, v_copied, padded = (
            m.sem(s) for s in ("normed", "turned", "t_copied", "projected", "p_copied", "v_ready", "v_copied", "padded"))
        stored = [m.sem("stored0"), m.sem("stored1")]
        nc.all_engine_barrier()
        block = ctx.enter_context(nc.Block())
        weights = (4, 5, 7, 6)

        @block.vector
        def _(v):
            def norm_chunk(c, u):
                normalise(v, g, norm, normed, turned, c, u)

            def copy_v(c, u):
                v.wait_ge(v_ready, 1 + c + 1)
                v.wait_ge(stored[u], 1 + c // 2 * 16)
                v.tensor_copy(v_c[:, u, :, :], ps_v[:, :, :]).then_inc(v_copied, 1)

            chunks_ahead(v, norm_chunk, copy_v)

        @block.tensor
        def _(pe):
            def turn_chunk(c, u):
                turn(pe, g["ident"], norm, normed, ps_t, t_copied, turned, c, u)

            def project(c, u):
                pe.wait_ge(t_copied, 1 + c + 1)
                for i in range(4):
                    if later_than(c, 1):
                        pe.wait_ge(p_copied, 1 + (c - 1) * 4 + i + 1)
                    pe.matmul(ps_p[:, i, :], g["w_t"][:, weights[i], :], norm_t[:, u, :], start=True, stop=True).then_inc(projected, 1)
                pe.wait_ge(v_copied, 1 + c)
                for k in range(CT):
                    mm = pe.matmul(ps_v[:, k, :], norm_t[:, u, k * P:(k + 1) * P], g["w_t"][:, 6, :], start=True, stop=True)
                mm.then_inc(v_ready, 1)

            chunks_in_turn(pe, turn_chunk, project)

        @block.scalar
        def _(act):
            def copy_turned(c, u):
                act.wait_ge(turned, 1 + c + 1)
                if later_than(c):
                    act.wait_ge(v_ready, 1 + c - 1)
                act.activation(norm_t[:, u, :], ps_t[:, u, :], ACT.Copy).then_inc(t_copied, 1)

            def copy_projected(c, u):
                for i, (dst, pad) in enumerate(((q_t, 0), (k_t, PAD), (kp_t, 0), (v_t, PAD))):
                    act.wait_ge(projected, 1 + c * 4 + i + 1)
                    act.activation(dst[:, ds(c // 2, 1), pad + u * CH:pad + (u + 1) * CH].rearrange("p a t -> p (a t)"),
                                   ps_p[:, i, :], ACT.Copy).then_inc(p_copied, 1)

            chunks_in_turn(act, copy_turned, copy_projected)
            act.wait_ge(p_copied, 1 + 4 * NCH)

        @block.gpsimd
        def _(pool):
            pool.memset(v_t[:, :, 0:PAD], 0.0).then_inc(padded, 1)
            pool.wait_ge(p_copied, 1 + 4 * NCH)
            pool.tensor_copy(k_t[:, :, 0:PAD], k_t[:, :, PAD:PAD + 1].to_broadcast([P, B, PAD])).then_inc(padded, 1)
            pool.wait_ge(padded, 3)

        @block.sync
        def _(sp):
            dst = v_rows.rearrange("(k p) e -> p k e", p=P)
            with sp.Fori(0, B) as b:
                for u in range(2):
                    c = b * 2 + u
                    sp.wait_ge(v_copied, 1 + c + 1)
                    sp.dma_start(dst[:, ds(c * CT, CT), :], v_c[:, u, :, :]).then_inc(stored[u], 16)
            for u in range(2):
                sp.wait_ge(stored[u], 1 + 16 * B)


BLK = 32
GK = 8
BLOCKS = NTOK // BLK
PER_SEQ = T // BLK
GROUPS = [(0, 0, 8), (1, 0, 16), (2, 0, 24), (0, 8, 32), (1, 16, 32), (2, 24, 32)]


def attn1_windows_stage(nc, g, io, q_t, k_t, kp_t, v_t, v_rows, z_t, l_inv):
    with ExitStack() as ctx:
        m = Mem(nc, ctx, "a1w")
        head_mask = m.sb("head_mask", [P, H])
        key_mask = m.sb("key_mask", [P, P])
        m_pick = m.sb("m_pick", [P, P], bf16)
        mask_rows = m.sb("mask_rows", [P, 2, 3, BLK, WIN], bf16)
        max_rows = m.sb("max_rows", [P, 2, BLK], bf16)
        qk = m.sb("qk", [P, 2, BLK, WIN])
        bd_k = m.sb("bd_k", [P, 2, BLK, H])
        v_raw = m.sb("v_raw", [P, 2, 4, P])
        bd_v = m.sb("bd_v", [P, 2, 4, P])
        probs = m.sb("probs", [P, 2, 3, BLK, WIN])
        p_sum = m.sb("p_sum", [P, 2, BLK])
        r_max = m.sb("r_max", [P, 2, BLK])
        max_h = m.sb("max_h", [BLK, H])
        nm = m.sb("nm", [P, 2, H], bf16)
        uv = m.sb("uv", [P, BLK, WIN])
        ps_a = m.ps("ps_a", [P, 2, 3, BLK, WIN])
        ps_u = m.ps("ps_u", [P, BLK, WIN])
        ps_m = m.ps("ps_m", [P, CH])
        ps_max = ps_m[0:BLK, 0:P]
        ps_nm = ps_m[0:BLK, P:P + P // 2].bitcast(bf16)
        ps_l = ps_m[:, 2 * P:2 * P + BLK]
        (const_loaded, zeroed, qk_built, k_built, v_built, prior_done, logits_ready, r_ready, max_turned, max_ready, nm_ready,
         nm_split, nm_turned, rows_ready, max_taken, p_ready, p_summed, v_prior_done, u_ready, l_ready, u_read, l_read, z_ready) = (
            m.sem(s) for s in ("const_loaded", "zeroed", "qk_built", "k_built", "v_built", "prior_done", "logits_ready", "r_ready",
                               "max_turned", "max_ready", "nm_ready", "nm_split", "nm_turned", "rows_ready", "max_taken", "p_ready",
                               "p_summed", "v_prior_done", "u_ready", "l_ready", "u_read", "l_read", "z_ready"))
        v_loaded = [m.sem("v_loaded0"), m.sem("v_loaded1")]
        N_CONST = 4 * 16
        N_ZERO = 4
        PAIRS = BLOCKS // 2
        nc.all_engine_barrier()
        block = ctx.enter_context(nc.Block())

        def at(i, u, k=0):
            i, p = i + (u + k) // 2, (u + k) % 2
            half = PER_SEQ // 2
            later = 1 if p else ((i % half) + half - 1) // half
            return i * 2 + p, p, i, i // half, (i % half) * 2 * BLK + p * BLK, later

        def pairs(eng, step):
            for u in range(2):
                step(0, u, u > 0, True, True)
            with eng.Fori(1, PAIRS - 1) as i:
                for u in range(2):
                    step(i, u, True, True, True)
            for u in range(2):
                step(PAIRS - 1, u, True, u == 0, False)

        @block.sync
        def _(sp):
            sp.dma_start(head_mask[:, :], io["head_mask"]).then_inc(const_loaded, 16)
            sp.dma_start(key_mask[:, :], io["key_mask"]).then_inc(const_loaded, 16)
            sp.dma_start(m_pick[:, :], io["m_pick"]).then_inc(const_loaded, 16)
            sp.dma_start(mask_rows[:, :, :, :, :].rearrange("p a b c d -> p a (b c d)"), io["window_rows"]).then_inc(const_loaded, 16)

            def load(i, u):
                n, p, i, b, s0, _ = at(i, u)
                if later_than(n):
                    sp.wait_ge(v_built, 1 + n - 1)
                rows = v_rows[ds(n * BLK, BLK), :]
                for k in range(GK):
                    src = bass.AP(rows.tensor, rows.offset + k * P, [[0, H], [GK * P, 4], [1, P]])
                    sp.dma_start(v_raw[k * H:(k + 1) * H, p, :, :], src).then_inc(v_loaded[p], 16)

            for u in range(2):
                load(0, u)
            with sp.Fori(1, PAIRS) as i:
                for u in range(2):
                    load(i, u)

        @block.gpsimd
        def _(pool):
            pool.memset(max_rows[:, :, :], 0.0).then_inc(zeroed, 1)
            pool.memset(bd_k[:, :, :, :], 0.0).then_inc(zeroed, 1)
            pool.memset(bd_v[:, :, :, :], 0.0).then_inc(zeroed, 1)
            pool.memset(nm[:, :, :], 0.0).then_inc(zeroed, 1)
            pool.wait_ge(const_loaded, 1 + N_CONST)
            pool.wait_ge(zeroed, 1 + N_ZERO)

            def build_keys(i, u, k=0, first=False):
                n, p, i, b, s0, _ = at(i, u, k)
                if not first:
                    pool.wait_ge(prior_done, 1 + n)
                keys = kp_t[:, ds(b, 1), ds(s0, BLK)].rearrange("p a t -> p (a t)").unsqueeze(2).to_broadcast([P, BLK, H])
                pool.tensor_tensor(bd_k[:, p, :, :], keys, head_mask[:, :].unsqueeze(1).to_broadcast([P, BLK, H]), ALU.mult).then_inc(k_built, 1)
                if later_than(n):
                    pool.wait_ge(logits_ready, 1 + n - 1)
                queries = q_t[:, ds(b, 1), ds(s0, BLK)].rearrange("p a t -> p (a t)").unsqueeze(2).to_broadcast([P, BLK, WIN])
                window = view(k_t[:, ds(b, 1), ds(s0 + PAD - WIN + 1, 1)], [[1, BLK], [1, WIN]])
                pool.tensor_tensor(qk[:, p, :, :], queries, window, ALU.mult).then_inc(qk_built, 1)

            def build_values(i, u, first=False):
                n, p, i, b, s0, _ = at(i, u)
                pool.wait_ge(v_loaded[p], 1 + (i + 1) * 16 * GK)
                if not first:
                    pool.wait_ge(v_prior_done, 1 + n)
                pool.tensor_tensor(bd_v[:, p, :, :], v_raw[:, p, :, :], key_mask[:, :].unsqueeze(1).to_broadcast([P, 4, P]), ALU.mult).then_inc(v_built, 1)

            build_keys(0, 0, 0, True)
            build_keys(0, 1)

            def step(i, u, prev, ahead, ahead2):
                build_values(i, u, not prev)
                if ahead2:
                    build_keys(i, u, 2)

            pairs(pool, step)

        @block.tensor
        def _(pe):
            def group_keys(ring, p, q):
                return ring[:, p, q - 2] if q >= 2 else ring[:, 1 - p, q + 2]

            k_ring = bd_k[:, :, :, :].rearrange("p a (q k) h -> p a q (k h)", q=4)

            def masks(i, u, k):
                n, p, _, _, _, later = at(i, u, k)
                if later_than(n):
                    pe.wait_ge(p_ready, 1 + n - 1)
                for slot in range(3):
                    rows = mask_rows[:, ds(later, 1), slot, :, :].rearrange("p a s j -> p (a s) j")
                    pe.matmul(ps_a[:, p, slot, :, :], m_pick[:, :], rows, start=True, stop=False, skip_group_check=True)

            def logits(i, u, k, groups):
                n, p, _, _, _, _ = at(i, u, k)
                if 0 in groups:
                    pe.wait_ge(k_built, 1 + n + 1)
                    pe.wait_ge(qk_built, 1 + n + 1)
                for q in groups:
                    slot, lo, hi = GROUPS[q]
                    mm = pe.matmul(ps_a[:, p, slot, lo:hi, :], group_keys(k_ring, p, q), qk[:, p, lo:hi, :],
                                   start=False, stop=False, skip_group_check=True)
                    if q == 1:
                        mm.then_inc(prior_done, 1)
                    if q == 5:
                        mm.then_inc(logits_ready, 1)

            def turn_max(i, u):
                n, p, _, _, _, _ = at(i, u)
                pe.wait_ge(r_ready, 1 + n + 1)
                if later_than(n):
                    pe.wait_ge(l_read, 1 + n - 1)
                pe.transpose(ps_max, r_max[:, p, :], g["ident"][:, :]).then_inc(max_turned, 1)

            def turn_back(i, u):
                n, _, _, _, _, _ = at(i, u)
                pe.wait_ge(nm_ready, 1 + n + 1)
                pe.transpose(ps_nm, nm[:, :, :].rearrange("p a h -> p (a h)"), g["ident_h"][:, :]).then_inc(nm_turned, 1)

            def add_max(i, u):
                n, p, _, _, _, _ = at(i, u)
                pe.wait_ge(rows_ready, 1 + n + 1)
                rows = max_rows[:, p, :].unsqueeze(2).to_broadcast([P, BLK, WIN])
                for slot in range(3):
                    mm = pe.matmul(ps_a[:, p, slot, :, :], m_pick[:, :], rows, start=False, stop=True, skip_group_check=True)
                mm.then_inc(max_taken, 1)

            def times_v(i, u, k, groups):
                n, p, _, _, _, _ = at(i, u, k)
                if 2 in groups:
                    pe.wait_ge(v_built, 1 + n + 1)
                    pe.wait_ge(p_ready, 1 + n + 1)
                    pe.wait_ge(u_read, 1 + n)
                for q in groups:
                    slot, lo, hi = GROUPS[q]
                    mm = pe.matmul(ps_u[:, lo:hi, :], group_keys(bd_v, p, q), probs[:, p, slot, lo:hi, :],
                                   start=q == 2, stop=q == 4, skip_group_check=True)
                    if q == 1:
                        mm.then_inc(v_prior_done, 1)
                    if q == 4:
                        mm.then_inc(u_ready, 1)

            def sums(i, u, k=0):
                n, p, _, _, _, _ = at(i, u, k)
                pe.wait_ge(p_summed, 1 + n + 1)
                pe.matmul(ps_l, key_mask[:, :], p_sum[:, p, :], start=True, stop=True).then_inc(l_ready, 1)

            pe.wait_ge(const_loaded, 1 + N_CONST)
            pe.wait_ge(zeroed, 1 + N_ZERO)
            masks(0, 0, 0)
            logits(0, 0, 0, range(6))

            def step(i, u, prev, ahead, ahead2):
                if prev:
                    times_v(i, u, -1, (2, 5, 0, 1, 3))
                turn_max(i, u)
                if prev:
                    times_v(i, u, -1, (4,))
                if ahead:
                    masks(i, u, 1)
                turn_back(i, u)
                if ahead:
                    logits(i, u, 1, (0, 1))
                add_max(i, u)
                if ahead:
                    logits(i, u, 1, (2, 3))
                if prev:
                    sums(i, u, -1)
                if ahead:
                    logits(i, u, 1, (4, 5))

            pairs(pe, step)
            times_v(PAIRS - 1, 1, 0, (2, 5, 0, 1, 3, 4))
            sums(PAIRS - 1, 1)

        @block.vector
        def _(v):
            def finish(i, u, k):
                n, p, _, b, s0, _ = at(i, u, k)
                window = view(v_t[:, ds(b, 1), ds(s0 + PAD - WIN + 1, 1)], [[1, BLK], [1, WIN]])
                v.wait_ge(u_ready, 1 + n + 1)
                v.wait_ge(z_ready, 1 + n)
                v.tensor_tensor(uv[:, :, :], ps_u[:, :, :], window, ALU.mult).then_inc(u_read, 1)
                v.wait_ge(u_read, 1 + n + 1)
                v.tensor_reduce(z_t[:, ds(n * BLK, BLK)], uv[:, :, :], AX.X, ALU.add).then_inc(z_ready, 1)
                v.wait_ge(l_ready, 1 + n + 1)
                v.reciprocal(l_inv[:, ds(n * BLK, BLK)], ps_l).then_inc(l_read, 1)

            def sum_pairs(i, u, k):
                n, p, _, _, _, _ = at(i, u, k)
                v.wait_ge(p_ready, 1 + n + 1)
                if later_than(n):
                    v.wait_ge(l_ready, 1 + n - 1)
                v.tensor_reduce(p_sum[:, p, :], probs[:, p, :, :, :].rearrange("p a s j -> p s a j"), AX.XY, ALU.add).then_inc(p_summed, 1)

            def negate(i, u):
                n, _, _, _, _, _ = at(i, u)
                v.wait_ge(max_turned, 1 + n + 1)
                v.tensor_reduce(max_h[:, :], ps_max.rearrange("s (k h) -> s h k", h=H), AX.X, ALU.max).then_inc(max_ready, 1)
                v.wait_ge(nm_turned, 1 + n)
                v.wait_ge(max_ready, 1 + n + 1)
                v.tensor_scalar(nm[0:BLK, 0, :], max_h[:, :], -1.0, None, ALU.mult).then_inc(nm_split, 1)
                v.wait_ge(nm_split, 1 + n + 1)
                v.scalar_tensor_tensor(nm[0:BLK, 1, :], max_h[:, :], -1.0, nm[0:BLK, 0, :], ALU.mult, ALU.subtract).then_inc(nm_ready, 1)

            def maximum(i, u, k=0):
                n, p, _, _, _, _ = at(i, u, k)
                v.wait_ge(logits_ready, 1 + n + 1)
                if later_than(n):
                    v.wait_ge(max_turned, 1 + n - 1)
                v.tensor_reduce(r_max[:, p, :], ps_a[:, p, :, :, :].rearrange("p a s j -> p s a j"), AX.XY, ALU.max).then_inc(r_ready, 1)

            v.wait_ge(zeroed, 1 + N_ZERO)

            def step(i, u, prev, ahead, ahead2):
                maximum(i, u)
                negate(i, u)
                if prev:
                    sum_pairs(i, u, -1)
                    finish(i, u, -1)

            pairs(v, step)
            sum_pairs(PAIRS - 1, 1, 0)
            finish(PAIRS - 1, 1, 0)
            v.wait_ge(z_ready, 1 + BLOCKS)
            v.wait_ge(l_read, 1 + BLOCKS)

        @block.scalar
        def _(act):
            act.wait_ge(zeroed, 1 + N_ZERO)

            def step(i, u, prev, ahead, ahead2):
                n, p, _, _, _, _ = at(i, u)
                act.wait_ge(nm_turned, 1 + n + 1)
                if later_than(n):
                    act.wait_ge(max_taken, 1 + n - 1)
                act.activation(max_rows[0:BLK, p, :], ps_nm[:, 0:BLK], ACT.Copy).then_inc(rows_ready, 1)
                if later_than(n):
                    act.wait_ge(u_ready, 1 + n - 1)
                    act.wait_ge(p_summed, 1 + n - 1)
                act.wait_ge(max_taken, 1 + n + 1)
                act.activation(probs[:, p, :, :, :], ps_a[:, p, :, :, :], ACT.Exp).then_inc(p_ready, 1)

            pairs(act, step)


def attn1_output_stage(nc, g, io, z_t, l_inv):
    with ExitStack() as ctx:
        m = Mem(nc, ctx, "a1o")
        s = stats_buffers(m)
        z_c = m.sb("z_c", [P, 2, CH])
        norm = m.sb("norm", [P, 2, CT, P])
        gamma, beta = m.sb("gamma", [P, P]), m.sb("beta", [P, P])
        y_mean, y_rstd, y_shift = m.sb("y_mean", [P, TILES]), m.sb("y_rstd", [P, TILES]), m.sb("y_shift", [P, TILES])
        ps_y = m.ps("ps_y", [P, 2, CT, P])
        loaded, picked, projected, normed, added, shift_ready, scaled = (
            m.sem(x) for x in ("loaded", "picked", "projected", "normed", "added", "shift_ready", "scaled"))
        y_normed = [m.sem("y_normed_by_vector"), m.sem("y_normed_by_scalar")]
        shifted = [m.sem("shifted_by_vector"), m.sem("shifted_by_pool")]
        y = g["y_tok"]

        def shift(eng, c):
            yc = y[:, c * CT:(c + 1) * CT, :]
            eng.tensor_tensor(yc, yc, beta[:, :].unsqueeze(1).to_broadcast([P, CT, P]), ALU.add).then_inc(shifted[c % 2], 1)

        nc.all_engine_barrier()
        block = ctx.enter_context(nc.Block())

        @block.sync
        def _(sp):
            sp.dma_start(gamma[:, :], io["L1_attn_gamma"].partition_broadcast(P)).then_inc(loaded, 16)
            sp.dma_start(beta[:, :], io["L1_attn_beta"].partition_broadcast(P)).then_inc(loaded, 16)
            sp.wait_ge(loaded, 33)

        @block.scalar
        def _(act):
            scalar_stats(act, s, 0)
            act.wait_ge(shift_ready, 2)
            for c in range(1, NCH, 2):
                for t in range(c * CT, (c + 1) * CT):
                    act.activation(y[:, t, :], y[:, t, :], ACT.Identity, bias=y_shift[:, t:t + 1], scale=y_rstd[:, t:t + 1]).then_inc(y_normed[1], 1)

        @block.tensor
        def _(pe):
            with pe.Fori(0, NCH // 2) as pair:
                for u in range(2):
                    c = pair * 2 + u
                    pe.wait_ge(picked, 1 + c + 1)
                    pe.wait_ge(added, 1 + c)
                    for k in range(CT):
                        mm = pe.matmul(ps_y[:, u, k, :], z_c[:, u, k * P:(k + 1) * P], g["w_t"][:, 8, :], start=True, stop=True)
                    mm.then_inc(projected, 1)

        @block.vector
        def _(v):
            with v.Fori(0, NCH // 2) as pair:
                for u in range(2):
                    c = pair * 2 + u
                    for k in range(CT):
                        t = c * CT + k
                        v.tensor_scalar(norm[:, u, k, :], g["x_tok"][:, ds(t, 1), :], g["mean"][:, ds(t, 1)], g["rstd"][:, ds(t, 1)],
                                        ALU.subtract, ALU.mult).then_inc(normed, 1)
                    v.wait_ge(normed, 1 + c * CT + CT)
                    v.wait_ge(projected, 1 + c + 1)
                    v.tensor_tensor(y[:, ds(c * CT, CT), :], ps_y[:, u, :, :], norm[:, u, :, :], ALU.add).then_inc(added, 1)
            v.wait_ge(added, 1 + NCH)
            raw_stats(v, y, s, range(TILES))
            vector_stats(v, s, y_mean, y_rstd, 0)
            v.scalar_tensor_tensor(y_shift[:, :], y_mean[:, :], -1.0, y_rstd[:, :], ALU.mult, ALU.mult).then_inc(shift_ready, 1)
            v.wait_ge(loaded, 33)
            for c in range(0, NCH, 2):
                for t in range(c * CT, (c + 1) * CT):
                    v.tensor_scalar(y[:, t, :], y[:, t, :], y_mean[:, t:t + 1], y_rstd[:, t:t + 1],
                                    ALU.subtract, ALU.mult).then_inc(y_normed[0], 1)
            for c in range(NCH):
                v.wait_ge(y_normed[c % 2], 1 + (c // 2 + 1) * CT)
                yc = y[:, c * CT:(c + 1) * CT, :]
                v.tensor_tensor(yc, yc, gamma[:, :].unsqueeze(1).to_broadcast([P, CT, P]), ALU.mult).then_inc(scaled, 1)
                if c % 2 == 0:
                    v.wait_ge(scaled, 1 + c + 1)
                    shift(v, c)

        @block.gpsimd
        def _(pool):
            with pool.Fori(0, NCH // 2) as pair:
                for u in range(2):
                    c = pair * 2 + u
                    pool.wait_ge(projected, 1 + c)
                    pool.tensor_tensor(z_c[:, u, :], z_t[:, ds(c * CH, CH)], l_inv[:, ds(c * CH, CH)], ALU.mult).then_inc(picked, 1)
            pool.wait_ge(loaded, 33)
            for c in range(1, NCH, 2):
                pool.wait_ge(scaled, 1 + c + 1)
                shift(pool, c)
            for done in shifted:
                pool.wait_ge(done, 1 + NCH // 2)


F1 = 512
FB = F1 // P
SHARED = E_
EXPERTS = E_ + 1


WEIGHT_LOADS, ZERO_LOADS = 6, 9


def start_moe1_loads(sp, io, w, weights_loaded):
    for dst, name in ((w["w1"], "w1"), (w["w3"], "w3")):
        sp.dma_start(dst[:, 0:E_, :], io[f"L1_ffn_{name}_e"].rearrange("e d f -> d e f")).then_inc(weights_loaded, 16)
        shared = dst[:, SHARED, :].rearrange("d (n f) -> d n f", n=E_)
        sp.dma_start(shared, io[f"L1_ffn_{name}_s"].rearrange("n d f -> d n f")).then_inc(weights_loaded, 16)


def clear_slots(sp, zeros, sorted_x, zero_done):
    rows = sorted_x.rearrange("(n p r) d -> n p (r d)", n=ZERO_LOADS, p=P)
    for n in range(ZERO_LOADS):
        sp.dma_start(rows[n], zeros[:, :]).then_inc(zero_done, 16)


def moe1_weights_stage(nc, g, io, w, weights_loaded, zeros, sorted_x, zero_done):
    with ExitStack() as ctx:
        m = Mem(nc, ctx, "m1w")
        gate = m.sb("gate", [P, P])
        ps_w = m.ps("ps_w", [P, P])
        gate_loaded, zeroed, turned, copied = (m.sem(s) for s in ("gate_loaded", "zeroed", "turned", "copied"))
        nc.all_engine_barrier()
        block = ctx.enter_context(nc.Block())

        @block.sync
        def _(sp):
            sp.wait_ge(zeroed, 3)
            sp.dma_start(gate[0:E_, :], io["L1_ffn_gate_W"]).then_inc(gate_loaded, 16)
            clear_slots(sp, zeros, sorted_x, zero_done)
            sp.dma_start(w["w2"][:, 0:E_, :, :].rearrange("p e b d -> p (e b) d"),
                         io["L1_ffn_w2_e"].rearrange("e (b p) d -> p (e b) d", p=P)).then_inc(weights_loaded, 16)
            sp.dma_start(w["w2"][:, SHARED, :, :],
                         io["L1_ffn_w2_s"].rearrange("n f d -> (n f) d").rearrange("(b p) d -> p b d", p=P)).then_inc(weights_loaded, 16)

        @block.gpsimd
        def _(pool):
            pool.memset(gate[:, :], 0.0).then_inc(zeroed, 1)
            pool.memset(zeros[:, :], 0.0).then_inc(zeroed, 1)

        @block.tensor
        def _(pe):
            pe.wait_ge(gate_loaded, 17)
            pe.matmul(ps_w[:, :], gate[:, :], g["ident"][:, :], start=True, stop=True).then_inc(turned, 1)

        @block.vector
        def _(v):
            v.wait_ge(turned, 2)
            v.tensor_copy(w["gate_w"][:, :], ps_w[:, :]).then_inc(copied, 1)
            v.wait_ge(copied, 2)


def moe1_route_stage(nc, g, w, r, x_t):
    with ExitStack() as ctx:
        m = Mem(nc, ctx, "m1r")
        norm = g["y_tok"]
        x_c = m.sb("x_c", [P, 2, CH])
        logits = m.sb("logits", [P, TILES, E_])
        exps = m.sb("exps", [P, TILES, E_])
        r["step"] = m.sem("route_step")
        ps_t = m.ps("ps_t", [P, 2, CH])
        ps_l = m.ps("ps_l", [P, 2, CT, P])
        normed, turned, t_copied, c_copied, scored, l_copied, exps_ready = (
            m.sem(s) for s in ("normed", "turned", "t_copied", "c_copied", "scored", "l_copied", "exps_ready"))
        nc.all_engine_barrier()
        block = ctx.enter_context(nc.Block())

        @block.vector
        def _(v):
            for t in range(TILES):
                v.tensor_scalar(norm[:, t, :], g["x_tok"][:, t, :], g["mean"][:, t:t + 1], g["rstd"][:, t:t + 1],
                                ALU.subtract, ALU.mult).then_inc(normed, 1)
            v.wait_ge(l_copied, 1 + NCH)
            step = Chain(v, r["step"])
            step(v.reduce_max(r["v1"][:, :], logits[:, :, :], AX.X))
            step(v.tensor_tensor(logits[:, :, :], logits[:, :, :], per_tile(r["v1"]), ALU.subtract))
            v.wait_ge(exps_ready, 2)
            step(v.tensor_reduce(r["w1"][:, :], exps[:, :, :], AX.X, ALU.add))
            step(v.reciprocal(r["w2"][:, :], r["w1"][:, :]))
            step(v.tensor_tensor(logits[:, :, :], exps[:, :, :], per_tile(r["w2"]), ALU.mult))
            top_two(v, step, r, logits, g)
            for gate in ("v1", "v2"):
                step(v.tensor_scalar(r[gate][:, :], r[gate][:, :], 0.5, None, ALU.mult))

        @block.tensor
        def _(pe):
            def turn_chunk(c, u):
                pe.wait_ge(normed, 1 + c * CT + CT)
                if c >= 2:
                    pe.wait_ge(t_copied, 1 + c - 1)
                for k in range(CT):
                    mm = pe.transpose(ps_t[:, u, k * P:(k + 1) * P], norm[:, c * CT + k, :], g["ident"][:, :])
                mm.then_inc(turned, 1)

            def score(c, u):
                pe.wait_ge(t_copied, 1 + c + 1)
                if later_than(c):
                    pe.wait_ge(l_copied, 1 + c - 1)
                for k in range(CT):
                    mm = pe.matmul(ps_l[:, u, k, :], x_c[:, u, k * P:(k + 1) * P], w["gate_w"][:, :], start=True, stop=True)
                mm.then_inc(scored, 1)

            turn_chunk(0, 0)
            for c in range(NCH):
                if c + 1 < NCH:
                    turn_chunk(c + 1, (c + 1) % 2)
                score(c, c % 2)

        @block.scalar
        def _(act):
            def copy_turned(c, u):
                act.wait_ge(turned, 1 + c + 1)
                if later_than(c):
                    act.wait_ge(scored, 1 + c - 1)
                    act.wait_ge(c_copied, 1 + c - 1)
                act.activation(x_c[:, u, :], ps_t[:, u, :], ACT.Copy).then_inc(t_copied, 1)

            def copy_logits(c, u):
                act.wait_ge(scored, 1 + c + 1)
                act.activation(logits[:, ds(c * CT, CT), :], ps_l[:, u, :, 0:E_], ACT.Copy).then_inc(l_copied, 1)

            chunks_ahead(act, copy_turned, copy_logits)
            act.wait_ge(r["step"], 3)
            act.activation(exps[:, :, :], logits[:, :, :], ACT.Exp).then_inc(exps_ready, 1)

        @block.gpsimd
        def _(pool):
            with pool.Fori(0, NCH // 2) as pair:
                for u in range(2):
                    c = pair * 2 + u
                    pool.wait_ge(t_copied, 1 + c + 1)
                    pool.tensor_copy(x_t[:, ds(c * CH, CH)], x_c[:, u, :]).then_inc(c_copied, 1)
            pool.wait_ge(c_copied, 1 + NCH)


SLOT_TILES = 2 * TILES + E_
SLOTS = SLOT_TILES * P


def moe1_sort_stage(nc, g, r, slots, tile_expert):
    with ExitStack() as ctx:
        m = Mem(nc, ctx, "m1s")
        int32 = mybir.dt.int32
        count_i, count = m.sb("count_i", [P, SLOT_TILES], int32), m.sb("count", [P, SLOT_TILES])
        earlier, ones = m.sb("earlier", [P, P], bf16), m.sb("ones", [P, P], bf16)
        both = m.sb("both", [P, TILES, E_], bf16)
        total, tiles, base, end = (m.sb(n, [P, E_]) for n in ("total", "tiles", "base", "end"))
        over = m.sb("over", [P, E_, TILES])
        before = m.sb("before", [P, E_, E_])
        passed = m.sb("passed", [P, SLOT_TILES, E_])
        expert = m.sb("expert", [P, SLOT_TILES])
        start = m.sb("start", [P, E_])
        slot = m.sb("slot", [P, TILES, E_])
        picked = m.sb("picked", [P, TILES, E_])
        which = m.sb("which", [P, TILES])
        ps_rank = m.ps("ps_rank", [P, TILES, E_])
        ps_count = m.ps("ps_count", [P, TILES, E_])
        consts, both_ready, counted, v_step = (m.sem(s) for s in ("consts", "both_ready", "counted", "v_step"))
        nc.all_engine_barrier()
        block = ctx.enter_context(nc.Block())

        @block.gpsimd
        def _(pool):
            pool.iota(count_i[:, :], pattern=[[1, SLOT_TILES]], base=0, channel_multiplier=0).then_inc(consts, 1)
            pool.memset(ones[:, :], 1.0).then_inc(consts, 1)
            pool.memset(earlier[:, :], 1.0).then_inc(consts, 1)
            pool.wait_ge(consts, 4)
            pool.tensor_copy(count[:, :], count_i[:, :]).then_inc(consts, 1)
            pool.affine_select(out=earlier[:, :], in_=earlier[:, :], compare_op=ALU.is_ge, fill=0.0,
                               base=-1, pattern=[[1, P]], channel_multiplier=-1).then_inc(consts, 1)

        @block.tensor
        def _(pe):
            pe.wait_ge(consts, 6)
            pe.wait_ge(both_ready, 2)
            pe.matmul(ps_rank[:, :, :], earlier[:, :], both[:, :, :], start=True, stop=False, skip_group_check=True)
            for s in range(1, TILES):
                pe.matmul(ps_rank[:, s:, :], ones[:, :], both[:, :TILES - s, :], start=False, stop=s == TILES - 1, skip_group_check=True)
            pe.matmul(ps_count[:, :, :], ones[:, :], both[:, :, :], start=True, stop=True).then_inc(counted, 1)

        @block.vector
        def _(v):
            step = Chain(v, v_step)
            v.tensor_tensor(both[:, :, :], r["sel1"][:, :, :], r["sel2"][:, :, :], ALU.add).then_inc(both_ready, 1)
            v.wait_ge(consts, 6)
            v.wait_ge(counted, 2)
            step(v.tensor_reduce(total[:, :], ps_count[:, :, :].rearrange("p t e -> p e t"), AX.X, ALU.add))
            step(v.tensor_scalar(total[:, :], total[:, :], 1.0 / P, None, ALU.mult))
            step(v.tensor_tensor(over[:, :, :], total[:, :].unsqueeze(2).to_broadcast([P, E_, TILES]),
                                 count[:, 0:TILES].unsqueeze(1).to_broadcast([P, E_, TILES]), ALU.is_gt))
            step(v.tensor_reduce(tiles[:, :], over[:, :, :], AX.X, ALU.add))
            step(v.tensor_tensor(before[:, :, :], g["place"][:, :].unsqueeze(1).to_broadcast([P, E_, E_]),
                                 g["place"][:, :].unsqueeze(2).to_broadcast([P, E_, E_]), ALU.is_lt))
            step(v.tensor_tensor(before[:, :, :], before[:, :, :], tiles[:, :].unsqueeze(1).to_broadcast([P, E_, E_]), ALU.mult))
            step(v.tensor_reduce(base[:, :], before[:, :, :], AX.X, ALU.add))
            step(v.tensor_tensor(end[:, :], base[:, :], tiles[:, :], ALU.add))
            step(v.tensor_tensor(passed[:, :, :], count[:, :].unsqueeze(2).to_broadcast([P, SLOT_TILES, E_]),
                                 end[:, :].unsqueeze(1).to_broadcast([P, SLOT_TILES, E_]), ALU.is_ge))
            step(v.tensor_reduce(expert[:, :], passed[:, :, :], AX.X, ALU.add))
            step(v.tensor_scalar(tile_expert[:, :], expert[:, :], E_ - 1.0, None, ALU.min))
            step(v.tensor_scalar(start[:, :], base[:, :], float(P), None, ALU.mult))
            step(v.tensor_tensor(slot[:, :, :], ps_rank[:, :, :], start[:, :].unsqueeze(1).to_broadcast([P, TILES, E_]), ALU.add))
            for sel, out in (("sel1", slots[0]), ("sel2", slots[1])):
                step(v.tensor_tensor(picked[:, :, :], slot[:, :, :], r[sel][:, :, :], ALU.mult))
                step(v.tensor_reduce(which[:, :], picked[:, :, :], AX.X, ALU.add))
                step(v.tensor_copy(out[:, :], which[:, :]))


def moe1_shared_stage(nc, g, w, weights_loaded, x_t, slots, sorted_x, zero_done, shared):
    with ExitStack() as ctx:
        m = Mem(nc, ctx, "m1c")
        silu, hid = m.sb("silu", [P, 2, CH]), m.sb("hid", [P, 2, CH])
        mixed = m.sb("mixed", [P, 2, CH])
        ps_h = m.ps("ps_h", [P, 2, 2, CH])
        ps_y = m.ps("ps_y", [P, 2, CH])
        ps_t = m.ps("ps_t", [P, CH])
        hid_ready = m.sem("hid_ready", 2)
        h_ready, silu_ready, down_done, mixed_ready, turned, y_copied = (
            m.sem(s) for s in ("h_ready", "silu_ready", "down_done", "mixed_ready", "turned", "y_copied"))
        sent = m.pool_dma_sem("sent")
        nc.all_engine_barrier()
        block = ctx.enter_context(nc.Block())

        def chunks(eng, body):
            with eng.Fori(0, NCH // 2) as pair:
                for u in range(2):
                    body(pair * 2 + u, u)

        @block.gpsimd
        def _(pool):
            pool.wait_ge(zero_done, 1 + ZERO_LOADS * 16)
            for k in range(2):
                for t in range(TILES):
                    pool.indirect_dma_start(out=sorted_x, out_offset=bass.IndirectOffsetOnAxis(ap=slots[k][:, t:t + 1], axis=0),
                                            in_=g["y_tok"][:, t, :], in_offset=None).then_inc(sent, 16)
            pool.wait_ge(sent, 2 * TILES * 16)

        @block.tensor
        def _(pe):
            def up(c, u, n):
                pe.wait_ge(hid_ready, 1 + c * FB + n + 1)
                for s, name in ((0, "w1"), (1, "w3")):
                    pe.matmul(ps_h[:, n % 2, s, :], w[name][:, SHARED, n * P:(n + 1) * P], x_t[:, ds(c * CH, CH)],
                              start=True, stop=True).then_inc(h_ready, 1)

            def down(c, u, n):
                pe.wait_ge(hid_ready, 1 + c * FB + n + 3)
                if n == 0:
                    if u == 0:
                        pe.wait_ge(mixed_ready, 1 + c)
                pe.matmul(ps_y[:, u, :], w["w2"][:, SHARED, n, :], hid[:, n % 2, :], start=n == 0, stop=n == FB - 1).then_inc(down_done, 1)

            def chunk(c, u):
                up(c, u, 0)
                for n in range(FB):
                    if n + 1 < FB:
                        up(c, u, n + 1)
                    down(c, u, n)
                pe.wait_ge(mixed_ready, 1 + c + 1)
                pe.wait_ge(y_copied, 1 + c)
                for k in range(CT):
                    mm = pe.transpose(ps_t[:, k * P:(k + 1) * P], mixed[:, u, k * P:(k + 1) * P], g["ident"][:, :])
                mm.then_inc(turned, 1)

            pe.wait_ge(weights_loaded, 1 + WEIGHT_LOADS * 16)
            chunks(pe, chunk)

        @block.scalar
        def _(act):
            def chunk(c, u):
                for n in range(FB):
                    act.wait_ge(h_ready, 1 + (c * FB + n) * 2 + 1)
                    act.wait_ge(hid_ready, 1 + c * FB + n + 1)
                    act.activation(silu[:, n % 2, :], ps_h[:, n % 2, 0, :], ACT.Silu).then_inc(silu_ready, 1)
                act.wait_ge(turned, 1 + c + 1)
                act.activation(shared[:, ds(c * CT, CT), :], ps_t[:, :].rearrange("p (k e) -> p k e", k=CT), ACT.Copy).then_inc(y_copied, 1)

            chunks(act, chunk)

        @block.vector
        def _(v):
            def chunk(c, u):
                for n in range(FB):
                    v.wait_ge(silu_ready, 1 + c * FB + n + 1)
                    v.wait_ge(h_ready, 1 + (c * FB + n) * 2 + 2)
                    if n < 2:
                        v.wait_ge(down_done, 1 + c * FB)
                    else:
                        v.wait_ge(down_done, 1 + c * FB + n - 1)
                    v.tensor_tensor(hid[:, n % 2, :], silu[:, n % 2, :], ps_h[:, n % 2, 1, :], ALU.mult).then_inc(hid_ready, 1)
                v.wait_ge(down_done, 1 + (c + 1) * FB)
                v.wait_ge(turned, 1 + c)
                v.tensor_scalar(mixed[:, u, :], ps_y[:, u, :], 0.5 / E_, None, ALU.mult).then_inc(mixed_ready, 1)

            chunks(v, chunk)


def moe1_experts_stage(nc, g, w, tile_expert, sorted_x, sorted_y):
    with ExitStack() as ctx:
        m = Mem(nc, ctx, "m1e")
        x_in, x_c = m.sb("x_in", [P, 4, P]), m.sb("x_c", [P, 2, P])
        silu, hid = m.sb("silu", [P, 2, F1]), m.sb("hid", [P, 2, F1])
        hid_c = m.sb("hid_c", [P, 2, F1])
        y_out = m.sb("y_out", [P, 2, P])
        ps_x = m.ps("ps_x", [P, CH])
        ps_g, ps_u = m.ps("ps_g", [P, 2, F1]), m.ps("ps_u", [P, 2, F1])
        ps_h = m.ps("ps_h", [P, F1])
        ps_y = m.ps("ps_y", [P, CH])
        hid_ready = m.sem("hid_ready", 2)
        x_turned, x_copied, g_ready, u_ready, silu_ready, h_turned, h_copied, y_ready, y_copied = (
            m.sem(s) for s in ("x_turned", "x_copied", "g_ready", "u_ready", "silu_ready", "h_turned", "h_copied", "y_ready", "y_copied"))
        loaded, stored = [m.sem(f"loaded{i}") for i in range(4)], [m.sem("stored0"), m.sem("stored1")]
        nc.all_engine_barrier()
        block = ctx.enter_context(nc.Block())
        PAIRS = SLOT_TILES // 2
        UNROLL = 4
        ROUNDS = SLOT_TILES // UNROLL

        @block.sync
        def _(sp):
            def load(j, u):
                if later_than(j, 4):
                    sp.wait_ge(x_turned, 1 + j - 3)
                sp.dma_start(x_in[:, u, :], sorted_x[ds(j * P, P), :]).then_inc(loaded[u], 16)

            def store(j, u):
                sp.wait_ge(y_copied, 1 + j + 1)
                sp.dma_start(sorted_y[ds(j * P, P), :], y_out[:, u, :]).then_inc(stored[u], 16)

            for u in range(4):
                load(u, u)
            with sp.Fori(0, ROUNDS - 1) as i:
                for u in range(4):
                    j = i * 4 + u
                    load(j + 4, u)
                    store(j, u % 2)
            for u in range(4):
                store(SLOT_TILES - 4 + u, u % 2)
            for u in range(2):
                sp.wait_ge(stored[u], 1 + 16 * PAIRS)

        @block.tensor
        def _(pe):
            def turn_x(j, u):
                pe.wait_ge(loaded[u], 1 + (j // 4 + 1) * 16)
                if later_than(j, 1):
                    pe.wait_ge(x_copied, 1 + j)
                pe.transpose(ps_x[:, 0:P], x_in[:, u, :], g["ident"][:, :]).then_inc(x_turned, 1)

            def gate_up(j, u, e, name, ps, ready):
                if name == "w1":
                    pe.wait_ge(x_copied, 1 + j + 1)
                    pe.wait_ge(hid_ready, 1 + j + 1)
                pe.matmul(ps[:, u, :], x_c[:, u, :], w[name][:, ds(e, 1), :].rearrange("p a f -> p (a f)"), start=True, stop=True).then_inc(ready, 1)

            def turn_hid(j, u):
                pe.wait_ge(hid_ready, 1 + j + 3)
                if later_than(j, 1):
                    pe.wait_ge(h_copied, 1 + j)
                for b in range(FB):
                    mm = pe.transpose(ps_h[:, b * P:(b + 1) * P], hid[:, u, b * P:(b + 1) * P], g["ident"][:, :])
                mm.then_inc(h_turned, 1)

            def down(j, u, e):
                pe.wait_ge(h_copied, 1 + j + 1)
                if later_than(j, 1):
                    pe.wait_ge(y_copied, 1 + j)
                for b in range(FB):
                    mm = pe.matmul(ps_y[:, 0:P], hid_c[:, u, b * P:(b + 1) * P], w["w2"][:, ds(e, 1), b, :].rearrange("p a d -> p (a d)"),
                                   start=b == 0, stop=b == FB - 1)
                mm.then_inc(y_ready, 1)

            def expert(j):
                return pe.value_load(tile_expert[0:1, ds(j, 1)], min_val=0, max_val=E_ - 1)

            def tile(j, place, last, e, ahead, load_next):
                u = place % 2
                gate_up(j, u, e, "w1", ps_g, g_ready)
                if last is not None:
                    turn_hid(j - 1, 1 - u)
                if ahead:
                    turn_x(j + 1, (place + 1) % 4)
                gate_up(j, u, e, "w3", ps_u, u_ready)
                following = expert(j + 1) if load_next else None
                if last is not None:
                    down(j - 1, 1 - u, last)
                return following

            def tiles(j, n, last, more):
                e = expert(j)
                for u in range(n):
                    last, e = e, tile(j + u, u, last, e, more or u + 1 < n, u + 1 < n)
                return last

            turn_x(0, 0)
            tiles(0, UNROLL, None, True)
            with pe.Fori(1, ROUNDS - 1) as i:
                tiles(i * UNROLL, UNROLL, expert(i * UNROLL - 1), True)
            last = tiles((ROUNDS - 1) * UNROLL, UNROLL, expert((ROUNDS - 1) * UNROLL - 1), False)
            turn_hid(SLOT_TILES - 1, 1)
            down(SLOT_TILES - 1, 1, last)

        @block.scalar
        def _(act):
            with act.Fori(0, PAIRS) as i:
                for u in range(2):
                    j = i * 2 + u
                    act.wait_ge(g_ready, 1 + j + 1)
                    act.wait_ge(hid_ready, 1 + j + 1)
                    act.activation(silu[:, u, :], ps_g[:, u, :], ACT.Silu).then_inc(silu_ready, 1)
                    act.wait_ge(h_turned, 1 + j + 1)
                    act.wait_ge(y_ready, 1 + j)
                    act.activation(hid_c[:, u, :], ps_h[:, :], ACT.Copy).then_inc(h_copied, 1)

        @block.vector
        def _(v):
            def copy_x(j, u):
                v.wait_ge(x_turned, 1 + j + 1)
                if later_than(j):
                    v.wait_ge(u_ready, 1 + j - 1)
                v.tensor_copy(x_c[:, u, :], ps_x[:, 0:P]).then_inc(x_copied, 1)

            def copy_y(j, u):
                v.wait_ge(y_ready, 1 + j + 1)
                v.wait_ge(stored[u], 1 + j // 2 * 16)
                v.tensor_copy(y_out[:, u, :], ps_y[:, 0:P]).then_inc(y_copied, 1)

            def tile(j, u, prev, ahead):
                if ahead:
                    copy_x(j + 1, 1 - u)
                v.wait_ge(silu_ready, 1 + j + 1)
                v.wait_ge(u_ready, 1 + j + 1)
                if later_than(j):
                    v.wait_ge(h_turned, 1 + j - 1)
                v.tensor_tensor(hid[:, u, :], silu[:, u, :], ps_u[:, u, :], ALU.mult).then_inc(hid_ready, 1)
                if prev:
                    copy_y(j - 1, 1 - u)

            copy_x(0, 0)
            tile(0, 0, False, True)
            tile(1, 1, True, True)
            with v.Fori(1, PAIRS - 1) as i:
                for u in range(2):
                    tile(i * 2 + u, u, True, True)
            tile(SLOT_TILES - 2, 0, True, True)
            tile(SLOT_TILES - 1, 1, True, False)
            copy_y(SLOT_TILES - 1, 1)


def moe1_combine_stage(nc, g, r, slots, sorted_y, shared, out):
    with ExitStack() as ctx:
        m = Mem(nc, ctx, "m1f")
        fetched = m.sb("fetched", [P, 2, 2, CT, P])
        half_sum = m.sb("half_sum", [P, TILES, P])
        s = stats_buffers(m)
        y_mean, y_rstd = m.sb("y_mean", [P, TILES]), m.sb("y_rstd", [P, TILES])
        added, summed, stat_step, normed, x_added, stored = (
            m.sem(n) for n in ("added", "summed", "stat_step", "normed", "x_added", "stored"))
        arrived = [m.pool_dma_sem("arrived0"), m.pool_dma_sem("arrived1")]
        x, y = g["x_tok"], g["y_tok"]
        nc.all_engine_barrier()
        block = ctx.enter_context(nc.Block())

        @block.gpsimd
        def _(pool):
            for c in range(NCH):
                u = c % 2
                if c >= 2:
                    pool.wait_ge(summed, 1 + (c - 1) * CT)
                for t in range(c * CT, (c + 1) * CT):
                    for k in range(2):
                        pool.indirect_dma_start(out=fetched[:, u, k, t % CT, :], out_offset=None, in_=sorted_y,
                                                in_offset=bass.IndirectOffsetOnAxis(ap=slots[k][:, t:t + 1], axis=0)).then_inc(arrived[u], 16)

        @block.vector
        def _(v):
            step = Chain(v, stat_step)
            for c in range(NCH):
                u, at = c % 2, slice(c * CT, (c + 1) * CT)
                v.wait_ge(arrived[u], (c // 2 + 1) * 2 * CT * 16)
                for t in range(c * CT, (c + 1) * CT):
                    v.scalar_tensor_tensor(half_sum[:, t, :], fetched[:, u, 0, t % CT, :], r["v1"][:, t:t + 1], shared[:, t, :],
                                           ALU.mult, ALU.add).then_inc(added, 1)
                for t in range(c * CT, (c + 1) * CT):
                    v.wait_ge(added, 1 + t + 1)
                    v.scalar_tensor_tensor(y[:, t, :], fetched[:, u, 1, t % CT, :], r["v2"][:, t:t + 1], half_sum[:, t, :],
                                           ALU.mult, ALU.add).then_inc(summed, 1)
                v.wait_ge(summed, 1 + (c + 1) * CT)
                raw_stats(v, y, s, range(c * CT, (c + 1) * CT))
                v.wait_ge(s["raw_done"], 1 + (c + 1) * CT)
                raw = s["raw"]
                step(v.tensor_tensor(s["sum"][:, at], raw[:, at, 1], raw[:, at, 4], ALU.add))
                step(v.tensor_tensor(s["dif"][:, at], raw[:, at, 1], raw[:, at, 4], ALU.subtract))
                step(v.tensor_tensor(s["m2"][:, at], raw[:, at, 2], raw[:, at, 5], ALU.add))
                step(v.tensor_scalar(y_mean[:, at], s["sum"][:, at], 0.5, None, ALU.mult))
                step(v.tensor_tensor(s["sq"][:, at], s["dif"][:, at], s["dif"][:, at], ALU.mult))
                step(v.tensor_scalar(s["var"][:, at], s["m2"][:, at], 1.0 / P, EPS, ALU.mult, ALU.add))
                v.scalar_tensor_tensor(s["m2"][:, at], s["sq"][:, at], 0.25, s["var"][:, at], ALU.mult, ALU.add).then_inc(s["var_ready"], 1)
                v.wait_ge(s["std_ready"], 1 + c + 1)
                step(v.reciprocal(y_rstd[:, at], s["std"][:, at]))
                for t in range(c * CT, (c + 1) * CT):
                    v.tensor_scalar(y[:, t, :], y[:, t, :], y_mean[:, t:t + 1], y_rstd[:, t:t + 1],
                                    ALU.subtract, ALU.mult).then_inc(normed, 1)
                v.wait_ge(normed, 1 + (c + 1) * CT)
                v.tensor_tensor(x[:, at, :], x[:, at, :], y[:, at, :], ALU.add).then_inc(x_added, 1)

        @block.scalar
        def _(act):
            for c in range(NCH):
                at = slice(c * CT, (c + 1) * CT)
                act.wait_ge(s["var_ready"], 1 + c + 1)
                act.activation(s["std"][:, at], s["m2"][:, at], ACT.Sqrt).then_inc(s["std_ready"], 1)

        @block.sync
        def _(sp):
            o = out.rearrange("b (k p) e -> p (b k) e", p=P)
            for c in range(NCH):
                sp.wait_ge(x_added, 1 + c + 1)
                sp.dma_start(o[:, c * CT:(c + 1) * CT, :], x[:, c * CT:(c + 1) * CT, :]).then_inc(stored, 16)
            sp.wait_ge(stored, 1 + 16 * NCH)


def moe0(nc, g, io):
    with ExitStack() as ctx:
        m = Mem(nc, ctx, "m0")
        w = {"up_t": m.sb("up_t", [P, 2, E_, P], bf16), "down_t": m.sb("down_t", [P, E_, P]), "gate_w": m.sb("gate_w", [P, E_], bf16),
             "b1_t": m.sb("b1_t", [P, 2, E_]), "b2_rows": m.sb("b2_rows", [P, P], bf16), "norm_w": m.sb("norm_w", [P, P]),
             "gate_b": m.sb("gate_b", [P, E_], bf16), "pick": g["pick"]}
        xc = m.sb("xc", [P, TILES, P], bf16)
        rms_inv = m.sb("rms_inv", [P, TILES])
        nf_t, gate_t = m.sb("nf_t", [P, NTOK], bf16), m.sb("gate_t", [P, NTOK], bf16)
        gate_parts = m.sb("gate_parts", [P, TILES, PARTS, E_], bf16)
        moe0_weights_stage(nc, g, io, w)
        moe0_norm_stage(nc, g, w, xc, rms_inv)
        moe0_route_stage(nc, g, w, xc, rms_inv, nf_t, gate_parts)
        gate_rows_stage(nc, g, gate_parts, gate_t, "m0g")
        moe0_experts_stage(nc, g, w, xc, nf_t, gate_t)


def attn1(nc, g, io, scratch):
    with ExitStack() as ctx:
        m = Mem(nc, ctx, "a1")
        q_t, kp_t = m.sb("q_t", [P, B, T]), m.sb("kp_t", [P, B, T])
        k_t, v_t = m.sb("k_t", [P, B, PAD + T]), m.sb("v_t", [P, B, PAD + T])
        z_t = m.sb("z_t", [P, NTOK])
        l_inv = g["y_tok"][:, :, :].rearrange("p t e -> p (t e)")
        attn1_project_stage(nc, g, q_t, k_t, kp_t, v_t, scratch["v_rows"])
        attn1_windows_stage(nc, g, io, q_t, k_t, kp_t, v_t, scratch["v_rows"], z_t, l_inv)
        attn1_output_stage(nc, g, io, z_t, l_inv)


def moe1(nc, g, io, w, weights_loaded, scratch, out):
    with ExitStack() as ctx:
        m = Mem(nc, ctx, "m1")
        w["gate_w"] = m.sb("gate_w", [P, P])
        w["w2"] = m.sb("w2", [P, EXPERTS, FB, P])
        x_t = m.sb("x_t", [P, NTOK])
        shared = m.sb("shared", [P, TILES, P])
        zeros = m.sb("zeros", [P, SLOTS // ZERO_LOADS])
        r = route_buffers(m)
        slots = [m.sb(f"slots{k}", [P, TILES], mybir.dt.int32) for k in range(2)]
        tile_expert = m.sb("tile_expert", [P, SLOT_TILES], mybir.dt.int32)
        zero_done = m.sem("zero_done")
        moe1_weights_stage(nc, g, io, w, weights_loaded, zeros, scratch["sorted_x"], zero_done)
        moe1_route_stage(nc, g, w, r, x_t)
        moe1_sort_stage(nc, g, r, slots, tile_expert)
        moe1_shared_stage(nc, g, w, weights_loaded, x_t, slots, scratch["sorted_x"], zero_done, shared)
        moe1_experts_stage(nc, g, w, tile_expert, scratch["sorted_x"], scratch["sorted_y"])
        moe1_combine_stage(nc, g, r, slots, scratch["sorted_y"], shared, out)


def build_program(nc, io, out):
    scratch = {
        "qk_parts": nc.dram_tensor("qk_parts", [2, 3, P, NTOK], bf16, kind="Internal").ap(),
        "o_raw": nc.dram_tensor("o_raw", [H, DH + 1, NTOK], fp32, kind="Internal").ap(),
        "l_inv": nc.dram_tensor("l_inv", [H, NTOK], fp32, kind="Internal").ap(),
    }
    scratch["sorted_x"] = nc.dram_tensor("sorted_x", [SLOTS, P], fp32, kind="Internal").ap()
    scratch["sorted_y"] = nc.dram_tensor("sorted_y", [SLOTS, P], fp32, kind="Internal").ap()
    scratch["v_rows"] = nc.dram_tensor("v_rows", [NTOK, P], fp32, kind="Internal").ap()
    with ExitStack() as ctx:
        m = Mem(nc, ctx, "g")
        g = {
            "x_tok": m.sb("x_tok", [P, TILES, P]), "y_tok": m.sb("y_tok", [P, TILES, P]), 
            "mean": m.sb("mean", [P, TILES]), "rstd": m.sb("rstd", [P, TILES]),
            "ident": m.sb("ident", [P, P]), "ident_h": m.sb("ident_h", [P, P], bf16),
            "mask_qk": m.sb("mask_qk", [P, P], bf16), "mask_kq": m.sb("mask_kq", [P, P], bf16),
            "w_t": m.sb("w_t", [P, 9, P]), "place": m.sb("place", [P, E_]), "pick": m.sb("pick", [P, E_, P], bf16),
        }
        w1 = {"w1": m.sb("m1_w1", [P, EXPERTS, F1]), "w3": m.sb("m1_w3", [P, EXPERTS, F1])}
        weights_loaded = m.sem("weights_loaded")
        with semaphores_of(nc):
            load_stage(nc, io, g, w1, weights_loaded)
            with ExitStack() as inner:
                g["v_tok"] = Mem(nc, inner, "attn0").sb("v_tok", [P, TILES, P])
                attn0_project_stage(nc, g, scratch)
                attn0_heads_stage(nc, g, scratch, io)
            attn0_output_stage(nc, g, scratch)
            residual_stage(nc, g, "res0")
        with semaphores_of(nc):
            moe0(nc, g, io)
            residual_stage(nc, g, "res1")
        with semaphores_of(nc):
            attn1(nc, g, io, scratch)
            residual_stage(nc, g, "res2")
        with semaphores_of(nc):
            moe1(nc, g, io, w1, weights_loaded, scratch, out)


def kernel(**inputs):
    import numpy as np
    from concourse import bacc
    from concourse.bass_utils import run_bass_kernel_spmd

    half = inputs["L0_ffn_gate_weight"].dtype
    start = 2.0 ** -0.5
    slopes = np.array([start * start ** i for i in range(H)], np.float32)
    high = slopes.astype(half).astype(np.float32)
    middle = (slopes - high).astype(half).astype(np.float32)
    low = slopes - high - middle
    pos = np.arange(T)
    key_rows = np.zeros((P - 48, T), np.float32)
    key_rows[0:6:2], key_rows[1:6:2], key_rows[6:8] = pos // P * P, pos % P, 1.0
    slope_rows = np.zeros((H, 8, T), np.float32)
    for i, part in enumerate((high, middle, low)):
        slope_rows[:, 2 * i:2 * i + 2] = -part[:, None, None]
    arrays = {"key_rows": key_rows.astype(half), "slope_rows": slope_rows.astype(half),
              "query_rows": np.zeros((P - 48, T), half)}
    p = np.arange(P)
    head_mask = (p[:, None] // DH == np.arange(H)).astype(np.float32)
    key_mask = (p[:, None] % H == p[None, :] // DH).astype(np.float32)
    outside = np.ones((GK, 2, 3, BLK), bool)
    for q, (slot, lo, hi) in enumerate(GROUPS):
        for s in range(lo, hi):
            key = GK * q + np.arange(GK) - 2 * GK
            off = (key > s) | (key < s - WIN + 1)
            outside[:, 1, slot, s] = off
            outside[:, 0, slot, s] = off | (key < 0)
    m_pick = np.zeros((P, P), np.float32)
    m_pick[0:H] = m_pick[H:2 * H] = p[None, :] % H == np.arange(H)[:, None]
    m_pick[2 * H:2 * H + GK] = p[None, :] // H == np.arange(GK)[:, None]
    m_pick[2 * H + GK] = 1.0
    window_rows = np.zeros((P, 2, 3, BLK, WIN), np.float32)
    window_rows[2 * H:2 * H + GK] = np.where(outside, NEG, 0.0)[..., None]
    before = np.arange(BLK)[:, None] - (WIN - 1) + np.arange(WIN) < 0
    window_rows[2 * H + GK, 0] = np.where(before, NEG, 0.0)
    arrays.update(head_mask=head_mask, key_mask=key_mask, m_pick=m_pick.astype(half),
                  window_rows=window_rows.reshape(P, 2, 3 * BLK * WIN).astype(half))
    arrays.update({k: np.ascontiguousarray(v) for k, v in inputs.items()})

    nc = bacc.Bacc("TRN2", target_bir_lowering=False, num_devices=1)
    io = {k: nc.dram_tensor("in_" + k, a.shape, mybir.dt.from_np(a.dtype), kind="ExternalInput").ap() for k, a in arrays.items()}
    out = nc.dram_tensor("out", (B, T, P), fp32, kind="ExternalOutput").ap()
    build_program(nc, io, out)
    done = run_bass_kernel_spmd(nc, [{"in_" + k: a for k, a in arrays.items()}], core_ids=[0])
    return done.results[0]["out"]
```
